# Optimizing a Trainium2 kernel written in Bass

```python
import numpy as np
import jax
import jax.numpy as jnp

def _softmax(x, axis=-1):
    return jax.nn.softmax(x, axis=axis)

def _gelu(x):
    return jax.nn.gelu(x, approximate=True)

def _silu(x):
    return jax.nn.silu(x)

def _sigmoid(x):
    return jax.nn.sigmoid(x)

def _layernorm(x, axis=-1, eps=1e-05):
    m = jnp.mean(x, axis=axis, keepdims=True)
    v = jnp.var(x, axis=axis, keepdims=True)
    return (x - m) / jnp.sqrt(v + eps)

def _scatter_add(tgt, idx, src, axis=0):
    return tgt.at[idx].add(src)

def _segment_sum(src, seg, n):
    return jax.ops.segment_sum(src, seg, n)
kernel_name = 'mk_flamingo_gated_d2_seqx_r4_202a75'

def setup_inputs(seed: int=0):
    np.random.seed(seed)
    _w = jnp.asarray

    def _rec_inputs():
        import jax
        import jax.numpy as jnp
        _rk = jax.random.key(seed)
        x = 7.22e-05 + 1 * jax.random.normal(jax.random.fold_in(_rk, 1), (4, 512, 256), jnp.float32)
        _lenS = 512 - jax.random.randint(jax.random.fold_in(_rk, 7), (4,), 0, max(1, 512 // 4) + 1, jnp.int32)
        _lenS2 = 512 - jax.random.randint(jax.random.fold_in(_rk, 8), (4,), 0, max(1, 512 // 4) + 1, jnp.int32)
        _ctx_1024P = jax.random.normal(jax.random.fold_in(_rk, 11), (4, 16, 256), jnp.float32)
        _ctx_1024c = jax.random.dirichlet(jax.random.fold_in(_rk, 511), 0.3 * jnp.ones((16,), jnp.float32), (4, 512))
        _ctx_1024t = jnp.einsum('bsk,bkd->bsd', _ctx_1024c, _ctx_1024P)
        _ctx_1024t = _ctx_1024t * jax.lax.rsqrt(jnp.mean(jnp.square(_ctx_1024t)) + 1e-12) * 0.953939
        ctx_1024 = 4.13588e-05 + 0.999923 * (_ctx_1024t + 0.3 * jax.random.normal(jax.random.fold_in(_rk, 611), (4, 512, 256), jnp.float32))
        _g = jax.random.normal(jax.random.fold_in(_rk, 9001), (2, 2), jnp.float32)
        _g = jnp.sign(_g) * jnp.maximum(jnp.abs(_g), 1.0) + (_g == 0) * 1.0
        g_xattn = _g[0]
        g_ffn = _g[1]
        return (x, ctx_1024, g_xattn, g_ffn)
    x, ctx_1024, g_xattn, g_ffn = _rec_inputs()

    def _L0_xattn_setup():
        import jax, jax.numpy as jnp
        import numpy as np
        D_EMB = 256
        N_HEADS = 16
        D_K = D_EMB // N_HEADS
        B, L = (4, 512)
        key = jax.random.key(seed)
        kx, kc, kq, kk, kv, ko = jax.random.split(key, 6)
        bound = float(np.sqrt(3.0 / D_EMB))
        uni = lambda k: jax.random.uniform(k, (D_EMB, D_EMB), jnp.float32, -bound, bound)
        return {'x': jax.random.normal(kx, (B, L, D_EMB), jnp.float32), 'context': jax.random.normal(kc, (B, L, D_EMB), jnp.float32), 'Wq': uni(kq), 'Wk': uni(kk), 'Wv': uni(kv), 'Wo': uni(ko)}
    _L0_xattn_all = _L0_xattn_setup()
    _L0_xattn_in = {k: v for k, v in _L0_xattn_all.items() if k in ('Wq', 'Wk', 'Wv', 'Wo')}
    del _L0_xattn_all

    def _L0_ffn_setup():
        import jax, jax.numpy as jnp
        import numpy as np
        HIDDEN = 256
        INTER = 1024
        N_EXPERTS = 8

        def geglu(x, w1, w2, w3):
            return jax.nn.gelu(x @ w1, approximate=False) * (x @ w2) @ w3
        key = jax.random.key(seed)
        ks = jax.random.split(key, 8)
        s = 0.02
        x = jax.random.normal(ks[0], (2, 512, HIDDEN), dtype=jnp.float32)
        w1s = jax.random.normal(ks[1], (HIDDEN, INTER), dtype=jnp.float32) * s
        w2s = jax.random.normal(ks[2], (HIDDEN, INTER), dtype=jnp.float32) * s
        w3s = jax.random.normal(ks[3], (INTER, HIDDEN), dtype=jnp.float32) * s
        W1 = jax.random.normal(ks[4], (N_EXPERTS, HIDDEN, INTER), dtype=jnp.float32) * s
        W2 = jax.random.normal(ks[5], (N_EXPERTS, HIDDEN, INTER), dtype=jnp.float32) * s
        W3 = jax.random.normal(ks[6], (N_EXPERTS, INTER, HIDDEN), dtype=jnp.float32) * s
        Wg = jax.random.normal(ks[7], (HIDDEN, N_EXPERTS), dtype=jnp.float32) * s
        return {'x': x, 'w1s': w1s, 'w2s': w2s, 'w3s': w3s, 'W1': W1, 'W2': W2, 'W3': W3, 'Wg': Wg}
    _L0_ffn_all = _L0_ffn_setup()
    _L0_ffn_in = {k: v for k, v in _L0_ffn_all.items() if k in ('w1s', 'w2s', 'w3s', 'W1', 'W2', 'W3', 'Wg')}
    del _L0_ffn_all

    def _L1_xattn_setup():
        import jax, jax.numpy as jnp
        import numpy as np
        D_MODEL = 256
        B, S = (4, 512)
        key = jax.random.key(seed)
        ks = jax.random.split(key, 10)
        s = 1.0 / np.sqrt(D_MODEL)
        return {'k': jax.random.normal(ks[0], (B, S, D_MODEL), jnp.float32), 'v': jax.random.normal(ks[1], (B, S, D_MODEL), jnp.float32), 'q': jax.random.normal(ks[2], (B, S, D_MODEL), jnp.float32), 'Wk': jax.random.normal(ks[3], (D_MODEL, D_MODEL), jnp.float32) * s, 'Wv': jax.random.normal(ks[4], (D_MODEL, D_MODEL), jnp.float32) * s, 'bv': jnp.zeros((D_MODEL,), jnp.float32), 'Wq': jax.random.normal(ks[5], (D_MODEL, D_MODEL), jnp.float32) * s, 'bq': jnp.zeros((D_MODEL,), jnp.float32), 'Wo': jax.random.normal(ks[6], (D_MODEL, D_MODEL), jnp.float32) * s, 'bo': jnp.zeros((D_MODEL,), jnp.float32)}
    _L1_xattn_all = _L1_xattn_setup()
    _L1_xattn_in = {k: v for k, v in _L1_xattn_all.items() if k in ('Wk', 'Wv', 'bv', 'Wq', 'bq', 'Wo', 'bo')}
    del _L1_xattn_all

    def _L1_ffn_setup():
        import jax, jax.numpy as jnp
        import numpy as np
        D_MODEL = 256
        EXPANSION = 4
        D_HIDDEN = D_MODEL * EXPANSION
        NUM_STAGES = int(np.log2(D_HIDDEN))

        def butterfly(y, weights, dim):
            lead = y.shape[:-1]
            for stage in range(weights.shape[0]):
                s = 2 ** stage
                nb = dim // (2 * s)
                yr = y.reshape(*lead, nb, 2, s)
                a = yr[..., 0, :]
                b = yr[..., 1, :]
                w = weights[stage].reshape(nb, s, 2, 2)
                na = w[..., 0, 0] * a + w[..., 0, 1] * b
                nb2 = w[..., 1, 0] * a + w[..., 1, 1] * b
                y = jnp.stack([na, nb2], axis=-2).reshape(*lead, dim)
            return y
        key = jax.random.key(seed)
        ks = jax.random.split(key, 6)
        B, S = (4, 512)
        x = jax.random.normal(ks[0], (B, S, D_MODEL), jnp.float32)
        W_exp = jax.random.normal(ks[1], (D_MODEL, D_HIDDEN), jnp.float32) * 0.02
        b_exp = jnp.zeros((D_HIDDEN,), jnp.float32)
        up_weights = jax.random.normal(ks[2], (NUM_STAGES, D_HIDDEN // 2, 2, 2), jnp.float32) * 0.02
        up_bias = jnp.zeros((D_HIDDEN,), jnp.float32)
        down_weights = jax.random.normal(ks[3], (NUM_STAGES, D_HIDDEN // 2, 2, 2), jnp.float32) * 0.02
        W_con = jax.random.normal(ks[4], (D_HIDDEN, D_MODEL), jnp.float32) * 0.02
        b_con = jnp.zeros((D_MODEL,), jnp.float32)
        down_bias = jnp.zeros((D_MODEL,), jnp.float32)
        return dict(x=x, W_exp=W_exp, b_exp=b_exp, up_weights=up_weights, up_bias=up_bias, down_weights=down_weights, W_con=W_con, b_con=b_con, down_bias=down_bias)
    _L1_ffn_all = _L1_ffn_setup()
    _L1_ffn_in = {k: v for k, v in _L1_ffn_all.items() if k in ('W_exp', 'b_exp', 'up_weights', 'up_bias', 'down_weights', 'W_con', 'b_con', 'down_bias')}
    del _L1_ffn_all
    return {'x': x, 'ctx_1024': ctx_1024, 'g_xattn': g_xattn, 'g_ffn': g_ffn, 'L0_xattn_Wq': _L0_xattn_in['Wq'], 'L0_xattn_Wk': _L0_xattn_in['Wk'], 'L0_xattn_Wv': _L0_xattn_in['Wv'], 'L0_xattn_Wo': _L0_xattn_in['Wo'], 'L0_ffn_w1s': _L0_ffn_in['w1s'], 'L0_ffn_w2s': _L0_ffn_in['w2s'], 'L0_ffn_w3s': _L0_ffn_in['w3s'], 'L0_ffn_W1': _L0_ffn_in['W1'], 'L0_ffn_W2': _L0_ffn_in['W2'], 'L0_ffn_W3': _L0_ffn_in['W3'], 'L0_ffn_Wg': _L0_ffn_in['Wg'], 'L1_xattn_Wk': _L1_xattn_in['Wk'], 'L1_xattn_Wv': _L1_xattn_in['Wv'], 'L1_xattn_bv': _L1_xattn_in['bv'], 'L1_xattn_Wq': _L1_xattn_in['Wq'], 'L1_xattn_bq': _L1_xattn_in['bq'], 'L1_xattn_Wo': _L1_xattn_in['Wo'], 'L1_xattn_bo': _L1_xattn_in['bo'], 'L1_ffn_W_exp': _L1_ffn_in['W_exp'], 'L1_ffn_b_exp': _L1_ffn_in['b_exp'], 'L1_ffn_up_weights': _L1_ffn_in['up_weights'], 'L1_ffn_up_bias': _L1_ffn_in['up_bias'], 'L1_ffn_down_weights': _L1_ffn_in['down_weights'], 'L1_ffn_W_con': _L1_ffn_in['W_con'], 'L1_ffn_b_con': _L1_ffn_in['b_con'], 'L1_ffn_down_bias': _L1_ffn_in['down_bias']}

def reference(x, ctx_1024, g_xattn, g_ffn, L0_xattn_Wq, L0_xattn_Wk, L0_xattn_Wv, L0_xattn_Wo, L0_ffn_w1s, L0_ffn_w2s, L0_ffn_w3s, L0_ffn_W1, L0_ffn_W2, L0_ffn_W3, L0_ffn_Wg, L1_xattn_Wk, L1_xattn_Wv, L1_xattn_bv, L1_xattn_Wq, L1_xattn_bq, L1_xattn_Wo, L1_xattn_bo, L1_ffn_W_exp, L1_ffn_b_exp, L1_ffn_up_weights, L1_ffn_up_bias, L1_ffn_down_weights, L1_ffn_W_con, L1_ffn_b_con, L1_ffn_down_bias):
    import jax
    import jax.numpy as jnp

    def _L0_xattn_ref(x, context, Wq, Wk, Wv, Wo):
        import jax, jax.numpy as jnp
        import numpy as np
        D_EMB = 256
        N_HEADS = 16
        D_K = D_EMB // N_HEADS
        B, L = (4, 512)
        b, length, d = x.shape
        Q = (x @ Wq.T).reshape(b, length, N_HEADS, D_K).swapaxes(-2, -1)
        K = (context @ Wk.T).reshape(b, length, N_HEADS, D_K).swapaxes(-2, -1)
        V = (context @ Wv.T).reshape(b, length, N_HEADS, D_K).swapaxes(-2, -1)
        qk = jnp.einsum('blih,bljh->blij', Q, K) / jnp.sqrt(jnp.asarray(D_K, x.dtype))
        attn = jax.nn.softmax(qk, axis=-1)
        valued = jnp.einsum('blij,bljh->blih', attn, V)
        concat = valued.swapaxes(-2, -1).reshape(b, length, d)
        return concat @ Wo.T

    def _L0_ffn_ref(x, w1s, w2s, w3s, W1, W2, W3, Wg):
        import jax, jax.numpy as jnp
        import numpy as np
        HIDDEN = 256
        INTER = 1024
        N_EXPERTS = 8

        def geglu(x, w1, w2, w3):
            return jax.nn.gelu(x @ w1, approximate=False) * (x @ w2) @ w3
        B, T, C = x.shape
        xf = x.reshape(-1, C)
        shared = geglu(xf, w1s, w2s, w3s)
        logits = xf @ Wg
        idx = jnp.argmax(logits, axis=-1)
        final = jnp.zeros_like(xf)
        for e in range(N_EXPERTS):
            y = geglu(xf, W1[e], W2[e], W3[e])
            final = final + jnp.where((idx == e)[:, None], y, 0.0)
        return (shared + final).reshape(B, T, C)

    def _L1_xattn_ref(k, v, q, Wk, Wv, bv, Wq, bq, Wo, bo):
        import jax, jax.numpy as jnp
        import numpy as np
        D_MODEL = 256
        B, S = (4, 512)
        kp = jnp.einsum('bsd,ed->bse', k, Wk)
        vp = jnp.einsum('bsd,ed->bse', v, Wv) + bv
        qp = jnp.einsum('bsd,ed->bse', q, Wq) + bq
        scale = 1.0 / jnp.sqrt(jnp.float32(kp.shape[-1]))
        scores = jnp.einsum('bqd,bkd->bqk', qp, kp) * scale
        probs = jax.nn.softmax(scores, axis=-1)
        ctx = jnp.einsum('bqk,bkd->bqd', probs, vp)
        return jnp.einsum('bqd,ed->bqe', ctx, Wo) + bo

    def _L1_ffn_ref(x, W_exp, b_exp, up_weights, up_bias, down_weights, W_con, b_con, down_bias):
        import jax, jax.numpy as jnp
        import numpy as np
        D_MODEL = 256
        EXPANSION = 4
        D_HIDDEN = D_MODEL * EXPANSION
        NUM_STAGES = int(np.log2(D_HIDDEN))

        def butterfly(y, weights, dim):
            lead = y.shape[:-1]
            for stage in range(weights.shape[0]):
                s = 2 ** stage
                nb = dim // (2 * s)
                yr = y.reshape(*lead, nb, 2, s)
                a = yr[..., 0, :]
                b = yr[..., 1, :]
                w = weights[stage].reshape(nb, s, 2, 2)
                na = w[..., 0, 0] * a + w[..., 0, 1] * b
                nb2 = w[..., 1, 0] * a + w[..., 1, 1] * b
                y = jnp.stack([na, nb2], axis=-2).reshape(*lead, dim)
            return y
        h = jnp.einsum('bsd,dh->bsh', x, W_exp) + b_exp
        h = butterfly(h, up_weights, D_HIDDEN)
        h = jax.nn.gelu(h + up_bias, approximate=False)
        h = butterfly(h, down_weights, D_HIDDEN)
        y = jnp.einsum('bsh,hd->bsd', h, W_con) + b_con
        return y + down_bias
    x = x + jnp.tanh(g_xattn[0]) * _L0_xattn_ref(_layernorm(x, axis=-1), ctx_1024, L0_xattn_Wq, L0_xattn_Wk, L0_xattn_Wv, L0_xattn_Wo)
    x = x + jnp.tanh(g_ffn[0]) * _L0_ffn_ref(_layernorm(x, axis=-1), L0_ffn_w1s, L0_ffn_w2s, L0_ffn_w3s, L0_ffn_W1, L0_ffn_W2, L0_ffn_W3, L0_ffn_Wg)
    x = x + jnp.tanh(g_xattn[1]) * _L1_xattn_ref(ctx_1024, ctx_1024, _layernorm(x, axis=-1), L1_xattn_Wk, L1_xattn_Wv, L1_xattn_bv, L1_xattn_Wq, L1_xattn_bq, L1_xattn_Wo, L1_xattn_bo)
    x = x + jnp.tanh(g_ffn[1]) * _L1_ffn_ref(_layernorm(x, axis=-1), L1_ffn_W_exp, L1_ffn_b_exp, L1_ffn_up_weights, L1_ffn_up_bias, L1_ffn_down_weights, L1_ffn_W_con, L1_ffn_b_con, L1_ffn_down_bias)
    return x

_drawn_inputs = setup_inputs


def setup_inputs(seed=0):
    import zlib

    import numpy as np

    out = dict(_drawn_inputs(seed))
    spreads = {'g_ffn': (-1.0, 0.6),
     'L1_xattn_bv': (0.0, 0.1),
     'L1_xattn_bq': (0.0, 0.519),
     'L1_xattn_bo': (0.0, 0.1),
     'L1_ffn_b_exp': (0.0, 0.1),
     'L1_ffn_up_bias': (0.0, 0.1),
     'L1_ffn_b_con': (0.0, 0.1),
     'L1_ffn_down_bias': (0.0, 0.1)}
    factors = {}
    for name, (base, spread) in spreads.items():
        noise = np.random.default_rng([zlib.crc32(name.encode()), seed]).standard_normal(out[name].shape)
        drawn = base * np.exp(spread * noise) if base else spread * noise
        out[name] = jnp.asarray(drawn.astype(out[name].dtype))
    for name, factor in factors.items():
        out[name] = (out[name] * factor).astype(out[name].dtype)
    return out
```

```python
from contextlib import ExitStack

import numpy as np

import concourse.bass as bass
from concourse import mybir

F32 = mybir.dt.float32
I32 = mybir.dt.int32
U32 = mybir.dt.uint32
ALU = mybir.AluOpType
ACT = mybir.ActivationFunctionType
AX = mybir.AxisListType

P = 128
B, L, D = 4, 512, 256
T = B * L // P
TB = L // P
KD = D // P
NH = 16
DK = D // NH
F = 1024
KF = F // P
NE = 8
NT = T + NE - 1
SLOTS = 3
WS = 3 * KD * F
LOW, HIGH = 7, 3
EPS = 1e-5


def spread(v, axis, n):
    shape = list(v.shape)
    shape[axis] = n
    return v.broadcast_to(shape)


def build(nc, x, ctxT, gates, wq0, wkv0, wo0, wg, wexp, wk1, wv1, wq1, wo1, bv1, bq1, bo1,
          weT, be, upw, upb, dnw, wc, bc, db, out):
    with ExitStack() as ctx:
        def sb(name, shape, dt=F32):
            return ctx.enter_context(nc.sbuf_tensor(name, shape, dt))

        def sem(name):
            return ctx.enter_context(nc.semaphore(name))

        xs = nc.dram_tensor("sorted_rows", (NT * P, D), F32).ap()
        ys = nc.dram_tensor("expert_rows", (NT * P, D), F32).ap()

        X = sb("X", [P, T, D])
        XN2 = sb("XN2", [P, T, D])
        SLOT = sb("SLOT", [P, SLOTS, WS])
        WQ0 = sb("WQ0", [P, KD, D])
        WKV0 = sb("WKV0", [P, KD, 2 * D])
        WO0 = sb("WO0", [P, KD, D])
        WG = sb("WG", [P, KD, NE])
        WK1 = sb("WK1", [P, KD, D])
        WV1 = sb("WV1", [P, KD, D])
        WQ1 = sb("WQ1", [P, KD, D])
        WO1 = sb("WO1", [P, KD, D])
        BIAS = sb("BIAS", [P, 4, D])
        BQ = sb("BQ", [P, KD])
        IDENT = sb("IDENT", [P, P])
        ABOVE = sb("ABOVE", [P, P])
        ONES = sb("ONES", [P, P])
        MHALF = sb("MHALF", [P, 1])
        GATE = sb("GATE", [P, 4])
        TG = sb("TG", [P, 4])
        IOTA8 = sb("IOTA8", [P, NE])
        IOTAM = sb("IOTAM", [P, T])
        IOTAT = sb("IOTAT", [1, NT])
        IOTAI = sb("IOTAI", [P, NE + T + NT], I32)
        PRODQ = sb("PRODQ", [P, DK * DK * NH])
        PRODV = sb("PRODV", [P, DK * DK * NH])
        SHARED = sb("SHARED", [P, 2 * F])
        CTX = SHARED[:, 0:2 * KD * P].rearrange("p (r k t) -> p r k t", r=2, k=KD)
        PR = SHARED[:, 2 * KD * P:2 * KD * P + 2 * D].rearrange("p (r d) -> p r d", r=2)
        KV = SHARED[:, 2 * KD * P + 2 * D:2 * F].rearrange("p (r d) -> p r d", r=2)
        XN = sb("XN", [P, D])
        XH = sb("XH", [P, D])
        XT = sb("XT", [P, KD, P])
        SC = sb("SC", [P, D])
        AO = sb("AO", [P, D])
        AT = sb("AT", [P, KD, P])
        X2T = sb("X2T", [P, KD, P])
        ST = sb("ST", [P, 2, 6])
        MV = sb("MV", [P, 2, 4])
        SM = sb("SM", [P, 2, DK])
        RI = sb("RI", [P, DK])
        LG = sb("LG", [P, NE])
        TOP = sb("TOP", [P, NE])
        TOPI = sb("TOPI", [P, NE], U32)
        TOPF = sb("TOPF", [P, 1])
        G = sb("G", [P, F])
        HA = sb("HA", [P, KF, P])
        OH = sb("OH", [P, T, NE])
        RANK = sb("RANK", [P, T, NE])
        LESS = sb("LESS", [P, NE, NE])
        CMP = sb("CMP", [P, NE * T])
        NTE = sb("NTE", [P, NE])
        BASE = sb("BASE", [P, NE])
        POSF = sb("POSF", [P, T])
        POS = sb("POS", [P, T], U32)
        EI = sb("EI", [1, NT])
        GE = sb("GE", [1, NT, NE])
        SUM2 = sb("SUM2", [1, SLOTS, NT])
        TAB = sb("TAB", [1, 1 + SLOTS, NT], I32)
        BASEI = sb("BASEI", [1, NE], I32)

        flatA = PRODQ[:, :]
        flatV = PRODV[:, :]
        XS = sb("XS", [P, 2, D])
        XST = sb("XST", [P, 2, KD, P])
        HB = SHARED[:, :].rearrange("p (r f) -> p r f", r=2)
        HBT = HA
        YS = sb("YS", [P, D])
        COEF = flatA.rearrange("p (r k c) -> p r k c", r=2, c=4)
        WEFF = flatA[:, 0:KD * F].rearrange("p (k f) -> p k f", k=KD)
        MDN = flatA[:, KD * F:2 * KD * F].rearrange("p (c d) -> p c d", c=KF)
        Z = flatV[:, 0:KF * D].rearrange("p (c d) -> p c d", c=KF)
        EB = flatV[:, KF * D:KF * D + 2 * F].rearrange("p (r f) -> p r f", r=2)
        W1P = D + 1
        x2 = XN2[:, :, :].rearrange("p t d -> p (t d)")
        RT = x2[:, 0:KF * W1P].rearrange("p (c d) -> p c d", c=KF)
        EC = x2[:, KF * W1P:KF * W1P + F]
        WET = sb("WET", [P, KF, W1P])
        HIC = sb("HIC", [P, 2, HIGH, 4, 4])
        UPB = sb("UPB", [P, KF])
        TMPH = sb("TMPH", [P, 4, W1P])
        TMP = TMPH[:, :, :].rearrange("p a b -> p (a b)")
        BH = sb("BH", [P, KF])
        sf = SLOT[:, :, :].rearrange("p s w -> p (s w)")
        at = [0]

        def part(n):
            at[0] += n
            return sf[:, at[0] - n:at[0]]

        XN3T = part(KD * L).rearrange("p (k t) -> p k t", k=KD)
        XN4T = part(KD * L).rearrange("p (k t) -> p k t", k=KD)
        CTXB = part(KD * L).rearrange("p (k t) -> p k t", k=KD)
        QT = part(KD * L).rearrange("p (k t) -> p k t", k=KD)
        K1T = part(KD * L).rearrange("p (k t) -> p k t", k=KD)
        V1 = part(TB * D).rearrange("p (t d) -> p t d", t=TB)
        PS = part(2 * L).rearrange("p (r t) -> p r t", r=2)
        PT = part(L).rearrange("p (k t) -> p k t", k=TB)
        XNC = part(2 * D).rearrange("p (r d) -> p r d", r=2)
        CC = part(D)
        CT = part(D).rearrange("p (k t) -> p k t", k=KD)
        H4 = part(KF * L).rearrange("p (c t) -> p c t", c=KF)
        TO = part(D)
        TY = part(D)
        YG = part(TB * D).rearrange("p (t d) -> p t d", t=TB)
        assert at[0] <= SLOTS * WS
        NM = sb("NM", [P, 1])
        NMS = sb("NMS", [P, 2])
        SU = sb("SU", [P, 2])
        RC = sb("RC", [P, 1])
        STC = sb("STC", [P, TB, 6])
        MVC = sb("MVC", [P, TB, 2])
        VE = sb("VE", [P, TB])
        RS = sb("RS", [P, TB])
        BCD = sb("BCD", [P, D])

        PB = [ctx.enter_context(nc.psum_tensor(f"bank{i}", [P, 512], F32)) for i in range(8)]

        w_in = sem("w_in")
        wg_in = sem("wg_in")
        c_in = sem("c_in")
        tile_in = [sem("tile_in0"), sem("tile_in1")]
        slot_in = [sem(f"slot_in{i}") for i in range(SLOTS)]
        consts = sem("consts")
        iotas = sem("iotas")
        iotaf = sem("iotaf")
        zero_ms = sem("zero_ms")
        zeroed = sem("zeroed")
        tanh_s = sem("tanh_s")

        names = """qk_prod scores rowmax shifted exp_done sums a_ready av_read ln1_stats ln1_agg ln1_eps
        ln1_rstd xn_ready ln2_stats ln2_agg ln2_eps ln2_rstd xn2_ready x1_ready xT_done xT_sb q_done
        kv_done kv_sb x2T_done x2T_sb aT_done aT_sb o_done gate_done lg_sb top_ok topi_ok topf_ok
        oh_ok xn2_kept h1_done h2_done gelu_done mult_done y_done y_added av_half recip""".split()
        s = {n: sem(n) for n in names}
        route = sem("route")
        held = sem("held")
        rank_ps = sem("rank_ps")
        tables = sem("tables")
        pos_ready = sem("pos_ready")
        scattered = sem("scattered")
        slot_uses = sem("slot_uses")

        bnames = """sT_done sT_sb b_h1 b_h2 b_gelu b_mult hT_done hT_a hT_d by_done by_sb""".split()
        e = {n: sem(n) for n in bnames}
        xs_in = [sem("xs_in0"), sem("xs_in1")]
        ys_out = sem("ys_out")
        pool = sem("pool")
        coef_in = [sem("coef_in0"), sem("coef_in1")]
        e_up = sem("e_up")
        rt_ps = sem("rt_ps")
        rt_sb = sem("rt_sb")
        rt_high = sem("rt_high")
        z_high = sem("z_high")
        wm_ps = sem("wm_ps")
        wm_sb = sem("wm_sb")
        gathered = sem("gathered")
        x2_added = sem("x2_added")
        ctx_in = sem("ctx_in")

        cnames = """c_stats c_agg c_eps c_rstd c_xn c_xT c_xT_sb sc_done nmax nmax_s p_done pT_done pT_sb
        av_done rinv c_ready cT_done cT_sb out_done tmp_o x3_ready fin_ready""".split()
        c = {n: sem(n) for n in cnames}
        ring_full = [sem("ring_full0"), sem("ring_full1")]
        ring_free = [sem("ring_free0"), sem("ring_free1")]
        stored = sem("stored")
        bcd_ready = sem("bcd_ready")

        block = ctx.enter_context(nc.Block())

        LAG = 4
        PAUSE = 7

        def lag(j, par, n):
            m = par - n
            return j + m // 2, m % 2

        def sweep(eng, step, count, lags, start, ahead=0, pause=None, at_pause=None):
            def tiles(j, par, t):
                def of(n):
                    if t is not None and not 0 <= t - n < count:
                        return None
                    return lag(j, par, n)
                return of
            for t in range(2 * start):
                step(tiles(t // 2, t % 2, t))
            end = (count - ahead) // 2
            for lo, hi in ((start, end),) if pause is None else ((start, pause), (pause, end)):
                with eng.Fori(lo, hi) as j:
                    step(tiles(j, 0, None))
                    step(tiles(j, 1, None))
                if hi == pause:
                    at_pause()
            for t in range(2 * end, count + lags):
                step(tiles(t // 2, t % 2, t))

        def sweep_a(eng, step):
            sweep(eng, step, T, LAG, LAG // 2)

        def sweep_b(eng, step, at_pause=None):
            sweep(eng, step, NT, 2, 2, 2, PAUSE if at_pause else None, at_pause)

        def num(jp):
            return 2 * jp[0] + jp[1]

        def first(jp, n):
            return isinstance(jp[0], int) and num(jp) < n

        def ring_before(b, n):
            if isinstance(b, int) and b == 0:
                return n // 2
            return 9 * b - 6 + (n - 6 if isinstance(b, int) and b == B else n) // 2

        def norm_c(b):
            return 0 if isinstance(b, int) and b == 0 else 2 * b - 1

        def norm_d(b):
            return 2 * b - 1 if isinstance(b, int) and b == B else 2 * b

        def sweep_cd(eng, step):
            step(0, True, False)
            with eng.Fori(1, B) as b:
                step(b, True, True)
            step(B, False, True)

        @block.sync
        def _(sp):
            def load_tile(j, par):
                t = 2 * j + par
                if not (isinstance(j, int) and j == 0):
                    sp.wait_ge(tile_in[par], 32 * j)
                    sp.wait_ge(s["kv_done"], t - 1)
                sp.dma_start(X[:, t, :], x[bass.ds(t * P, P), :]).then_inc(tile_in[par], 16)
                sp.dma_start(CTX[:, par, :, :],
                             ctxT[:, bass.ds(t * P, P)].rearrange("(k p) t -> p k t", p=P))\
                    .then_inc(tile_in[par], 16)

            load_tile(0, 0)
            for w, src in ((WQ0, wq0), (WKV0, wkv0)):
                sp.dma_start(w[:, :, :], src.rearrange("(k p) n -> p k n", p=P)).then_inc(w_in, 16)
            load_tile(0, 1)
            for w, src in ((WO0, wo0), (WG, wg)):
                sp.dma_start(w[:, :, :], src.rearrange("(k p) n -> p k n", p=P)).then_inc(wg_in, 16)
            sp.dma_start(GATE[:, :], gates.partition_broadcast(P)).then_inc(wg_in, 16)
            sp.dma_start(SLOT[:, 2, :], wexp[NE]).then_inc(slot_in[2], 16)
            with sp.Fori(1, T // 2) as j:
                load_tile(j, 0)
                load_tile(j, 1)
            for w, src in ((WK1, wk1), (WV1, wv1), (WQ1, wq1), (WO1, wo1)):
                sp.dma_start(w[:, :, :], src.rearrange("(k p) n -> p k n", p=P)).then_inc(c_in, 16)
            for n, src in enumerate((bv1, bo1, bc, db)):
                sp.dma_start(BIAS[:, n, :], src.partition_broadcast(P)).then_inc(c_in, 16)
            with nc.allow_non_contiguous_dma("biases and coefficients by partition"):
                sp.dma_start(BQ[:, :], bq1.rearrange("(k p) -> p k", p=P)).then_inc(c_in, 16)
                sp.dma_start(UPB[:, :], upb.rearrange("(k p) -> p k", p=P)).then_inc(c_in, 16)
                for n, src in enumerate((upw, dnw)):
                    sp.dma_start(HIC[:, n, :, :, :], src[LOW:LOW + HIGH].rearrange(
                        "s (q p) c -> p s q c", p=P)).then_inc(c_in, 16)
                sp.dma_start(WET[:, :, 0:D], weT.rearrange("(c p) d -> p c d", p=P)).then_inc(c_in, 16)
                sp.dma_start(WET[:, :, D:W1P], be.rearrange("(c p o) -> p c o", p=P, o=1))\
                    .then_inc(c_in, 16)
            sp.dma_start(SLOT[:, 0, :], wexp[0]).then_inc(slot_in[0], 16)
            sp.dma_start(SLOT[:, 1, :], wexp[1]).then_inc(slot_in[1], 16)
            sp.wait_ge(s["y_done"], T)
            sp.dma_start(SLOT[:, 2, :], wexp[2]).then_inc(slot_in[2], 16)
            sp.wait_ge(tables, 1)
            for n in range(SLOTS, NE):
                base = sp.value_load(BASEI[0:1, n - 2:n - 1], min_val=1, max_val=NT + 1)
                sp.wait_ge(slot_uses, base)
                sp.dma_start(SLOT[:, n % SLOTS, :], wexp[n]).then_inc(slot_in[n % SLOTS], 16)
            sp.wait_ge(slot_uses, 1 + NT)

            def load_ctx(b):
                sp.dma_start(CTXB, ctxT[:, bass.ds(b * L, L)].rearrange("(k p) t -> p k t", p=P))\
                    .then_inc(ctx_in, 16)

            load_ctx(0)

            def outputs(b):
                for q in range(TB):
                    tile = b * TB + q
                    sp.wait_ge(c["fin_ready"], tile + 1)
                    sp.dma_start(out[bass.ds(tile * P, P), :], X[:, tile, :]).then_inc(stored, 16)

            def context_used(b):
                for n in (4, 5):
                    sp.wait_ge(ring_free[n % 2], ring_before(b, n) + 1)

            context_used(0)
            load_ctx(1)
            with sp.Fori(1, B - 1) as b:
                context_used(b)
                load_ctx(b + 1)
                outputs(b - 1)
            outputs(B - 2)
            outputs(B - 1)
            sp.wait_ge(stored, 16 * T)

        @block.gpsimd
        def _(gp):
            gp.memset(IDENT[:, :], 0.0).then_inc(consts, 1)
            gp.memset(ABOVE[:, :], 0.0).then_inc(consts, 1)
            gp.memset(ONES[:, :], 1.0).then_inc(consts, 1)
            gp.memset(MHALF[:, :], -0.5).then_inc(consts, 1)
            gp.wait_ge(consts, 4)
            gp.affine_select(out=IDENT[:, :], in_=IDENT[:, :], compare_op=ALU.not_equal, fill=1.0,
                             base=0, pattern=[[-1, P]], channel_multiplier=1).then_inc(consts, 1)
            gp.affine_select(out=ABOVE[:, :], in_=ABOVE[:, :], compare_op=ALU.is_ge, fill=1.0,
                             base=0, pattern=[[-1, P]], channel_multiplier=1).then_inc(consts, 1)
            gp.iota(IOTAI[:, 0:NE], pattern=[[1, NE]], base=0, channel_multiplier=0).then_inc(iotas, 1)
            gp.iota(IOTAI[:, NE:NE + T], pattern=[[P, T]], base=0, channel_multiplier=0).then_inc(iotas, 1)
            gp.iota(IOTAI[:, NE + T:], pattern=[[1, NT]], base=0, channel_multiplier=0).then_inc(iotas, 1)
            gp.memset(PRODV[:, :], 0.0).then_inc(zero_ms, 1)
            gp.wait_ge(zero_ms, 1)
            for r0 in range(0, NT, T):
                n = min(T, NT - r0)
                gp.dma_start(xs[r0 * P:(r0 + n) * P, :].rearrange("(t p) d -> p t d", p=P),
                             PRODV[:, 0:n * D].rearrange("p (t d) -> p t d", t=n)).then_inc(zeroed, 16)

            def step(of):
                if (t3 := of(3)) is not None:
                    gp.wait_ge(s["ln2_eps"], num(t3) + 1)
                    gp.tensor_tensor(MV[:, 1, 3:4], MV[:, 1, 2:3], MHALF[:, :], ALU.pow)\
                        .then_inc(s["ln2_rstd"], 1)
                if (t0 := of(0)) is not None:
                    gp.wait_ge(s["ln1_eps"], num(t0) + 1)
                    gp.tensor_tensor(MV[:, 0, 3:4], MV[:, 0, 2:3], MHALF[:, :], ALU.pow)\
                        .then_inc(s["ln1_rstd"], 1)
                if (t1 := of(1)) is not None:
                    n, par = num(t1), t1[1]
                    gp.wait_ge(s["exp_done"], n + 1)
                    gp.wait_ge(s["kv_sb"], n + 1)
                    if first(t1, 1):
                        gp.wait_ge(zeroed, 32)
                    for hf in range(2):
                        if not first(t1, 1):
                            gp.wait_ge(s["av_read"], 2 * (n - 1) + hf + 1)
                        H2 = NH // 2
                        o = PRODV[:, :].rearrange("p (f i h j) -> p f i h j", f=2, i=DK, h=H2)[:, hf]
                        pr = spread(PR[:, par, :].rearrange("p (i o j) -> p i o j", i=DK, o=1), 2, H2)
                        v = KV[:, par, D + hf * H2 * DK:D + (hf + 1) * H2 * DK]
                        v = spread(v.rearrange("p (o h j) -> p o h j", o=1, j=DK), 1, DK)
                        gp.tensor_tensor(o, pr, v, ALU.mult).then_inc(s["av_half"], 1)

            sweep_a(gp, step)

            gp.wait_ge(zeroed, 32)
            gp.wait_ge(pos_ready, 1)
            for t in range(T):
                gp.indirect_dma_start(out=xs, out_offset=bass.IndirectOffsetOnAxis(ap=POS[:, t:t + 1], axis=0),
                                      in_=XN2[:, t, :], in_offset=None).then_inc(scattered, 16)

            done = [0]

            def run(ins):
                done[0] += 1
                ins.then_inc(pool, 1)

            def settle():
                gp.wait_ge(pool, done[0])

            stages = [(0, upw, k) for k in range(LOW)] + [(1, dnw, k) for k in reversed(range(LOW))]

            def load_coef(n):
                _, src, k = stages[n]
                gp.dma_start(COEF[:, n % 2, :, :].rearrange("p k c -> p (k c)"),
                             src[k].rearrange("k c -> (k c)").partition_broadcast(P))\
                    .then_inc(coef_in[n % 2], 16)

            gp.wait_ge(s["a_ready"], T)
            load_coef(0)
            load_coef(1)
            gp.wait_ge(scattered, 16 * T)
            gp.dma_start(Z, wc.rearrange("(c p) d -> p c d", p=P)).then_inc(zeroed, 16)
            bufs = [EB[:, 0, :], EB[:, 1, :], EC]

            def low(n, src, dst):
                down, _, k = stages[n]
                w = 2 ** k
                a, b = (src.rearrange("p (n two w) -> p n two w", two=2, w=w)[:, :, i, :] for i in (0, 1))
                oa, ob = (dst.rearrange("p (n two w) -> p n two w", two=2, w=w)[:, :, i, :] for i in (0, 1))
                cf = [COEF[:, n % 2, :, i].rearrange("p (n w) -> p n w", w=w) for i in range(4)]
                if down:
                    cf[1], cf[2] = cf[2], cf[1]
                t = [TMP[:, i * F // 2:(i + 1) * F // 2].rearrange("p (n w) -> p n w", w=w) for i in range(2)]
                gp.wait_ge(coef_in[n % 2], 16 * (n // 2 + 1))
                settle()
                run(gp.tensor_tensor(oa, a, cf[0], ALU.mult))
                run(gp.tensor_tensor(t[0], b, cf[1], ALU.mult))
                run(gp.tensor_tensor(ob, a, cf[2], ALU.mult))
                run(gp.tensor_tensor(t[1], b, cf[3], ALU.mult))
                settle()
                if n + 2 < len(stages):
                    load_coef(n + 2)
                run(gp.tensor_tensor(oa, oa, t[0], ALU.add))
                run(gp.tensor_tensor(ob, ob, t[1], ALU.add))

            def eye(dst):
                settle()
                run(gp.memset(dst, 0.0))
                settle()
                v = dst.rearrange("p (c m) -> p c m", c=KF)
                run(gp.affine_select(out=v, in_=v, compare_op=ALU.not_equal, fill=1.0, base=0,
                                     pattern=[[0, KF], [-1, P]], channel_multiplier=1))

            def high(n, m, width, stage):
                bit = stage
                for q in range(4):
                    c0 = ((q >> bit) << (bit + 1)) | (q & ((1 << bit) - 1))
                    c1 = c0 | (1 << bit)
                    cf = [HIC[:, n, stage, q, i:i + 1] for i in range(4)]
                    if n:
                        cf[1], cf[2] = cf[2], cf[1]
                    settle()
                    for i, (src, k) in enumerate(((c0, 0), (c1, 1), (c0, 2), (c1, 3))):
                        run(gp.tensor_scalar(TMPH[:, i, 0:width], m[:, src, :], cf[k], None, ALU.mult))
                    settle()
                    run(gp.tensor_tensor(m[:, c0, :], TMPH[:, 0, 0:width], TMPH[:, 1, 0:width], ALU.add))
                    run(gp.tensor_tensor(m[:, c1, :], TMPH[:, 2, 0:width], TMPH[:, 3, 0:width], ALU.add))

            eye(bufs[0])
            for n in range(LOW):
                low(n, bufs[n % 2], bufs[1 - n % 2])
            settle()
            gp.nop().then_inc(e_up, 1)
            eye(bufs[0])
            order = [0, 2]
            for n in range(LOW):
                low(LOW + n, bufs[order[n % 2]], bufs[order[1 - n % 2]])
            gp.wait_ge(c_in, 16 * 14)
            gp.wait_ge(zeroed, 48)
            for st in reversed(range(HIGH)):
                high(1, Z, D, st)
            settle()
            gp.nop().then_inc(z_high, 1)
            gp.wait_ge(rt_sb, KF)
            for st in range(HIGH):
                high(0, RT, W1P, st)
            settle()
            run(gp.tensor_tensor(BH[:, :], RT[:, :, D], UPB[:, :], ALU.add))
            settle()
            gp.nop().then_inc(rt_high, 1)

            gp.wait_ge(ys_out, 16 * NT)

            def gather(b):
                if b:
                    gp.wait_ge(x2_added, TB * b)
                for q in range(TB):
                    t = TB * b + q
                    gp.indirect_dma_start(out=YG[:, q, :], out_offset=None, in_=ys,
                                          in_offset=bass.IndirectOffsetOnAxis(ap=POS[:, t:t + 1], axis=0))\
                        .then_inc(gathered, 16)

            def roots(g):
                gp.wait_ge(c["c_eps"], TB * (g + 1))
                gp.tensor_tensor(RS[:, :], VE[:, :], spread(MHALF[:, :], 1, TB), ALU.pow)\
                    .then_inc(c["c_rstd"], 1)

            gather(0)
            for b in range(B):
                if b + 1 < B:
                    gather(b + 1)
                roots(2 * b - 1 if b else 0)
                if b:
                    roots(2 * b)
            roots(2 * B - 1)

        @block.tensor
        def _(pe):
            def product(dst, lhs, rhs, chunks, signal=None):
                for k in range(chunks):
                    last = pe.matmul(dst, lhs(k), rhs(k), start=(k == 0), stop=(k == chunks - 1))
                if signal is not None:
                    last.then_inc(signal, 1)

            def flip(bank, src, signal, n=KD):
                for k in range(n):
                    last = pe.transpose(bank[:, k * P:(k + 1) * P], src[:, k * P:(k + 1) * P], IDENT[:, :])
                last.then_inc(signal, 1)

            pe.nop().then_inc(slot_uses, 1)
            pe.wait_ge(consts, 6)
            W1 = SLOT[:, 2, 0:KD * F].rearrange("p (k f) -> p k f", k=KD)
            W2 = SLOT[:, 2, KD * F:2 * KD * F].rearrange("p (k f) -> p k f", k=KD)
            W3 = SLOT[:, 2, 2 * KD * F:WS].rearrange("p (c d) -> p c d", c=KF)

            def up_half(t3, hf):
                n = 2 * num(t3) + hf
                for bank, w, done, free in ((PB[6], W1, "h1_done", "gelu_done"),
                                            (PB[7], W2, "h2_done", "mult_done")):
                    if not (first(t3, 1) and hf == 0):
                        pe.wait_ge(s[free], n)
                    for q in range(4):
                        m = 4 * hf + q
                        product(bank[:, q * P:(q + 1) * P], lambda k: w[:, k, m * P:(m + 1) * P],
                                lambda k: X2T[:, k, :], KD, s[done] if q == 3 else None)

            def step(of):
                t0, t2, t3, t4 = of(0), of(2), of(3), of(4)
                if t4 is not None:
                    n = num(t4)
                    pe.wait_ge(s["mult_done"], 2 * n + 2)
                    if t3 is not None:
                        pe.wait_ge(s["x1_ready"], n + 2)
                    product(PB[5][:, 0:D], lambda k: HA[:, k, :], lambda k: W3[:, k, :], KF, s["y_done"])
                if t0 is not None:
                    n = num(t0)
                    pe.wait_ge(s["xn_ready"], n + 1)
                    if not first(t0, 1):
                        pe.wait_ge(s["xT_sb"], n)
                    flip(PB[0], XN[:, :], s["xT_done"])
                if t3 is not None:
                    n3 = num(t3)
                    pe.wait_ge(s["xn2_ready"], n3 + 1)
                    pe.wait_ge(s["aT_sb"], n3 + 1)
                    flip(PB[3], XH[:, :], s["x2T_done"])
                if t0 is not None:
                    if first(t0, 1):
                        pe.wait_ge(w_in, 32)
                    pe.wait_ge(s["xT_sb"], n + 1)
                    if not first(t0, 2):
                        pe.wait_ge(s["qk_prod"], n - 1)
                    product(PB[1 + t0[1]][:, 0:D], lambda k: XT[:, k, :], lambda k: WQ0[:, k, :], KD,
                            s["q_done"])
                    pe.wait_ge(tile_in[t0[1]], 32 * t0[0] + 32)
                    if not first(t0, 1):
                        pe.wait_ge(s["kv_sb"], n)
                    product(PB[4][:, :], lambda k: CTX[:, t0[1], k, :], lambda k: WKV0[:, k, :], KD,
                            s["kv_done"])
                if t3 is not None:
                    if first(t3, 1):
                        pe.wait_ge(wg_in, 48)
                        pe.wait_ge(slot_in[2], 16)
                    pe.wait_ge(s["x2T_sb"], n3 + 1)
                    if not first(t3, 1):
                        pe.wait_ge(s["y_added"], n3)
                    product(PB[5][:, 0:NE], lambda k: X2T[:, k, :], lambda k: WG[:, k, :], KD,
                            s["gate_done"])
                    up_half(t3, 0)
                if t2 is not None:
                    n2 = num(t2)
                    pe.wait_ge(s["a_ready"], n2 + 1)
                    if t3 is not None:
                        pe.wait_ge(s["x2T_sb"], n3 + 1)
                    elif not first(t2, 1):
                        pe.wait_ge(s["aT_sb"], n2)
                    flip(PB[3], AO[:, :], s["aT_done"])
                    if first(t2, 1):
                        pe.wait_ge(wg_in, 48)
                    pe.wait_ge(s["aT_sb"], n2 + 1)
                    if t3 is not None:
                        pe.wait_ge(s["lg_sb"], n3 + 1)
                    product(PB[5][:, 0:D], lambda k: AT[:, k, :], lambda k: WO0[:, k, :], KD, s["o_done"])
                if t3 is not None:
                    up_half(t3, 1)

            sweep_a(pe, step)

            pe.wait_ge(s["oh_ok"], T)
            pe.matmul(PB[1][:, 0:T * NE], ABOVE[:, :], OH[:, :, :].rearrange("p t e -> p (t e)"),
                      start=True, stop=False)
            for t in range(T - 1):
                last = pe.matmul(PB[1][:, (t + 1) * NE:T * NE].rearrange("p (t e) -> p t e", e=NE), ONES[:, :],
                                 spread(OH[:, t:t + 1, :], 1, T - 1 - t), start=False, stop=(t == T - 2))
            last.then_inc(rank_ps, 1)
            for t in range(T):
                last = pe.matmul(PB[2][:, 0:NE], ONES[:, :], OH[:, t, :], start=(t == 0), stop=(t == T - 1))
            last.then_inc(rank_ps, 1)

            pe.wait_ge(tables, 1)

            def step_b(of):
                t0, t1, t2 = of(0), of(1), of(2)
                if t0 is not None:
                    n = num(t0)
                    pe.wait_ge(xs_in[t0[1]], 16 * t0[0] + 16)
                    if not first(t0, 1):
                        pe.wait_ge(e["sT_sb"], n)
                    flip(PB[0], XS[:, t0[1], :], e["sT_done"])
                if t1 is not None:
                    n = num(t1)
                    slot, *counts = [pe.value_load(TAB[0:1, r, bass.ds(n, 1)], min_val=lo, max_val=hi)
                                     for r, (lo, hi) in enumerate([(0, SLOTS - 1)] + SLOTS * [(16, 64)])]
                    for k in range(SLOTS):
                        pe.wait_ge(slot_in[k], counts[k])
                    pe.wait_ge(e["sT_sb"], n + 1)
                    for hf in range(2):
                        for bank, at, done, free in ((PB[1 + hf], 0, "b_h1", "b_gelu"),
                                                     (PB[3 + hf], KD * F, "b_h2", "b_mult")):
                            if not first(t1, 1):
                                pe.wait_ge(e[free], 2 * n + hf - 1)
                            product(bank[:, :], lambda k: XST[:, t1[1], k, :],
                                    lambda k: SLOT[:, bass.ds(slot, 1), at + k * F + hf * 512:
                                                   at + k * F + hf * 512 + 512].rearrange("p o f -> p (o f)"),
                                    KD, e[done])
                if t2 is not None:
                    n = num(t2)
                    for r, free in enumerate(("hT_a", "hT_d")):
                        pe.wait_ge(e["b_mult"], 2 * n + 1 + r)
                        if not first(t2, 1):
                            pe.wait_ge(e[free], n)
                        flip(PB[5 + r], HB[:, t2[1], r * 512:(r + 1) * 512], e["hT_done"], 4)
                    slot = pe.value_load(TAB[0:1, 0, bass.ds(n, 1)], min_val=0, max_val=SLOTS - 1)
                    pe.wait_ge(e["hT_a"], n + 1)
                    pe.wait_ge(e["hT_d"], n + 1)
                    if not first(t2, 1):
                        pe.wait_ge(e["by_sb"], n)
                    product(PB[7][:, 0:D], lambda k: HBT[:, k, :],
                            lambda k: SLOT[:, bass.ds(slot, 1), 2 * KD * F + k * D:
                                           2 * KD * F + (k + 1) * D].rearrange("p o f -> p (o f)"),
                            KF, slot_uses)

            def fold_up():
                pe.wait_ge(e_up, 1)
                pe.wait_ge(c_in, 16 * 14)
                pe.wait_ge(e["sT_sb"], 2 * PAUSE)
                pe.wait_ge(e["by_sb"], 2 * PAUSE - 2)
                for m in range(KF):
                    if m >= 2:
                        pe.wait_ge(rt_sb, m - 1)
                    product(PB[0 if m % 2 == 0 else 7][:, 0:W1P], lambda k: EB[:, 1, m * P:(m + 1) * P],
                            lambda k: WET[:, m, :], 1, rt_ps)
                pe.wait_ge(rt_sb, KF)

            sweep_b(pe, step_b, fold_up)

            def fill(b, n, make):
                before = ring_before(b, n)
                if not (isinstance(before, int) and before == 0):
                    pe.wait_ge(ring_free[n % 2], before)
                make(PB[6 + n % 2], ring_full[n % 2])

            def flips(b, g):
                for q in range(TB):
                    f = TB * g + q
                    pe.wait_ge(c["c_xn"], f + 1)
                    if not (isinstance(f, int) and f < 2):
                        pe.wait_ge(c["c_xT_sb"], f - 1)
                    if q == 1 and not (isinstance(b, int) and b == 0):
                        pe.wait_ge(c["cT_sb"], TB * b)
                    flip(PB[0 if q % 2 == 0 else 5], XNC[:, q % 2, :], c["c_xT"])
                pe.wait_ge(c["c_xT_sb"], TB * g + TB)

            def wide(w, m, rhs):
                return lambda bank, full: product(bank[:, :], lambda k: w[:, k, m * P:(m + 1) * P],
                                                  lambda k: rhs[:, k, :], KD, full)

            def values(r):
                def make(bank, full):
                    for h in range(2):
                        q = 2 * r + h
                        product(bank[:, h * D:(h + 1) * D], lambda k: CTXB[:, k, q * P:(q + 1) * P],
                                lambda k: WV1[:, k, :], KD, full if h else None)
                return make

            def down(q):
                return lambda bank, full: product(bank[:, 0:D], lambda k: H4[:, k, q * P:(q + 1) * P],
                                                  lambda k: MDN[:, k, :], KF, full)

            def piece(b, n):
                if n < 4:
                    for m in (2 * n, 2 * n + 1):
                        fill(b, 6 + m, wide(WEFF, m, XN4T))
                else:
                    if n == 4:
                        pe.wait_ge(ring_free[0], ring_before(b, 12) + 1)
                        pe.wait_ge(ring_free[1], ring_before(b, 13) + 1)
                    fill(b, 10 + n, down(n - 4))

            def step_cd(b, has_c, has_d):
                if has_c:
                    flips(b, norm_c(b))
                    for m in range(KD):
                        fill(b, m, wide(WQ1, m, XN3T))
                    pe.wait_ge(ctx_in, 16 * b + 16)
                    for m in range(KD):
                        fill(b, 2 + m, wide(WK1, m, CTXB))
                    for r in range(2):
                        fill(b, 4 + r, values(r))
                    for n in (4, 5):
                        pe.wait_ge(ring_free[n % 2], ring_before(b, n) + 1)
                if has_d:
                    flips(b, norm_d(b))
                    if not has_c:
                        for n in range(8):
                            piece(b, n)
                        return

                def out_product(q):
                    n = TB * b + q
                    pe.wait_ge(c["cT_sb"], n + 1)
                    if not (isinstance(n, int) and n == 0):
                        pe.wait_ge(c["x3_ready"], n)
                    product(PB[4][:, 0:D], lambda k: CT[:, k, :], lambda k: WO1[:, k, :], KD, c["out_done"])

                def flip_c(q):
                    n = TB * b + q
                    pe.wait_ge(c["c_ready"], n + 1)
                    if not (isinstance(n, int) and n == 0):
                        pe.wait_ge(c["cT_sb"], n)
                    flip(PB[5], CC, c["cT_done"])

                for q in range(TB):
                    n = TB * b + q
                    if not (isinstance(n, int) and n == 0):
                        pe.wait_ge(c["p_done"], n)
                    product(PB[1][:, :], lambda k: QT[:, k, q * P:(q + 1) * P], lambda k: K1T[:, k, :], KD,
                            c["sc_done"])
                    if q:
                        flip_c(q - 1)
                    if has_d:
                        piece(b, 2 * q)
                    pe.wait_ge(c["p_done"], n + 1)
                    if not (isinstance(n, int) and n == 0):
                        pe.wait_ge(c["pT_sb"], n)
                    flip(PB[2], PS[:, q % 2, :], c["pT_done"], TB)
                    if q:
                        out_product(q - 1)
                    if has_d:
                        piece(b, 2 * q + 1)
                    pe.wait_ge(c["pT_sb"], n + 1)
                    if not (isinstance(n, int) and n == 0):
                        pe.wait_ge(c["c_ready"], n)
                    product(PB[3][:, 0:D], lambda k: PT[:, k, :], lambda k: V1[:, k, :], TB, c["av_done"])
                flip_c(TB - 1)
                out_product(TB - 1)

            def fold_down():
                pe.wait_ge(rt_high, 1)
                for n in range(KF):
                    k, m0 = n // 4, 2 * (n % 4)
                    if n >= 2:
                        pe.wait_ge(wm_sb, n - 1)
                    for h in range(2):
                        last = pe.transpose(PB[6 + n % 2][:, h * P:(h + 1) * P],
                                            RT[:, m0 + h, k * P:(k + 1) * P], IDENT[:, :])
                    last.then_inc(wm_ps, 1)
                for m in range(KF):
                    pe.wait_ge(wm_sb, KF + m - 1)
                    product(PB[6 + m % 2][:, 0:D], lambda k: EC[:, m * P:(m + 1) * P],
                            lambda k: Z[:, m, :], 1, wm_ps)
                pe.wait_ge(wm_sb, 2 * KF)

            pe.wait_ge(c_in, 16 * 14)
            step_cd(0, True, False)
            fold_down()
            with pe.Fori(1, B) as b:
                step_cd(b, True, True)
            step_cd(B, False, True)

        @block.scalar
        def _(act):
            act.wait_ge(wg_in, 48)
            act.activation(TG[:, :], GATE[:, :], ACT.Tanh).then_inc(tanh_s, 1)

            def step(of):
                t0, t1, t2, t3 = of(0), of(1), of(2), of(3)
                if t1 is not None:
                    n = num(t1)
                    act.wait_ge(s["shifted"], n + 1)
                    if not first(t1, 2):
                        act.wait_ge(s["av_half"], 2 * n - 2)
                        act.wait_ge(s["sums"], n - 1)
                    act.activation(PR[:, t1[1], :], SC[:, :], ACT.Exp, scale=float(DK) ** -0.5)\
                        .then_inc(s["exp_done"], 1)
                if t0 is not None:
                    act.wait_ge(s["xT_done"], num(t0) + 1)
                    act.activation(XT[:, :, :].rearrange("p k t -> p (k t)"), PB[0][:, 0:D], ACT.Copy)\
                        .then_inc(s["xT_sb"], 1)
                if t3 is not None:
                    act.wait_ge(s["x2T_done"], num(t3) + 1)
                    act.activation(X2T[:, :, :].rearrange("p k t -> p (k t)"), PB[3][:, 0:D], ACT.Copy)\
                        .then_inc(s["x2T_sb"], 1)
                    act.wait_ge(s["xn2_ready"], num(t3) + 1)
                    act.activation(XN2[:, num(t3), :], XH[:, :], ACT.Copy).then_inc(s["xn2_kept"], 1)
                if t0 is not None:
                    n = num(t0)
                    act.wait_ge(s["kv_done"], n + 1)
                    if not first(t0, 2):
                        act.wait_ge(s["qk_prod"], n - 1)
                        act.wait_ge(s["av_half"], 2 * n - 2)
                    act.activation(KV[:, t0[1], :], PB[4][:, :], ACT.Copy).then_inc(s["kv_sb"], 1)

                def gelu(hf):
                    n = 2 * num(t3) + hf
                    act.wait_ge(s["h1_done"], n + 1)
                    if not first(t3, 1):
                        act.wait_ge(s["mult_done"], n - 1)
                    act.activation(G[:, hf * 512:(hf + 1) * 512], PB[6][:, :], ACT.Gelu)\
                        .then_inc(s["gelu_done"], 1)

                if t3 is not None:
                    gelu(0)
                if t2 is not None:
                    act.wait_ge(s["aT_done"], num(t2) + 1)
                    act.activation(AT[:, :, :].rearrange("p k t -> p (k t)"), PB[3][:, 0:D], ACT.Copy)\
                        .then_inc(s["aT_sb"], 1)
                if t3 is not None:
                    gelu(1)

            sweep_a(act, step)

            def load_rows(jp):
                act.dma_start(XS[:, jp[1], :], xs[bass.ds(num(jp) * P, P), :]).then_inc(xs_in[jp[1]], 16)

            act.wait_ge(scattered, 16 * T)
            load_rows((0, 0))
            load_rows((0, 1))

            def step_b(of):
                t0, t1, t2 = of(0), of(1), of(2)
                if t0 is not None:
                    n = num(t0)
                    act.wait_ge(e["sT_done"], n + 1)
                    act.activation(XST[:, t0[1], :, :].rearrange("p k t -> p (k t)"), PB[0][:, 0:D], ACT.Copy)\
                        .then_inc(e["sT_sb"], 1)
                    if not isinstance(n, int) or n + 2 < NT:
                        load_rows((t0[0] + 1, t0[1]))
                if t1 is not None:
                    n = num(t1)
                    for hf in range(2):
                        act.wait_ge(e["b_h1"], 2 * n + hf + 1)
                        if not first(t1, 1):
                            act.wait_ge(e["b_mult"], 2 * n + hf - 1)
                        act.activation(G[:, hf * 512:(hf + 1) * 512], PB[1 + hf][:, :], ACT.Gelu)\
                            .then_inc(e["b_gelu"], 1)
                if t2 is not None:
                    n = num(t2)
                    act.wait_ge(e["hT_done"], 2 * n + 1)
                    act.activation(HBT[:, 0:4, :].rearrange("p k t -> p (k t)"), PB[5][:, :], ACT.Copy)\
                        .then_inc(e["hT_a"], 1)
                    act.wait_ge(slot_uses, n + 2)
                    if not first(t2, 1):
                        act.wait_ge(ys_out, 16 * n)
                    act.activation(YS[:, :], PB[7][:, 0:D], ACT.Copy).then_inc(e["by_sb"], 1)
                    act.wait_ge(e["by_sb"], n + 1)
                    act.dma_start(ys[bass.ds(n * P, P), :], YS[:, :]).then_inc(ys_out, 16)

            def fold_up():
                act.wait_ge(scattered, 16 * T)
                for m in range(KF):
                    act.wait_ge(rt_ps, m + 1)
                    act.activation(RT[:, m, :], PB[0 if m % 2 == 0 else 7][:, 0:W1P], ACT.Copy)\
                        .then_inc(rt_sb, 1)

            sweep_b(act, step_b, fold_up)

            def take(b, n, out, func, src=slice(0, 512), bias=None):
                act.wait_ge(ring_full[n % 2], ring_before(b, n) + 1)
                extra = {} if bias is None else {"bias": bias}
                act.activation(out, PB[6 + n % 2][:, src], func, **extra).then_inc(ring_free[n % 2], 1)

            def copies(g, dst):
                for q in range(TB):
                    act.wait_ge(c["c_xT"], TB * g + q + 1)
                    act.activation(dst[:, :, q * P:(q + 1) * P],
                                   PB[0 if q % 2 == 0 else 5][:, 0:D].rearrange("p (k t) -> p k t", k=KD),
                                   ACT.Copy).then_inc(c["c_xT_sb"], 1)

            def piece(b, n):
                if n < 4:
                    for m in (2 * n, 2 * n + 1):
                        take(b, 6 + m, H4[:, m, :], ACT.Gelu, bias=BH[:, m:m + 1])

            def step_cd(b, has_c, has_d):
                if has_c:
                    copies(norm_c(b), XN3T)
                    for m in range(KD):
                        take(b, m, QT[:, m, :], ACT.Identity, bias=BQ[:, m:m + 1])
                    for m in range(KD):
                        take(b, 2 + m, K1T[:, m, :], ACT.Copy)
                if has_d:
                    copies(norm_d(b), XN4T)
                    if not has_c:
                        for n in range(4):
                            piece(b, n)
                        return
                for q in range(TB):
                    n = TB * b + q
                    if q:
                        copy_c(n - 1)
                    act.wait_ge(c["nmax_s"], n + 1)
                    if not (isinstance(n, int) and n < 2):
                        act.wait_ge(c["pT_done"], n - 1)
                        act.wait_ge(c["rinv"], n - 1)
                    act.activation(PS[:, q % 2, :], PB[1][:, :], ACT.Exp, bias=NMS[:, q % 2:q % 2 + 1],
                                   scale=float(D) ** -0.5, accum_out=SU[:, q % 2:q % 2 + 1])\
                        .then_inc(c["p_done"], 1)
                    if has_d:
                        piece(b, 2 * q)
                    act.wait_ge(c["pT_done"], n + 1)
                    act.activation(PT.rearrange("p k t -> p (k t)"), PB[2][:, :], ACT.Copy)\
                        .then_inc(c["pT_sb"], 1)
                    if has_d:
                        piece(b, 2 * q + 1)
                copy_c(TB * b + TB - 1)

            def copy_c(n):
                act.wait_ge(c["cT_done"], n + 1)
                act.activation(CT.rearrange("p k t -> p (k t)"), PB[5][:, 0:D], ACT.Copy)\
                    .then_inc(c["cT_sb"], 1)

            step_cd(0, True, False)
            for n in range(KF):
                k, m0 = n // 4, 2 * (n % 4)
                act.wait_ge(wm_ps, n + 1)
                act.activation(WEFF[:, k, m0 * P:(m0 + 2) * P], PB[6 + n % 2][:, 0:2 * P], ACT.Copy)\
                    .then_inc(wm_sb, 1)
            for m in range(KF):
                act.wait_ge(wm_ps, KF + m + 1)
                act.activation(MDN[:, m, :], PB[6 + m % 2][:, 0:D], ACT.Copy).then_inc(wm_sb, 1)
            with act.Fori(1, B) as b:
                step_cd(b, True, True)
            step_cd(B, False, True)

        @block.vector
        def _(dve):
            def hold(signal, value):
                dve.wait_ge(signal, value)
                if not isinstance(value, int):
                    dve.sem_inc(held, 1)

            def step(of):
                t0, t1, t2, t3, t4 = of(0), of(1), of(2), of(3), of(4)
                if t1 is not None:
                    n, par = num(t1), t1[1]
                    dve.wait_ge(s["q_done"], n + 1)
                    dve.wait_ge(s["kv_sb"], n + 1)
                    prod = PRODQ[:, :].rearrange("p (i j h) -> p i j h", i=DK, j=DK)
                    dve.tensor_tensor(
                        prod,
                        spread(PB[1 + par][:, 0:D].rearrange("p (i o h) -> p i o h", i=DK, o=1), 2, DK),
                        spread(KV[:, par, 0:D].rearrange("p (o j h) -> p o j h", o=1, j=DK), 1, DK),
                        ALU.mult).then_inc(s["qk_prod"], 1)
                if t4 is not None:
                    mult(t4, 1)
                if t1 is not None:
                    dve.wait_ge(s["qk_prod"], n + 1)
                    if not first(t1, 1):
                        dve.wait_ge(s["exp_done"], n)
                    dve.tensor_reduce(SC[:, :].rearrange("p (i j) -> p i j", i=DK), prod, AX.X, ALU.add)\
                        .then_inc(s["scores"], 1)
                if t3 is not None:
                    n3 = num(t3)
                    dve.wait_ge(s["o_done"], n3 + 1)
                    if first(t3, 1):
                        dve.wait_ge(tanh_s, 1)
                    dve.scalar_tensor_tensor(X[:, n3, :], PB[5][:, 0:D], TG[:, 0:1], X[:, n3, :],
                                             ALU.mult, ALU.add).then_inc(s["x1_ready"], 1)
                if t0 is not None:
                    n0 = num(t0)
                    hold(tile_in[t0[1]], 32 * t0[0] + 32)
                    dve.bn_stats(ST[:, 0, :], X[:, n0, :]).then_inc(s["ln1_stats"], 1)
                if t3 is not None:
                    hold(s["x1_ready"], n3 + 1)
                    dve.bn_stats(ST[:, 1, :], X[:, n3, :]).then_inc(s["ln2_stats"], 1)
                if t1 is not None:
                    dve.wait_ge(s["scores"], n + 1)
                    dve.tensor_reduce(SM[:, 0, :], SC[:, :].rearrange("p (i j) -> p i j", i=DK), AX.X, ALU.max)\
                        .then_inc(s["rowmax"], 1)
                for tt, r, nm in ((t0, 0, "ln1"), (t3, 1, "ln2")):
                    if tt is not None:
                        hold(s[nm + "_stats"], num(tt) + 1)
                        dve.bn_aggr(MV[:, r, 0:2], ST[:, r, :]).then_inc(s[nm + "_agg"], 1)
                if t1 is not None:
                    dve.wait_ge(s["rowmax"], n + 1)
                    dve.tensor_tensor(SC[:, :].rearrange("p (i j) -> p i j", i=DK),
                                      SC[:, :].rearrange("p (i j) -> p i j", i=DK),
                                      spread(SM[:, 0, :].rearrange("p (i o) -> p i o", o=1), 2, DK),
                                      ALU.subtract).then_inc(s["shifted"], 1)
                for tt, r, nm in ((t3, 1, "ln2"), (t0, 0, "ln1")):
                    if tt is not None:
                        dve.wait_ge(s[nm + "_agg"], num(tt) + 1)
                        dve.tensor_scalar(MV[:, r, 2:3], MV[:, r, 1:2], EPS, None, ALU.add)\
                            .then_inc(s[nm + "_eps"], 1)
                if t2 is not None:
                    n2 = num(t2)
                    dve.wait_ge(s["exp_done"], n2 + 1)
                    dve.tensor_reduce(SM[:, 1, :], PR[:, t2[1], :].rearrange("p (i j) -> p i j", i=DK),
                                      AX.X, ALU.add).then_inc(s["sums"], 1)
                if t3 is not None:
                    dve.wait_ge(s["ln2_rstd"], n3 + 1)
                    if not first(t3, 1):
                        dve.wait_ge(s["x2T_done"], n3)
                        dve.wait_ge(s["xn2_kept"], n3)
                    dve.tensor_scalar(XH[:, :], X[:, n3, :], MV[:, 1, 0:1], MV[:, 1, 3:4],
                                      ALU.subtract, ALU.mult).then_inc(s["xn2_ready"], 1)
                if t0 is not None:
                    dve.wait_ge(s["ln1_rstd"], n0 + 1)
                    if not first(t0, 1):
                        dve.wait_ge(s["xT_done"], n0)
                    dve.tensor_scalar(XN[:, :], X[:, n0, :], MV[:, 0, 0:1], MV[:, 0, 3:4],
                                      ALU.subtract, ALU.mult).then_inc(s["xn_ready"], 1)
                if t2 is not None:
                    dve.wait_ge(s["sums"], n2 + 1)
                    dve.reciprocal(RI[:, :], SM[:, 1, :]).then_inc(s["recip"], 1)
                    if not first(t2, 1):
                        dve.wait_ge(s["aT_done"], n2)
                    aov = AO[:, :].rearrange("p (i h) -> p i h", i=DK)
                    for hf in range(2):
                        H2 = NH // 2
                        dve.wait_ge(s["av_half"], 2 * n2 + hf + 1)
                        dve.tensor_reduce(
                            aov[:, :, hf * H2:(hf + 1) * H2],
                            PRODV[:, :].rearrange("p (f i h j) -> p f i h j", f=2, i=DK, h=H2)[:, hf],
                            AX.X, ALU.add).then_inc(s["av_read"], 1)
                    dve.wait_ge(s["av_read"], 2 * n2 + 2)
                    dve.wait_ge(s["recip"], n2 + 1)
                    dve.tensor_tensor(aov, aov, spread(RI[:, :].rearrange("p (i o) -> p i o", o=1), 2, NH),
                                      ALU.mult).then_inc(s["a_ready"], 1)
                if t4 is not None:
                    n4 = num(t4)
                    dve.wait_ge(s["y_done"], n4 + 1)
                    dve.scalar_tensor_tensor(X[:, n4, :], PB[5][:, 0:D], TG[:, 2:3], X[:, n4, :],
                                             ALU.mult, ALU.add).then_inc(s["y_added"], 1)
                if t3 is not None:
                    dve.wait_ge(s["gate_done"], n3 + 1)
                    dve.tensor_copy(LG[:, :], PB[5][:, 0:NE]).then_inc(s["lg_sb"], 1)
                    hold(s["lg_sb"], n3 + 1)
                    dve.max(TOP[:, :], LG[:, :]).then_inc(s["top_ok"], 1)
                    hold(s["top_ok"], n3 + 1)
                    dve.max_index(TOPI[:, :], TOP[:, :], LG[:, :]).then_inc(s["topi_ok"], 1)
                    mult(t3, 0)
                    dve.wait_ge(s["topi_ok"], n3 + 1)
                    dve.tensor_copy(TOPF[:, :], TOPI[:, 0:1]).then_inc(s["topf_ok"], 1)
                    if first(t3, 1):
                        dve.wait_ge(iotaf, 3)
                    dve.wait_ge(s["topf_ok"], n3 + 1)
                    dve.tensor_scalar(OH[:, n3, :], IOTA8[:, :], TOPF[:, :], None, ALU.is_equal)\
                        .then_inc(s["oh_ok"], 1)

            def mult(t, hf):
                n = 2 * num(t) + hf
                dve.wait_ge(s["gelu_done"], n + 1)
                dve.wait_ge(s["h2_done"], n + 1)
                dve.tensor_tensor(HA[:, 4 * hf:4 * hf + 4, :].rearrange("p k t -> p (k t)"),
                                  PB[7][:, :], G[:, hf * 512:(hf + 1) * 512], ALU.mult)\
                    .then_inc(s["mult_done"], 1)

            dve.wait_ge(iotas, 3)
            dve.tensor_copy(IOTA8[:, :], IOTAI[:, 0:NE]).then_inc(iotaf, 1)
            dve.tensor_copy(IOTAM[:, :], IOTAI[:, NE:NE + T]).then_inc(iotaf, 1)
            dve.tensor_copy(IOTAT[:, :], IOTAI[0:1, NE + T:NE + T + NT]).then_inc(iotaf, 1)
            sweep_a(dve, step)

            steps = [0]

            def link(ins):
                steps[0] += 1
                ins.then_inc(route, 1)
                dve.wait_ge(route, steps[0])

            def row(v, n, parts=P):
                return spread(v.rearrange("p (o e) -> p o e", o=1), 1, n)

            def col(v, n):
                return spread(v.rearrange("p (e o) -> p e o", o=1), 2, n)

            def grid(v, a):
                return v.rearrange("p (a b) -> p a b", a=a)

            link(dve.tensor_tensor(LESS[:, :, :], row(IOTA8[:, :], NE), col(IOTA8[:, :], NE), ALU.is_lt))
            dve.wait_ge(rank_ps, 2)
            link(dve.tensor_copy(NTE[:, :], PB[2][:, 0:NE]))
            link(dve.tensor_tensor(grid(CMP[:, :], NE), col(NTE[:, :], T), row(IOTAM[:, :], NE), ALU.is_gt))
            link(dve.tensor_reduce(NTE[:, :], grid(CMP[:, :], NE), AX.X, ALU.add))
            link(dve.tensor_tensor(LESS[:, :, :], LESS[:, :, :], row(NTE[:, :], NE), ALU.mult))
            link(dve.tensor_reduce(BASE[:, :], LESS[:, :, :], AX.X, ALU.add))
            link(dve.tensor_scalar(NTE[:, :], BASE[:, :], float(P), None, ALU.mult))
            link(dve.tensor_tensor(RANK[:, :, :], row(NTE[:, :], T), grid(PB[1][:, 0:T * NE], T), ALU.add))
            link(dve.tensor_tensor(RANK[:, :, :], RANK[:, :, :], OH[:, :, :], ALU.mult))
            link(dve.tensor_reduce(POSF[:, :], RANK[:, :, :], AX.X, ALU.add))
            dve.tensor_copy(POS[:, :], POSF[:, :]).then_inc(pos_ready, 1)
            b1 = BASE[0:1, :]
            link(dve.tensor_tensor(GE[:, :, :], row(b1, NT), col(IOTAT[:, :], NE), ALU.is_le))
            link(dve.tensor_reduce(EI[:, :], GE[:, :, :], AX.X, ALU.add))
            link(dve.tensor_scalar(EI[:, :], EI[:, :], -1.0, None, ALU.add))
            link(dve.tensor_tensor(GE[:, :, :], row(IOTA8[0:1, :], NT), col(EI[:, :], NE), ALU.is_le))
            for k, (lo, hi) in enumerate(((3, 6), (4, 7), (2, 5))):
                link(dve.tensor_tensor(SUM2[:, k, :], GE[:, :, lo], GE[:, :, hi], ALU.add))
                link(dve.tensor_scalar(TAB[:, 1 + k, :], SUM2[:, k, :], 16.0, 16.0, ALU.mult, ALU.add))
            link(dve.scalar_tensor_tensor(TAB[:, 0, :], SUM2[:, 0, :], -3.0, EI[:, :], ALU.mult, ALU.add))
            dve.tensor_scalar(BASEI[:, :], b1, 1.0, None, ALU.add).then_inc(tables, 1)

            def step_b(of):
                t1, t2 = of(1), of(2)
                if t1 is not None:
                    n = num(t1)
                    for hf in range(2):
                        dve.wait_ge(e["b_gelu"], 2 * n + hf + 1)
                        dve.wait_ge(e["b_h2"], 2 * n + hf + 1)
                        if not first(t1, 2):
                            dve.wait_ge(e["hT_done"], 2 * n - 2)
                        dve.tensor_tensor(HB[:, t1[1], hf * 512:(hf + 1) * 512], PB[3 + hf][:, :],
                                          G[:, hf * 512:(hf + 1) * 512], ALU.mult).then_inc(e["b_mult"], 1)
                if t2 is not None:
                    n = num(t2)
                    dve.wait_ge(e["hT_done"], 2 * n + 2)
                    dve.tensor_copy(HBT[:, 4:8, :].rearrange("p k t -> p (k t)"), PB[6][:, :])\
                        .then_inc(e["hT_d"], 1)

            sweep_b(dve, step_b, lambda: None)

            dve.wait_ge(c_in, 16 * 14)
            dve.tensor_tensor(BCD[:, :], BIAS[:, 2, :], BIAS[:, 3, :], ALU.add).then_inc(bcd_ready, 1)

            def norm(t0, g):
                for q in range(TB):
                    dve.bn_stats(STC[:, q, :], X[:, t0 + q, :]).then_inc(c["c_stats"], 1)
                for q in range(TB):
                    hold(c["c_stats"], TB * g + q + 1)
                    dve.bn_aggr(MVC[:, q, :], STC[:, q, :]).then_inc(c["c_agg"], 1)
                for q in range(TB):
                    dve.wait_ge(c["c_agg"], TB * g + q + 1)
                    dve.tensor_scalar(VE[:, q:q + 1], MVC[:, q, 1:2], EPS, None, ALU.add).then_inc(c["c_eps"], 1)
                dve.wait_ge(c["c_rstd"], g + 1)
                for q in range(TB):
                    f = TB * g + q
                    if not (isinstance(f, int) and f < 2):
                        dve.wait_ge(c["c_xT"], f - 1)
                    dve.tensor_scalar(XNC[:, q % 2, :], X[:, t0 + q, :], MVC[:, q, 0:1], RS[:, q:q + 1],
                                      ALU.subtract, ALU.mult).then_inc(c["c_xn"], 1)

            def finish(b, q):
                m = TB * b - TB + q
                dve.wait_ge(ring_full[q % 2], ring_before(b, 14 + q) + 1)
                if isinstance(m, int) or q:
                    dve.wait_ge(c["fin_ready"], m)
                dve.tensor_tensor(TY, PB[6 + q % 2][:, 0:D], BCD[:, :], ALU.add).then_inc(ring_free[q % 2], 1)
                dve.wait_ge(ring_free[q % 2], ring_before(b, 14 + q) + 1)
                dve.scalar_tensor_tensor(X[:, m, :], TY, TG[:, 3:4], X[:, m, :], ALU.mult, ALU.add)\
                    .then_inc(c["fin_ready"], 1)

            def step_cd(b, has_c, has_d):
                if has_c:
                    dve.wait_ge(gathered, 16 * TB * b + 16 * TB)
                    for q in range(TB):
                        dve.scalar_tensor_tensor(X[:, TB * b + q, :], YG[:, q, :], TG[:, 2:3], X[:, TB * b + q, :],
                                                 ALU.mult, ALU.add).then_inc(x2_added, 1)
                    hold(x2_added, TB * b + TB)
                    norm(TB * b, norm_c(b))
                    for r in range(2):
                        dve.wait_ge(ring_full[r], ring_before(b, 4 + r) + 1)
                        dve.tensor_copy(V1[:, 2 * r:2 * r + 2, :].rearrange("p t d -> p (t d)"), PB[6 + r][:, :])\
                            .then_inc(ring_free[r], 1)
                if has_d:
                    hold(c["x3_ready"], TB * b)
                    norm(TB * b - TB, norm_d(b))
                    if not has_c:
                        for q in range(TB):
                            finish(b, q)
                        return

                def add_out(q):
                    m = TB * b + q
                    dve.wait_ge(c["out_done"], m + 1)
                    dve.tensor_tensor(TO, PB[4][:, 0:D], BIAS[:, 1, :], ALU.add).then_inc(c["tmp_o"], 1)
                    dve.wait_ge(c["tmp_o"], m + 1)
                    dve.scalar_tensor_tensor(X[:, m, :], TO, TG[:, 1:2], X[:, m, :], ALU.mult, ALU.add)\
                        .then_inc(c["x3_ready"], 1)

                for q in range(TB):
                    m = TB * b + q
                    dve.wait_ge(c["sc_done"], m + 1)
                    dve.tensor_reduce(NM[:, :], PB[1][:, :], AX.X, ALU.max, negate=True).then_inc(c["nmax"], 1)
                    dve.wait_ge(c["nmax"], m + 1)
                    if not (isinstance(m, int) and m < 2):
                        dve.wait_ge(c["p_done"], m - 1)
                    dve.tensor_scalar(NMS[:, q % 2:q % 2 + 1], NM[:, :], float(D) ** -0.5, None, ALU.mult)\
                        .then_inc(c["nmax_s"], 1)
                    if has_d and q >= 2:
                        finish(b, 2 * q - 4)
                    if q:
                        add_out(q - 1)
                    if has_d and q >= 2:
                        finish(b, 2 * q - 3)
                    dve.wait_ge(c["p_done"], m + 1)
                    dve.reciprocal(RC[:, :], SU[:, q % 2:q % 2 + 1]).then_inc(c["rinv"], 1)
                    dve.wait_ge(c["av_done"], m + 1)
                    dve.wait_ge(c["rinv"], m + 1)
                    if not (isinstance(m, int) and m == 0):
                        dve.wait_ge(c["cT_done"], m)
                    dve.scalar_tensor_tensor(CC, PB[3][:, 0:D], RC[:, :], BIAS[:, 0, :], ALU.mult, ALU.add)\
                        .then_inc(c["c_ready"], 1)
                add_out(TB - 1)

            dve.wait_ge(bcd_ready, 1)
            sweep_cd(dve, step_cd)


def kernel(x, ctx_1024, g_xattn, g_ffn, L0_xattn_Wq, L0_xattn_Wk, L0_xattn_Wv, L0_xattn_Wo,
           L0_ffn_w1s, L0_ffn_w2s, L0_ffn_w3s, L0_ffn_W1, L0_ffn_W2, L0_ffn_W3, L0_ffn_Wg,
           L1_xattn_Wk, L1_xattn_Wv, L1_xattn_bv, L1_xattn_Wq, L1_xattn_bq, L1_xattn_Wo, L1_xattn_bo,
           L1_ffn_W_exp, L1_ffn_b_exp, L1_ffn_up_weights, L1_ffn_up_bias, L1_ffn_down_weights,
           L1_ffn_W_con, L1_ffn_b_con, L1_ffn_down_bias):
    import concourse.bacc as bacc
    from concourse.bass_utils import run_bass_kernel_spmd

    def by_dim(w):
        return np.asarray(w).reshape(NH, DK, D).transpose(2, 1, 0).reshape(D, D)

    def chunks(w):
        w = np.asarray(w)
        return w.reshape(w.shape[0] // P, P, w.shape[1]).transpose(1, 0, 2).reshape(P, -1)

    experts = [[chunks(w[n]) for w in (L0_ffn_W1, L0_ffn_W2, L0_ffn_W3)] for n in range(NE)]
    experts.append([chunks(w) for w in (L0_ffn_w1s, L0_ffn_w2s, L0_ffn_w3s)])
    arrays = {
        "x": np.asarray(x).reshape(B * L, D),
        "ctxT": np.asarray(ctx_1024).reshape(B * L, D).T,
        "gates": np.concatenate([np.asarray(g_xattn), np.asarray(g_ffn)]),
        "wq0": by_dim(L0_xattn_Wq),
        "wkv0": np.concatenate([by_dim(L0_xattn_Wk), np.asarray(L0_xattn_Wv).T], axis=1),
        "wo0": np.asarray(L0_xattn_Wo).T.reshape(NH, DK, D).transpose(1, 0, 2).reshape(D, D),
        "wg": np.asarray(L0_ffn_Wg),
        "wexp": np.stack([np.concatenate(w, axis=1) for w in experts]),
        "wk1": np.asarray(L1_xattn_Wk).T, "wv1": np.asarray(L1_xattn_Wv).T,
        "wq1": np.asarray(L1_xattn_Wq).T, "wo1": np.asarray(L1_xattn_Wo).T,
        "bv1": np.asarray(L1_xattn_bv), "bq1": np.asarray(L1_xattn_bq), "bo1": np.asarray(L1_xattn_bo),
        "weT": np.asarray(L1_ffn_W_exp).T, "be": np.asarray(L1_ffn_b_exp),
        "upw": np.asarray(L1_ffn_up_weights).reshape(LOW + HIGH, F // 2, 4),
        "upb": np.asarray(L1_ffn_up_bias),
        "dnw": np.asarray(L1_ffn_down_weights).reshape(LOW + HIGH, F // 2, 4),
        "wc": np.asarray(L1_ffn_W_con), "bc": np.asarray(L1_ffn_b_con), "db": np.asarray(L1_ffn_down_bias),
    }
    arrays = {k: np.ascontiguousarray(v) for k, v in arrays.items()}
    nc = bacc.Bacc("TRN2", target_bir_lowering=False, num_devices=1)
    args = [nc.dram_tensor(k, v.shape, mybir.dt.from_np(v.dtype), kind="ExternalInput").ap()
            for k, v in arrays.items()]
    out = nc.dram_tensor("out", (B * L, D), F32, kind="ExternalOutput").ap()
    build(nc, *args, out)
    r = run_bass_kernel_spmd(nc, [arrays], core_ids=[0])
    return r.results[0]["out"].reshape(B, L, D)
```

```python
from contextlib import ExitStack

import numpy as np

import concourse.bass as bass
from concourse import mybir

F32 = mybir.dt.float32
I32 = mybir.dt.int32
U32 = mybir.dt.uint32
ALU = mybir.AluOpType
ACT = mybir.ActivationFunctionType
AX = mybir.AxisListType

P = 128
B, L, D = 4, 512, 256
T = B * L // P
TB = L // P
KD = D // P
NH = 16
DK = D // NH
F = 1024
KF = F // P
NE = 8
NT = T + NE - 1
SLOTS = 3
WS = 3 * KD * F
LOW, HIGH = 7, 3
EPS = 1e-5


def spread(v, axis, n):
    shape = list(v.shape)
    shape[axis] = n
    return v.broadcast_to(shape)


def build(nc, x, ctxT, gates, wq0, wkv0, wo0, wg, wexp, wk1, wv1, wq1, wo1, bv1, bq1, bo1,
          weT, be, upw, upb, dnw, wc, bc, db, out):
    with ExitStack() as ctx:
        def sb(name, shape, dt=F32):
            return ctx.enter_context(nc.sbuf_tensor(name, shape, dt))

        def sem(name):
            return ctx.enter_context(nc.semaphore(name))

        xs = nc.dram_tensor("sorted_rows", (NT * P, D), F32).ap()
        ys = nc.dram_tensor("expert_rows", (NT * P, D), F32).ap()

        X = sb("X", [P, T, D])
        XN2 = sb("XN2", [P, T, D])
        SLOT = sb("SLOT", [P, SLOTS, WS])
        WQ0 = sb("WQ0", [P, KD, D])
        WKV0 = sb("WKV0", [P, KD, 2 * D])
        WO0 = sb("WO0", [P, KD, D])
        WG = sb("WG", [P, KD, NE])
        WK1 = sb("WK1", [P, KD, D])
        WV1 = sb("WV1", [P, KD, D])
        WQ1 = sb("WQ1", [P, KD, D])
        WO1 = sb("WO1", [P, KD, D])
        BIAS = sb("BIAS", [P, 4, D])
        BQ = sb("BQ", [P, KD])
        IDENT = sb("IDENT", [P, P])
        ABOVE = sb("ABOVE", [P, P])
        ONES = sb("ONES", [P, P])
        MHALF = sb("MHALF", [P, 1])
        GATE = sb("GATE", [P, 4])
        TG = sb("TG", [P, 4])
        IOTA8 = sb("IOTA8", [P, NE])
        IOTAM = sb("IOTAM", [P, T])
        IOTAT = sb("IOTAT", [1, NT])
        IOTAI = sb("IOTAI", [P, NE + T + NT], I32)
        PRODQ = sb("PRODQ", [P, DK * DK * NH])
        PRODV = sb("PRODV", [P, DK * DK * NH])
        SHARED = sb("SHARED", [P, 2 * F])
        CTX = SHARED[:, 0:2 * KD * P].rearrange("p (r k t) -> p r k t", r=2, k=KD)
        PR = SHARED[:, 2 * KD * P:2 * KD * P + 2 * D].rearrange("p (r d) -> p r d", r=2)
        KV = SHARED[:, 2 * KD * P + 2 * D:2 * F].rearrange("p (r d) -> p r d", r=2)
        XN = sb("XN", [P, D])
        XH = sb("XH", [P, D])
        XT = sb("XT", [P, KD, P])
        SC = sb("SC", [P, D])
        AO = sb("AO", [P, D])
        AT = sb("AT", [P, KD, P])
        X2T = sb("X2T", [P, KD, P])
        ST = sb("ST", [P, 2, 6])
        MV = sb("MV", [P, 2, 4])
        SM = sb("SM", [P, 2, DK])
        RI = sb("RI", [P, DK])
        LG = sb("LG", [P, NE])
        TOP = sb("TOP", [P, NE])
        TOPI = sb("TOPI", [P, NE], U32)
        TOPF = sb("TOPF", [P, 1])
        G = sb("G", [P, F])
        HA = sb("HA", [P, KF, P])
        OH = sb("OH", [P, T, NE])
        RANK = sb("RANK", [P, T, NE])
        LESS = sb("LESS", [P, NE, NE])
        CMP = sb("CMP", [P, NE * T])
        NTE = sb("NTE", [P, NE])
        BASE = sb("BASE", [P, NE])
        POSF = sb("POSF", [P, T])
        POS = sb("POS", [P, T], U32)
        EI = sb("EI", [1, NT])
        GE = sb("GE", [1, NT, NE])
        SUM2 = sb("SUM2", [1, SLOTS, NT])
        TAB = sb("TAB", [1, 1 + SLOTS, NT], I32)
        BASEI = sb("BASEI", [1, NE], I32)

        flatA = PRODQ[:, :]
        flatV = PRODV[:, :]
        XS = sb("XS", [P, 2, D])
        XST = sb("XST", [P, 2, KD, P])
        HB = SHARED[:, :].rearrange("p (r f) -> p r f", r=2)
        HBT = HA
        YS = sb("YS", [P, D])
        COEF = flatA.rearrange("p (r k c) -> p r k c", r=2, c=4)
        WEFF = flatA[:, 0:KD * F].rearrange("p (k f) -> p k f", k=KD)
        MDN = flatA[:, KD * F:2 * KD * F].rearrange("p (c d) -> p c d", c=KF)
        Z = flatV[:, 0:KF * D].rearrange("p (c d) -> p c d", c=KF)
        EB = flatV[:, KF * D:KF * D + 2 * F].rearrange("p (r f) -> p r f", r=2)
        W1P = D + 1
        x2 = XN2[:, :, :].rearrange("p t d -> p (t d)")
        RT = x2[:, 0:KF * W1P].rearrange("p (c d) -> p c d", c=KF)
        EC = x2[:, KF * W1P:KF * W1P + F]
        WET = sb("WET", [P, KF, W1P])
        CTXB = WET[:, :, :].rearrange("p c d -> p (c d)")[:, 0:KD * L].rearrange("p (k t) -> p k t", k=KD)
        HIC = sb("HIC", [P, 2, HIGH, 4, 4])
        UPB = sb("UPB", [P, KF])
        TMPH = sb("TMPH", [P, 4, W1P])
        TMP = TMPH[:, :, :].rearrange("p a b -> p (a b)")
        BH = sb("BH", [P, KF])
        sf = SLOT[:, :, :].rearrange("p s w -> p (s w)")
        at = [0]

        def part(n):
            at[0] += n
            return sf[:, at[0] - n:at[0]]

        XN3T = part(KD * L).rearrange("p (k t) -> p k t", k=KD)
        XN4T = part(KD * L).rearrange("p (k t) -> p k t", k=KD)
        QT = part(KD * L).rearrange("p (k t) -> p k t", k=KD)
        K1T = part(KD * L).rearrange("p (k t) -> p k t", k=KD)
        V1 = part(TB * D).rearrange("p (t d) -> p t d", t=TB)
        PS = part(2 * L).rearrange("p (r t) -> p r t", r=2)
        PT = part(L).rearrange("p (k t) -> p k t", k=TB)
        XNC = part(TB * D).rearrange("p (r d) -> p r d", r=TB)
        CC = part(D)
        CT = part(D).rearrange("p (k t) -> p k t", k=KD)
        H4 = part(KF * L).rearrange("p (c t) -> p c t", c=KF)
        TO = part(D)
        TY = part(D)
        YG = part(TB * D).rearrange("p (t d) -> p t d", t=TB)
        assert at[0] <= SLOTS * WS
        NM = sb("NM", [P, 1])
        NMS = sb("NMS", [P, 2])
        SU = sb("SU", [P, 2])
        RC = sb("RC", [P, 1])
        STC = sb("STC", [P, TB, 6])
        MVC = sb("MVC", [P, TB, 2])
        VE = sb("VE", [P, TB])
        RS = sb("RS", [P, TB])
        BCD = sb("BCD", [P, D])

        PB = [ctx.enter_context(nc.psum_tensor(f"bank{i}", [P, 512], F32)) for i in range(8)]

        w_in = sem("w_in")
        wg_in = sem("wg_in")
        c_in = sem("c_in")
        tile_in = [sem("tile_in0"), sem("tile_in1")]
        slot_in = [sem(f"slot_in{i}") for i in range(SLOTS)]
        consts = sem("consts")
        iotas = sem("iotas")
        iotaf = sem("iotaf")
        zero_ms = sem("zero_ms")
        zeroed = sem("zeroed")
        tanh_s = sem("tanh_s")

        names = """qk_prod scores rowmax shifted exp_done sums a_ready av_read ln1_stats ln1_agg ln1_eps
        ln1_rstd xn_ready ln2_stats ln2_agg ln2_eps ln2_rstd xn2_ready x1_ready xT_done xT_sb q_done
        kv_done kv_sb x2T_done x2T_sb aT_done aT_sb o_done gate_done lg_sb top_ok topi_ok topf_ok
        oh_ok xn2_kept h1_done h2_done gelu_done mult_done y_done y_added av_prod av_half recip""".split()
        s = {n: sem(n) for n in names}
        route = sem("route")
        held = sem("held")
        rank_ps = sem("rank_ps")
        tables = sem("tables")
        pos_ready = sem("pos_ready")
        scattered = sem("scattered")
        slot_uses = sem("slot_uses")

        bnames = """sT_done sT_sb b_h1 b_h2 b_gelu b_mult hT_done hT_a hT_d by_done by_sb""".split()
        e = {n: sem(n) for n in bnames}
        xs_in = [sem("xs_in0"), sem("xs_in1")]
        ys_out = sem("ys_out")
        pool = sem("pool")
        coef_in = [sem("coef_in0"), sem("coef_in1")]
        e_up = sem("e_up")
        rt_ps = sem("rt_ps")
        rt_sb = sem("rt_sb")
        rt_high = sem("rt_high")
        z_high = sem("z_high")
        wm_ps = sem("wm_ps")
        wm_sb = sem("wm_sb")
        gathered = sem("gathered")
        x2_added = sem("x2_added")
        ctx_in = sem("ctx_in")

        cnames = """c_stats c_agg c_eps c_rstd c_xn c_xT c_xT_sb sc_done nmax nmax_s p_done pT_done pT_sb
        av_done rinv c_ready cT_done cT_sb out_done tmp_o x3_ready fin_ready""".split()
        c = {n: sem(n) for n in cnames}
        ring_full = [sem("ring_full0"), sem("ring_full1")]
        ring_free = [sem("ring_free0"), sem("ring_free1")]
        stored = sem("stored")
        bcd_ready = sem("bcd_ready")

        block = ctx.enter_context(nc.Block())

        LAG = 4
        PAUSE = 7

        def lag(j, par, n):
            m = par - n
            return j + m // 2, m % 2

        def sweep(eng, step, count, lags, start, ahead=0, pause=None, at_pause=None):
            def tiles(j, par, t):
                def of(n):
                    if t is not None and not 0 <= t - n < count:
                        return None
                    return lag(j, par, n)
                return of
            for t in range(2 * start):
                step(tiles(t // 2, t % 2, t))
            end = (count - ahead) // 2
            for lo, hi in ((start, end),) if pause is None else ((start, pause), (pause, end)):
                with eng.Fori(lo, hi) as j:
                    step(tiles(j, 0, None))
                    step(tiles(j, 1, None))
                if hi == pause:
                    at_pause()
            for t in range(2 * end, count + lags):
                step(tiles(t // 2, t % 2, t))

        def sweep_a(eng, step):
            sweep(eng, step, T, LAG, LAG // 2 + 1)

        def sweep_b(eng, step, at_pause=None):
            sweep(eng, step, NT, 2, 2, 2, PAUSE if at_pause else None, at_pause)

        def num(jp):
            return 2 * jp[0] + jp[1]

        def first(jp, n):
            return isinstance(jp[0], int) and num(jp) < n

        def ring_before(b, n):
            if isinstance(b, int) and b == 0:
                return n // 2
            return 9 * b - 6 + (n - 6 if isinstance(b, int) and b == B else n) // 2

        def norm_c(b):
            return 0 if isinstance(b, int) and b == 0 else 2 * b - 1

        def norm_d(b):
            return 2 * b - 1 if isinstance(b, int) and b == B else 2 * b

        def sweep_cd(eng, step):
            step(0, True, False, True)
            with eng.Fori(1, B - 1) as b:
                step(b, True, True, True)
            step(B - 1, True, True, False)
            step(B, False, True, False)

        @block.sync
        def _(sp):
            def load_tile(j, par):
                t = 2 * j + par
                if not (isinstance(j, int) and j == 0):
                    sp.wait_ge(tile_in[par], 32 * j)
                    sp.wait_ge(s["kv_done"], t - 1)
                sp.dma_start(X[:, t, :], x[bass.ds(t * P, P), :]).then_inc(tile_in[par], 16)
                sp.dma_start(CTX[:, par, :, :],
                             ctxT[:, bass.ds(t * P, P)].rearrange("(k p) t -> p k t", p=P))\
                    .then_inc(tile_in[par], 16)

            load_tile(0, 0)
            for w, src in ((WQ0, wq0), (WKV0, wkv0)):
                sp.dma_start(w[:, :, :], src.rearrange("(k p) n -> p k n", p=P)).then_inc(w_in, 16)
            load_tile(0, 1)
            for w, src in ((WO0, wo0), (WG, wg)):
                sp.dma_start(w[:, :, :], src.rearrange("(k p) n -> p k n", p=P)).then_inc(wg_in, 16)
            sp.dma_start(GATE[:, :], gates.partition_broadcast(P)).then_inc(wg_in, 16)
            sp.dma_start(SLOT[:, 2, :], wexp[NE]).then_inc(slot_in[2], 16)
            with sp.Fori(1, T // 2) as j:
                load_tile(j, 0)
                load_tile(j, 1)
            for w, src in ((WK1, wk1), (WV1, wv1), (WQ1, wq1), (WO1, wo1)):
                sp.dma_start(w[:, :, :], src.rearrange("(k p) n -> p k n", p=P)).then_inc(c_in, 16)
            for n, src in enumerate((bv1, bo1, bc, db)):
                sp.dma_start(BIAS[:, n, :], src.partition_broadcast(P)).then_inc(c_in, 16)
            with nc.allow_non_contiguous_dma("biases and coefficients by partition"):
                sp.dma_start(BQ[:, :], bq1.rearrange("(k p) -> p k", p=P)).then_inc(c_in, 16)
                sp.dma_start(UPB[:, :], upb.rearrange("(k p) -> p k", p=P)).then_inc(c_in, 16)
                for n, src in enumerate((upw, dnw)):
                    sp.dma_start(HIC[:, n, :, :, :], src[LOW:LOW + HIGH].rearrange(
                        "s (q p) c -> p s q c", p=P)).then_inc(c_in, 16)
                sp.dma_start(WET[:, :, 0:D], weT.rearrange("(c p) d -> p c d", p=P)).then_inc(c_in, 16)
                sp.dma_start(WET[:, :, D:W1P], be.rearrange("(c p o) -> p c o", p=P, o=1))\
                    .then_inc(c_in, 16)
            sp.dma_start(SLOT[:, 0, :], wexp[0]).then_inc(slot_in[0], 16)
            sp.dma_start(SLOT[:, 1, :], wexp[1]).then_inc(slot_in[1], 16)
            sp.wait_ge(s["y_done"], T)
            sp.dma_start(SLOT[:, 2, :], wexp[2]).then_inc(slot_in[2], 16)
            sp.wait_ge(tables, 1)
            for n in range(SLOTS, NE):
                base = sp.value_load(BASEI[0:1, n - 2:n - 1], min_val=1, max_val=NT + 1)
                sp.wait_ge(slot_uses, base)
                sp.dma_start(SLOT[:, n % SLOTS, :], wexp[n]).then_inc(slot_in[n % SLOTS], 16)
            sp.wait_ge(rt_ps, KF)

            def load_ctx(b):
                sp.dma_start(CTXB, ctxT[:, bass.ds(b * L, L)].rearrange("(k p) t -> p k t", p=P))\
                    .then_inc(ctx_in, 16)

            load_ctx(0)

            def outputs(b):
                for q in range(TB):
                    tile = b * TB + q
                    sp.wait_ge(c["fin_ready"], tile + 1)
                    sp.dma_start(out[bass.ds(tile * P, P), :], X[:, tile, :]).then_inc(stored, 16)

            def context_used(b):
                for n in (2, 3):
                    sp.wait_ge(ring_free[n % 2], ring_before(b, n) + 1)

            context_used(0)
            load_ctx(1)
            with sp.Fori(1, B - 1) as b:
                context_used(b)
                load_ctx(b + 1)
                outputs(b - 1)
            outputs(B - 2)
            outputs(B - 1)
            sp.wait_ge(stored, 16 * T)

        @block.gpsimd
        def _(gp):
            gp.memset(IDENT[:, :], 0.0).then_inc(consts, 1)
            gp.memset(ABOVE[:, :], 0.0).then_inc(consts, 1)
            gp.memset(ONES[:, :], 1.0).then_inc(consts, 1)
            gp.memset(MHALF[:, :], -0.5).then_inc(consts, 1)
            gp.wait_ge(consts, 4)
            gp.affine_select(out=IDENT[:, :], in_=IDENT[:, :], compare_op=ALU.not_equal, fill=1.0,
                             base=0, pattern=[[-1, P]], channel_multiplier=1).then_inc(consts, 1)
            gp.affine_select(out=ABOVE[:, :], in_=ABOVE[:, :], compare_op=ALU.is_ge, fill=1.0,
                             base=0, pattern=[[-1, P]], channel_multiplier=1).then_inc(consts, 1)
            gp.iota(IOTAI[:, 0:NE], pattern=[[1, NE]], base=0, channel_multiplier=0).then_inc(iotas, 1)
            gp.iota(IOTAI[:, NE:NE + T], pattern=[[P, T]], base=0, channel_multiplier=0).then_inc(iotas, 1)
            gp.iota(IOTAI[:, NE + T:], pattern=[[1, NT]], base=0, channel_multiplier=0).then_inc(iotas, 1)
            gp.memset(PRODV[:, :], 0.0).then_inc(zero_ms, 1)
            gp.wait_ge(zero_ms, 1)
            for r0 in range(0, NT, T):
                n = min(T, NT - r0)
                gp.dma_start(xs[r0 * P:(r0 + n) * P, :].rearrange("(t p) d -> p t d", p=P),
                             PRODV[:, 0:n * D].rearrange("p (t d) -> p t d", t=n)).then_inc(zeroed, 16)

            def step(of):
                if (t3 := of(3)) is not None:
                    gp.wait_ge(s["ln2_eps"], num(t3) + 1)
                    gp.tensor_tensor(MV[:, 1, 3:4], MV[:, 1, 2:3], MHALF[:, :], ALU.pow)\
                        .then_inc(s["ln2_rstd"], 1)
                if (t0 := of(0)) is not None:
                    gp.wait_ge(s["ln1_eps"], num(t0) + 1)
                    gp.tensor_tensor(MV[:, 0, 3:4], MV[:, 0, 2:3], MHALF[:, :], ALU.pow)\
                        .then_inc(s["ln1_rstd"], 1)
                if (t1 := of(1)) is not None:
                    n, par = num(t1), t1[1]
                    gp.wait_ge(s["exp_done"], n + 1)
                    gp.wait_ge(s["kv_sb"], n + 1)
                    if first(t1, 1):
                        gp.wait_ge(zeroed, 32)
                    for hf in range(2):
                        if not first(t1, 1):
                            gp.wait_ge(s["av_read"], 2 * (n - 1) + hf + 1)
                        H2 = NH // 2
                        o = PRODV[:, :].rearrange("p (f i h j) -> p f i h j", f=2, i=DK, h=H2)[:, hf]
                        pr = spread(PR[:, par, :].rearrange("p (i o j) -> p i o j", i=DK, o=1), 2, H2)
                        v = KV[:, par, D + hf * H2 * DK:D + (hf + 1) * H2 * DK]
                        v = spread(v.rearrange("p (o h j) -> p o h j", o=1, j=DK), 1, DK)
                        gp.tensor_tensor(o, pr, v, ALU.mult).then_inc(s["av_prod"], 1)
                        gp.wait_ge(s["av_prod"], 2 * n + hf + 1)
                        gp.tensor_tensor(o[:, :, :, 0:DK // 2], o[:, :, :, 0:DK // 2], o[:, :, :, DK // 2:DK],
                                         ALU.add).then_inc(s["av_half"], 1)

            sweep_a(gp, step)

            gp.wait_ge(zeroed, 32)
            gp.wait_ge(pos_ready, 1)
            gp.wait_ge(s["xn2_kept"], T)
            for t in range(T):
                gp.indirect_dma_start(out=xs, out_offset=bass.IndirectOffsetOnAxis(ap=POS[:, t:t + 1], axis=0),
                                      in_=XN2[:, t, :], in_offset=None).then_inc(scattered, 16)

            done = [0]

            def run(ins):
                done[0] += 1
                ins.then_inc(pool, 1)

            def settle():
                gp.wait_ge(pool, done[0])

            stages = [(0, upw, k) for k in range(LOW)] + [(1, dnw, k) for k in reversed(range(LOW))]

            def load_coef(n):
                _, src, k = stages[n]
                gp.dma_start(COEF[:, n % 2, :, :].rearrange("p k c -> p (k c)"),
                             src[k].rearrange("k c -> (k c)").partition_broadcast(P))\
                    .then_inc(coef_in[n % 2], 16)

            gp.wait_ge(s["a_ready"], T)
            gp.wait_ge(scattered, 16 * T)
            gp.wait_ge(xs_in[1], 16)
            load_coef(0)
            load_coef(1)
            gp.dma_start(Z, wc.rearrange("(c p) d -> p c d", p=P)).then_inc(zeroed, 16)
            bufs = [EB[:, 0, :], EB[:, 1, :], EC]

            def low(n, src, dst):
                down, _, k = stages[n]
                w = 2 ** k
                a, b = (src.rearrange("p (n two w) -> p n two w", two=2, w=w)[:, :, i, :] for i in (0, 1))
                oa, ob = (dst.rearrange("p (n two w) -> p n two w", two=2, w=w)[:, :, i, :] for i in (0, 1))
                cf = [COEF[:, n % 2, :, i].rearrange("p (n w) -> p n w", w=w) for i in range(4)]
                if down:
                    cf[1], cf[2] = cf[2], cf[1]
                t = [TMP[:, i * F // 2:(i + 1) * F // 2].rearrange("p (n w) -> p n w", w=w) for i in range(2)]
                gp.wait_ge(coef_in[n % 2], 16 * (n // 2 + 1))
                settle()
                run(gp.tensor_tensor(oa, a, cf[0], ALU.mult))
                run(gp.tensor_tensor(t[0], b, cf[1], ALU.mult))
                run(gp.tensor_tensor(ob, a, cf[2], ALU.mult))
                run(gp.tensor_tensor(t[1], b, cf[3], ALU.mult))
                settle()
                if n + 2 < len(stages):
                    load_coef(n + 2)
                run(gp.tensor_tensor(oa, oa, t[0], ALU.add))
                run(gp.tensor_tensor(ob, ob, t[1], ALU.add))

            def eye(dst):
                settle()
                run(gp.memset(dst, 0.0))
                settle()
                v = dst.rearrange("p (c m) -> p c m", c=KF)
                run(gp.affine_select(out=v, in_=v, compare_op=ALU.not_equal, fill=1.0, base=0,
                                     pattern=[[0, KF], [-1, P]], channel_multiplier=1))

            def high(n, m, width, stage):
                bit = stage
                for q in range(4):
                    c0 = ((q >> bit) << (bit + 1)) | (q & ((1 << bit) - 1))
                    c1 = c0 | (1 << bit)
                    cf = [HIC[:, n, stage, q, i:i + 1] for i in range(4)]
                    if n:
                        cf[1], cf[2] = cf[2], cf[1]
                    settle()
                    for i, (src, k) in enumerate(((c0, 0), (c1, 1), (c0, 2), (c1, 3))):
                        run(gp.tensor_scalar(TMPH[:, i, 0:width], m[:, src, :], cf[k], None, ALU.mult))
                    settle()
                    run(gp.tensor_tensor(m[:, c0, :], TMPH[:, 0, 0:width], TMPH[:, 1, 0:width], ALU.add))
                    run(gp.tensor_tensor(m[:, c1, :], TMPH[:, 2, 0:width], TMPH[:, 3, 0:width], ALU.add))

            eye(bufs[0])
            for n in range(LOW):
                low(n, bufs[n % 2], bufs[1 - n % 2])
            settle()
            gp.nop().then_inc(e_up, 1)
            eye(bufs[0])
            order = [0, 2]
            for n in range(LOW):
                low(LOW + n, bufs[order[n % 2]], bufs[order[1 - n % 2]])
            gp.wait_ge(c_in, 16 * 14)
            gp.wait_ge(zeroed, 48)
            for st in reversed(range(HIGH)):
                high(1, Z, D, st)
            settle()
            gp.nop().then_inc(z_high, 1)
            gp.wait_ge(rt_sb, KF)
            for st in range(HIGH):
                high(0, RT, W1P, st)
            settle()
            run(gp.tensor_tensor(BH[:, :], RT[:, :, D], UPB[:, :], ALU.add))
            settle()
            gp.nop().then_inc(rt_high, 1)

            gp.wait_ge(ys_out, 16 * NT)

            def gather(b):
                if b:
                    gp.wait_ge(x2_added, TB * b)
                for q in range(TB):
                    t = TB * b + q
                    gp.indirect_dma_start(out=YG[:, q, :], out_offset=None, in_=ys,
                                          in_offset=bass.IndirectOffsetOnAxis(ap=POS[:, t:t + 1], axis=0))\
                        .then_inc(gathered, 16)

            def roots(g):
                gp.wait_ge(c["c_eps"], TB * (g + 1))
                gp.tensor_tensor(RS[:, :], VE[:, :], spread(MHALF[:, :], 1, TB), ALU.pow)\
                    .then_inc(c["c_rstd"], 1)

            gather(0)
            for g in range(2 * B):
                roots(g)
                if g in (0, 1, 3):
                    gather(g // 2 + 1 + g % 2 if g < 3 else 3)

        @block.tensor
        def _(pe):
            def product(dst, lhs, rhs, chunks, signal=None):
                for k in range(chunks):
                    last = pe.matmul(dst, lhs(k), rhs(k), start=(k == 0), stop=(k == chunks - 1))
                if signal is not None:
                    last.then_inc(signal, 1)

            def flip(bank, src, signal, n=KD):
                for k in range(n):
                    last = pe.transpose(bank[:, k * P:(k + 1) * P], src[:, k * P:(k + 1) * P], IDENT[:, :])
                last.then_inc(signal, 1)

            pe.nop().then_inc(slot_uses, 1)
            pe.wait_ge(consts, 6)
            W1 = SLOT[:, 2, 0:KD * F].rearrange("p (k f) -> p k f", k=KD)
            W2 = SLOT[:, 2, KD * F:2 * KD * F].rearrange("p (k f) -> p k f", k=KD)
            W3 = SLOT[:, 2, 2 * KD * F:WS].rearrange("p (c d) -> p c d", c=KF)

            def up_half(t3, hf):
                n = 2 * num(t3) + hf
                for bank, w, done, free in ((PB[6], W1, "h1_done", "gelu_done"),
                                            (PB[7], W2, "h2_done", "mult_done")):
                    if not (first(t3, 1) and hf == 0):
                        pe.wait_ge(s[free], n)
                    for q in range(4):
                        m = 4 * hf + q
                        product(bank[:, q * P:(q + 1) * P], lambda k: w[:, k, m * P:(m + 1) * P],
                                lambda k: X2T[:, k, :], KD, s[done] if q == 3 else None)

            def step(of):
                t0, t3, t4 = of(0), of(3), of(4)
                if t3 is not None:
                    n3 = num(t3)
                    pe.wait_ge(s["a_ready"], n3 + 1)
                    if first(t3, 1):
                        pe.wait_ge(wg_in, 48)
                        pe.wait_ge(slot_in[2], 16)
                    else:
                        pe.wait_ge(s["x2T_sb"], n3)
                    flip(PB[3], AO[:, :], s["aT_done"])
                    pe.wait_ge(s["aT_sb"], n3 + 1)
                    if not first(t3, 1):
                        pe.wait_ge(s["lg_sb"], n3)
                    product(PB[5][:, 0:D], lambda k: AT[:, k, :], lambda k: WO0[:, k, :], KD, s["o_done"])
                if t4 is not None:
                    up_half(t4, 1)
                if t0 is not None:
                    n = num(t0)
                    pe.wait_ge(tile_in[t0[1]], 32 * t0[0] + 32)
                    if first(t0, 1):
                        pe.wait_ge(w_in, 32)
                    else:
                        pe.wait_ge(s["kv_sb"], n)
                    product(PB[4][:, :], lambda k: CTX[:, t0[1], k, :], lambda k: WKV0[:, k, :], KD,
                            s["kv_done"])
                if t4 is not None:
                    n4 = num(t4)
                    pe.wait_ge(s["mult_done"], 2 * n4 + 2)
                    if not first(t4, 1):
                        pe.wait_ge(s["y_added"], n4)
                    product(PB[2][:, 0:D], lambda k: HA[:, k, :], lambda k: W3[:, k, :], KF, s["y_done"])
                if t3 is not None:
                    pe.wait_ge(s["xn2_ready"], n3 + 1)
                    flip(PB[3], XH[:, :], s["x2T_done"])
                if t0 is not None:
                    pe.wait_ge(s["xn_ready"], n + 1)
                    if not first(t0, 1):
                        pe.wait_ge(s["xT_sb"], n)
                    flip(PB[0], XN[:, :], s["xT_done"])
                if t3 is not None:
                    pe.wait_ge(s["x2T_sb"], n3 + 1)
                    product(PB[5][:, 0:NE], lambda k: X2T[:, k, :], lambda k: WG[:, k, :], KD,
                            s["gate_done"])
                if t0 is not None:
                    pe.wait_ge(s["xT_sb"], n + 1)
                    if not first(t0, 1):
                        pe.wait_ge(s["qk_prod"], n)
                    product(PB[1][:, 0:D], lambda k: XT[:, k, :], lambda k: WQ0[:, k, :], KD, s["q_done"])
                if t3 is not None:
                    up_half(t3, 0)
                    if isinstance(n3, int) and n3 == T - 1:
                        ranks()

            def ranks():
                pe.wait_ge(s["oh_ok"], T)
                pe.matmul(PB[1][:, 0:T * NE], ABOVE[:, :], OH[:, :, :].rearrange("p t e -> p (t e)"),
                          start=True, stop=False)
                for t in range(T - 1):
                    last = pe.matmul(PB[1][:, (t + 1) * NE:T * NE].rearrange("p (t e) -> p t e", e=NE), ONES[:, :],
                                     spread(OH[:, t:t + 1, :], 1, T - 1 - t), start=False, stop=(t == T - 2))
                last.then_inc(rank_ps, 1)
                for t in range(T):
                    last = pe.matmul(PB[4][:, 0:NE], ONES[:, :], OH[:, t, :], start=(t == 0), stop=(t == T - 1))
                last.then_inc(rank_ps, 1)

            sweep_a(pe, step)

            pe.wait_ge(tables, 1)
            pe.wait_ge(s["y_added"], T)

            def step_b(of):
                t0, t1, t2 = of(0), of(1), of(2)
                if t2 is not None:
                    n2 = num(t2)
                    for r, free in enumerate(("hT_a", "hT_d")):
                        pe.wait_ge(e["b_mult"], 2 * n2 + 1 + r)
                        if not first(t2, 1):
                            pe.wait_ge(e[free], n2)
                        flip(PB[5 + r], HB[:, t2[1], r * 512:(r + 1) * 512], e["hT_done"], 4)
                if t0 is not None:
                    n = num(t0)
                    pe.wait_ge(xs_in[t0[1]], 16 * t0[0] + 16)
                    if not first(t0, 1):
                        pe.wait_ge(e["sT_sb"], n)
                    flip(PB[0], XS[:, t0[1], :], e["sT_done"])
                if t1 is not None:
                    n = num(t1)
                    slot, *counts = [pe.value_load(TAB[0:1, r, bass.ds(n, 1)], min_val=lo, max_val=hi)
                                     for r, (lo, hi) in enumerate([(0, SLOTS - 1)] + SLOTS * [(16, 64)])]
                    for k in range(SLOTS):
                        pe.wait_ge(slot_in[k], counts[k])
                    pe.wait_ge(e["sT_sb"], n + 1)
                    for hf in range(2):
                        for bank, at, done, free in ((PB[1 + hf], 0, "b_h1", "b_gelu"),
                                                     (PB[3 + hf], KD * F, "b_h2", "b_mult")):
                            if not first(t1, 1):
                                pe.wait_ge(e[free], 2 * n + hf - 1)
                            product(bank[:, :], lambda k: XST[:, t1[1], k, :],
                                    lambda k: SLOT[:, bass.ds(slot, 1), at + k * F + hf * 512:
                                                   at + k * F + hf * 512 + 512].rearrange("p o f -> p (o f)"),
                                    KD, e[done])
                if t2 is not None:
                    slot = pe.value_load(TAB[0:1, 0, bass.ds(n2, 1)], min_val=0, max_val=SLOTS - 1)
                    pe.wait_ge(e["hT_a"], n2 + 1)
                    pe.wait_ge(e["hT_d"], n2 + 1)
                    if not first(t2, 1):
                        pe.wait_ge(e["by_sb"], n2)
                    product(PB[7][:, 0:D], lambda k: HBT[:, k, :],
                            lambda k: SLOT[:, bass.ds(slot, 1), 2 * KD * F + k * D:
                                           2 * KD * F + (k + 1) * D].rearrange("p o f -> p (o f)"),
                            KF, slot_uses)

            def fold_up():
                pe.wait_ge(e_up, 1)
                pe.wait_ge(c_in, 16 * 14)
                pe.wait_ge(e["sT_sb"], 2 * PAUSE)
                pe.wait_ge(e["by_sb"], 2 * PAUSE - 2)
                for m in range(KF):
                    if m >= 2:
                        pe.wait_ge(rt_sb, m - 1)
                    product(PB[0 if m % 2 == 0 else 7][:, 0:W1P], lambda k: EB[:, 1, m * P:(m + 1) * P],
                            lambda k: WET[:, m, :], 1, rt_ps)
                pe.wait_ge(rt_sb, KF)

            sweep_b(pe, step_b, fold_up)

            def fill(b, n, make):
                before = ring_before(b, n)
                if not (isinstance(before, int) and before == 0):
                    pe.wait_ge(ring_free[n % 2], before)
                make(PB[6 + n % 2], ring_full[n % 2])

            def flips(g, r):
                for q in (2 * r, 2 * r + 1):
                    f = TB * g + q
                    pe.wait_ge(c["c_xn"], f + 1)
                    if q % 2 == 0 and not (isinstance(f, int) and f == 0):
                        pe.wait_ge(c["c_xT_sb"], 2 * g + q // 2)
                    for k in range(KD):
                        last = pe.transpose(PB[0][:, (KD * (q % 2) + k) * P:(KD * (q % 2) + k + 1) * P],
                                            XNC[:, q, k * P:(k + 1) * P], IDENT[:, :])
                    last.then_inc(c["c_xT"], 1)

            def flipped(g):
                pe.wait_ge(c["c_xT_sb"], 2 * g + 2)

            def wide(w, m, rhs):
                return lambda bank, full: product(bank[:, :], lambda k: w[:, k, m * P:(m + 1) * P],
                                                  lambda k: rhs[:, k, :], KD, full)

            def values(r):
                def make(bank, full):
                    for h in range(2):
                        q = 2 * r + h
                        product(bank[:, h * D:(h + 1) * D], lambda k: CTXB[:, k, q * P:(q + 1) * P],
                                lambda k: WV1[:, k, :], KD, full if h else None)
                return make

            def down(q):
                return lambda bank, full: product(bank[:, 0:D], lambda k: H4[:, k, q * P:(q + 1) * P],
                                                  lambda k: MDN[:, k, :], KF, full)

            def piece(b, n):
                if n < 4:
                    for m in (2 * n, 2 * n + 1):
                        fill(b, 6 + m, wide(WEFF, m, XN4T))
                else:
                    if n == 4:
                        pe.wait_ge(ring_free[0], ring_before(b, 12) + 1)
                        pe.wait_ge(ring_free[1], ring_before(b, 13) + 1)
                    fill(b, 10 + n, down(n - 4))

            def keys_values(b):
                pe.wait_ge(ctx_in, 16 * b + 16)
                for m in range(KD):
                    fill(b, m, wide(WK1, m, CTXB))
                for r in range(2):
                    fill(b, 2 + r, values(r))

            def step_cd(b, has_c, has_d, has_next):
                if has_c:
                    if has_d:
                        keys_values(b)
                        flips(norm_d(b), 0)
                    flipped(norm_c(b))
                    for m in range(KD):
                        fill(b, 4 + m, wide(WQ1, m, XN3T))
                    if has_d:
                        flips(norm_d(b), 1)
                else:
                    for r in range(2):
                        flips(norm_d(b), r)
                    flipped(norm_d(b))
                    for n in range(8):
                        piece(b, n)
                    return
                for n in (4, 5):
                    pe.wait_ge(ring_free[n % 2], ring_before(b, n) + 1)

                def out_product(q):
                    n = TB * b + q
                    pe.wait_ge(c["cT_sb"], n + 1)
                    if not (isinstance(n, int) and n == 0):
                        pe.wait_ge(c["x3_ready"], n)
                    product(PB[4][:, 0:D], lambda k: CT[:, k, :], lambda k: WO1[:, k, :], KD, c["out_done"])

                def flip_c(q):
                    n = TB * b + q
                    pe.wait_ge(c["c_ready"], n + 1)
                    if not (isinstance(n, int) and n == 0):
                        pe.wait_ge(c["cT_sb"], n)
                    flip(PB[5], CC, c["cT_done"])

                def scores(q):
                    n = TB * b + q
                    if not (isinstance(n, int) and n == 0):
                        pe.wait_ge(c["p_done"], n)
                    product(PB[1][:, :], lambda k: QT[:, k, q * P:(q + 1) * P], lambda k: K1T[:, k, :], KD,
                            c["sc_done"])

                scores(0)
                for q in range(TB):
                    n = TB * b + q
                    pe.wait_ge(c["p_done"], n + 1)
                    if not (isinstance(n, int) and n == 0):
                        pe.wait_ge(c["pT_sb"], n)
                    flip(PB[2], PS[:, q % 2, :], c["pT_done"], TB)
                    if q + 1 < TB:
                        scores(q + 1)
                    if has_next and q == 2:
                        flips(norm_c(b + 1), 0)
                    pe.wait_ge(c["pT_sb"], n + 1)
                    if not (isinstance(n, int) and n == 0):
                        pe.wait_ge(c["c_ready"], n)
                    product(PB[3][:, 0:D], lambda k: PT[:, k, :], lambda k: V1[:, k, :], TB, c["av_done"])
                    if has_d:
                        if q == 0:
                            flipped(norm_d(b))
                        piece(b, 2 * q)
                    if has_next and q == 2:
                        flips(norm_c(b + 1), 1)
                    flip_c(q)
                    if has_d:
                        piece(b, 2 * q + 1)
                    out_product(q)

            def fold_down():
                pe.wait_ge(rt_high, 1)
                pe.wait_ge(e["hT_d"], NT)
                pe.wait_ge(e["by_sb"], NT)
                for n in range(KF):
                    k, m0 = n // 4, 2 * (n % 4)
                    if n >= 2:
                        pe.wait_ge(wm_sb, n - 1)
                    for h in range(2):
                        last = pe.transpose(PB[6 + n % 2][:, h * P:(h + 1) * P],
                                            RT[:, m0 + h, k * P:(k + 1) * P], IDENT[:, :])
                    last.then_inc(wm_ps, 1)
                for m in range(KF):
                    pe.wait_ge(wm_sb, KF + m - 1)
                    product(PB[6 + m % 2][:, 0:D], lambda k: EC[:, m * P:(m + 1) * P],
                            lambda k: Z[:, m, :], 1, wm_ps)
                pe.wait_ge(wm_sb, 2 * KF)

            pe.wait_ge(c_in, 16 * 14)
            fold_down()
            keys_values(0)
            for r in range(2):
                flips(0, r)
            sweep_cd(pe, step_cd)

        @block.scalar
        def _(act):
            act.wait_ge(wg_in, 48)
            act.activation(TG[:, :], GATE[:, :], ACT.Tanh).then_inc(tanh_s, 1)

            def step(of):
                t0, t1, t3, t4 = of(0), of(1), of(3), of(4)

                def gelu(hf):
                    n = 2 * num(t4) + hf
                    act.wait_ge(s["h1_done"], n + 1)
                    if not first(t4, 1):
                        act.wait_ge(s["mult_done"], n - 1)
                    act.activation(G[:, hf * 512:(hf + 1) * 512], PB[6][:, :], ACT.Gelu)\
                        .then_inc(s["gelu_done"], 1)

                if t4 is not None:
                    gelu(0)
                if t3 is not None:
                    act.wait_ge(s["aT_done"], num(t3) + 1)
                    act.activation(AT[:, :, :].rearrange("p k t -> p (k t)"), PB[3][:, 0:D], ACT.Copy)\
                        .then_inc(s["aT_sb"], 1)
                if t4 is not None:
                    gelu(1)
                if t0 is not None:
                    n = num(t0)
                    act.wait_ge(s["kv_done"], n + 1)
                    if not first(t0, 2):
                        act.wait_ge(s["qk_prod"], n - 1)
                        act.wait_ge(s["av_prod"], 2 * n - 2)
                    act.activation(KV[:, t0[1], :], PB[4][:, :], ACT.Copy).then_inc(s["kv_sb"], 1)
                if t1 is not None:
                    n1 = num(t1)
                    act.wait_ge(s["shifted"], n1 + 1)
                    if not first(t1, 2):
                        act.wait_ge(s["av_prod"], 2 * n1 - 2)
                        act.wait_ge(s["sums"], n1 - 1)
                    act.activation(PR[:, t1[1], :], SC[:, :], ACT.Exp, scale=float(DK) ** -0.5)\
                        .then_inc(s["exp_done"], 1)
                if t3 is not None:
                    act.wait_ge(s["x2T_done"], num(t3) + 1)
                    act.activation(X2T[:, :, :].rearrange("p k t -> p (k t)"), PB[3][:, 0:D], ACT.Copy)\
                        .then_inc(s["x2T_sb"], 1)
                if t0 is not None:
                    act.wait_ge(s["xT_done"], num(t0) + 1)
                    act.activation(XT[:, :, :].rearrange("p k t -> p (k t)"), PB[0][:, 0:D], ACT.Copy)\
                        .then_inc(s["xT_sb"], 1)
                if t3 is not None:
                    act.activation(XN2[:, num(t3), :], XH[:, :], ACT.Copy).then_inc(s["xn2_kept"], 1)

            sweep_a(act, step)

            def load_rows(jp):
                act.dma_start(XS[:, jp[1], :], xs[bass.ds(num(jp) * P, P), :]).then_inc(xs_in[jp[1]], 16)

            act.wait_ge(scattered, 16 * T)
            load_rows((0, 0))
            load_rows((0, 1))

            def step_b(of):
                t0, t1, t2 = of(0), of(1), of(2)
                if t2 is not None:
                    n2 = num(t2)
                    act.wait_ge(e["hT_done"], 2 * n2 + 1)
                    act.activation(HBT[:, 0:4, :].rearrange("p k t -> p (k t)"), PB[5][:, :], ACT.Copy)\
                        .then_inc(e["hT_a"], 1)
                if t0 is not None:
                    n = num(t0)
                    act.wait_ge(e["sT_done"], n + 1)
                    act.activation(XST[:, t0[1], :, :].rearrange("p k t -> p (k t)"), PB[0][:, 0:D], ACT.Copy)\
                        .then_inc(e["sT_sb"], 1)
                    if not isinstance(n, int) or n + 2 < NT:
                        load_rows((t0[0] + 1, t0[1]))
                if t1 is not None:
                    n = num(t1)
                    for hf in range(2):
                        act.wait_ge(e["b_h1"], 2 * n + hf + 1)
                        if not first(t1, 1):
                            act.wait_ge(e["b_mult"], 2 * n + hf - 1)
                        act.activation(G[:, hf * 512:(hf + 1) * 512], PB[1 + hf][:, :], ACT.Gelu)\
                            .then_inc(e["b_gelu"], 1)
                if t2 is not None:
                    act.wait_ge(slot_uses, n2 + 2)
                    if not first(t2, 1):
                        act.wait_ge(ys_out, 16 * n2)
                    act.activation(YS[:, :], PB[7][:, 0:D], ACT.Copy).then_inc(e["by_sb"], 1)
                    act.wait_ge(e["by_sb"], n2 + 1)
                    act.dma_start(ys[bass.ds(n2 * P, P), :], YS[:, :]).then_inc(ys_out, 16)

            def fold_up():
                act.wait_ge(scattered, 16 * T)
                for m in range(KF):
                    act.wait_ge(rt_ps, m + 1)
                    act.activation(RT[:, m, :], PB[0 if m % 2 == 0 else 7][:, 0:W1P], ACT.Copy)\
                        .then_inc(rt_sb, 1)

            sweep_b(act, step_b, fold_up)

            def take(b, n, out, func, src=slice(0, 512), bias=None):
                act.wait_ge(ring_full[n % 2], ring_before(b, n) + 1)
                extra = {} if bias is None else {"bias": bias}
                act.activation(out, PB[6 + n % 2][:, src], func, **extra).then_inc(ring_free[n % 2], 1)

            def copies(g, r, dst):
                act.wait_ge(c["c_xT"], TB * g + 2 * r + 2)
                act.activation(dst[:, :, 2 * r * P:(2 * r + 2) * P].rearrange("p k (q t) -> p k q t", q=2),
                               PB[0][:, :].rearrange("p (q k t) -> p k q t", q=2, k=KD),
                               ACT.Copy).then_inc(c["c_xT_sb"], 1)

            def piece(b, n):
                if n < 4:
                    for m in (2 * n, 2 * n + 1):
                        take(b, 6 + m, H4[:, m, :], ACT.Gelu, bias=BH[:, m:m + 1])

            def keys_values(b):
                for m in range(KD):
                    take(b, m, K1T[:, m, :], ACT.Copy)
                for r in range(2):
                    take(b, 2 + r, V1[:, 2 * r:2 * r + 2, :].rearrange("p t d -> p (t d)"), ACT.Copy)

            def step_cd(b, has_c, has_d, has_next):
                if has_c:
                    if has_d:
                        keys_values(b)
                        copies(norm_d(b), 0, XN4T)
                    for m in range(KD):
                        take(b, 4 + m, QT[:, m, :], ACT.Identity, bias=BQ[:, m:m + 1])
                    if has_d:
                        copies(norm_d(b), 1, XN4T)
                else:
                    for r in range(2):
                        copies(norm_d(b), r, XN4T)
                    for n in range(4):
                        piece(b, n)
                    return
                def weights(q):
                    n = TB * b + q
                    act.wait_ge(c["nmax_s"], n + 1)
                    if not (isinstance(n, int) and n < 2):
                        act.wait_ge(c["pT_done"], n - 1)
                        act.wait_ge(c["rinv"], n - 1)
                    act.activation(PS[:, q % 2, :], PB[1][:, :], ACT.Exp, bias=NMS[:, q % 2:q % 2 + 1],
                                   scale=float(D) ** -0.5, accum_out=SU[:, q % 2:q % 2 + 1])\
                        .then_inc(c["p_done"], 1)

                weights(0)
                for q in range(TB):
                    n = TB * b + q
                    act.wait_ge(c["pT_done"], n + 1)
                    act.activation(PT.rearrange("p k t -> p (k t)"), PB[2][:, :], ACT.Copy)\
                        .then_inc(c["pT_sb"], 1)
                    if q + 1 < TB:
                        weights(q + 1)
                    if has_next and q == 2:
                        copies(norm_c(b + 1), 0, XN3T)
                    if has_d:
                        piece(b, 2 * q)
                    if has_next and q == 2:
                        copies(norm_c(b + 1), 1, XN3T)
                    copy_c(n)
                    if has_d:
                        piece(b, 2 * q + 1)

            def copy_c(n):
                act.wait_ge(c["cT_done"], n + 1)
                act.activation(CT.rearrange("p k t -> p (k t)"), PB[5][:, 0:D], ACT.Copy)\
                    .then_inc(c["cT_sb"], 1)

            for n in range(KF):
                k, m0 = n // 4, 2 * (n % 4)
                act.wait_ge(wm_ps, n + 1)
                act.activation(WEFF[:, k, m0 * P:(m0 + 2) * P], PB[6 + n % 2][:, 0:2 * P], ACT.Copy)\
                    .then_inc(wm_sb, 1)
            for m in range(KF):
                act.wait_ge(wm_ps, KF + m + 1)
                act.activation(MDN[:, m, :], PB[6 + m % 2][:, 0:D], ACT.Copy).then_inc(wm_sb, 1)
            keys_values(0)
            for r in range(2):
                copies(0, r, XN3T)
            sweep_cd(act, step_cd)

        @block.vector
        def _(dve):
            def hold(signal, value):
                dve.wait_ge(signal, value)
                if not isinstance(value, int):
                    dve.sem_inc(held, 1)

            def step(of):
                t0, t1, t2, t3, t4 = of(0), of(1), of(2), of(3), of(4)
                if t1 is not None:
                    n, par = num(t1), t1[1]
                    dve.wait_ge(s["q_done"], n + 1)
                    dve.wait_ge(s["kv_sb"], n + 1)
                    prod = PRODQ[:, :].rearrange("p (i j h) -> p i j h", i=DK, j=DK)
                    dve.tensor_tensor(
                        prod,
                        spread(PB[1][:, 0:D].rearrange("p (i o h) -> p i o h", i=DK, o=1), 2, DK),
                        spread(KV[:, par, 0:D].rearrange("p (o j h) -> p o j h", o=1, j=DK), 1, DK),
                        ALU.mult).then_inc(s["qk_prod"], 1)
                if t4 is not None:
                    if isinstance(t4[0], int) and num(t4) == T - 1:
                        places()
                    mult(t4, 0)
                if t1 is not None:
                    dve.wait_ge(s["qk_prod"], n + 1)
                    if not first(t1, 1):
                        dve.wait_ge(s["exp_done"], n)
                    dve.tensor_reduce(SC[:, :].rearrange("p (i j) -> p i j", i=DK), prod, AX.X, ALU.add)\
                        .then_inc(s["scores"], 1)
                if t4 is not None:
                    mult(t4, 1)
                if t3 is not None:
                    n3 = num(t3)
                    dve.wait_ge(s["o_done"], n3 + 1)
                    if first(t3, 1):
                        dve.wait_ge(tanh_s, 1)
                    dve.scalar_tensor_tensor(X[:, n3, :], PB[5][:, 0:D], TG[:, 0:1], X[:, n3, :],
                                             ALU.mult, ALU.add).then_inc(s["x1_ready"], 1)
                if t0 is not None:
                    n0 = num(t0)
                    hold(tile_in[t0[1]], 32 * t0[0] + 32)
                    dve.bn_stats(ST[:, 0, :], X[:, n0, :]).then_inc(s["ln1_stats"], 1)
                if t3 is not None:
                    hold(s["x1_ready"], n3 + 1)
                    dve.bn_stats(ST[:, 1, :], X[:, n3, :]).then_inc(s["ln2_stats"], 1)
                if t1 is not None:
                    dve.wait_ge(s["scores"], n + 1)
                    dve.tensor_reduce(SM[:, 0, :], SC[:, :].rearrange("p (i j) -> p i j", i=DK), AX.X, ALU.max)\
                        .then_inc(s["rowmax"], 1)
                for tt, r, nm in ((t0, 0, "ln1"), (t3, 1, "ln2")):
                    if tt is not None:
                        hold(s[nm + "_stats"], num(tt) + 1)
                        dve.bn_aggr(MV[:, r, 0:2], ST[:, r, :]).then_inc(s[nm + "_agg"], 1)
                if t1 is not None:
                    dve.wait_ge(s["rowmax"], n + 1)
                    dve.tensor_tensor(SC[:, :].rearrange("p (i j) -> p i j", i=DK),
                                      SC[:, :].rearrange("p (i j) -> p i j", i=DK),
                                      spread(SM[:, 0, :].rearrange("p (i o) -> p i o", o=1), 2, DK),
                                      ALU.subtract).then_inc(s["shifted"], 1)
                for tt, r, nm in ((t3, 1, "ln2"), (t0, 0, "ln1")):
                    if tt is not None:
                        dve.wait_ge(s[nm + "_agg"], num(tt) + 1)
                        dve.tensor_scalar(MV[:, r, 2:3], MV[:, r, 1:2], EPS, None, ALU.add)\
                            .then_inc(s[nm + "_eps"], 1)
                if t2 is not None:
                    n2 = num(t2)
                    dve.wait_ge(s["exp_done"], n2 + 1)
                    dve.tensor_reduce(SM[:, 1, :], PR[:, t2[1], :].rearrange("p (i j) -> p i j", i=DK),
                                      AX.X, ALU.add).then_inc(s["sums"], 1)
                if t3 is not None:
                    dve.wait_ge(s["ln2_rstd"], n3 + 1)
                    if not first(t3, 1):
                        dve.wait_ge(s["x2T_done"], n3)
                        dve.wait_ge(s["xn2_kept"], n3)
                    dve.tensor_scalar(XH[:, :], X[:, n3, :], MV[:, 1, 0:1], MV[:, 1, 3:4],
                                      ALU.subtract, ALU.mult).then_inc(s["xn2_ready"], 1)
                if t0 is not None:
                    dve.wait_ge(s["ln1_rstd"], n0 + 1)
                    if not first(t0, 1):
                        dve.wait_ge(s["xT_done"], n0)
                    dve.tensor_scalar(XN[:, :], X[:, n0, :], MV[:, 0, 0:1], MV[:, 0, 3:4],
                                      ALU.subtract, ALU.mult).then_inc(s["xn_ready"], 1)
                if t2 is not None:
                    dve.wait_ge(s["sums"], n2 + 1)
                    dve.reciprocal(RI[:, :], SM[:, 1, :]).then_inc(s["recip"], 1)
                    if not first(t2, 1):
                        dve.wait_ge(s["aT_done"], n2)
                    aov = AO[:, :].rearrange("p (i h) -> p i h", i=DK)
                    for hf in range(2):
                        H2 = NH // 2
                        dve.wait_ge(s["av_half"], 2 * n2 + hf + 1)
                        dve.tensor_reduce(
                            aov[:, :, hf * H2:(hf + 1) * H2],
                            PRODV[:, :].rearrange("p (f i h j) -> p f i h j", f=2, i=DK, h=H2)
                            [:, hf, :, :, 0:DK // 2], AX.X, ALU.add).then_inc(s["av_read"], 1)
                if t3 is not None:
                    dve.wait_ge(s["gate_done"], n3 + 1)
                    dve.tensor_copy(LG[:, :], PB[5][:, 0:NE]).then_inc(s["lg_sb"], 1)
                if t2 is not None:
                    dve.wait_ge(s["av_read"], 2 * n2 + 2)
                    dve.wait_ge(s["recip"], n2 + 1)
                    dve.tensor_tensor(aov, aov, spread(RI[:, :].rearrange("p (i o) -> p i o", o=1), 2, NH),
                                      ALU.mult).then_inc(s["a_ready"], 1)
                if t3 is not None:
                    hold(s["lg_sb"], n3 + 1)
                    dve.max(TOP[:, :], LG[:, :]).then_inc(s["top_ok"], 1)
                if t4 is not None:
                    n4 = num(t4)
                    dve.wait_ge(s["y_done"], n4 + 1)
                    dve.scalar_tensor_tensor(X[:, n4, :], PB[2][:, 0:D], TG[:, 2:3], X[:, n4, :],
                                             ALU.mult, ALU.add).then_inc(s["y_added"], 1)
                if t3 is not None:
                    if first(t3, 1):
                        dve.wait_ge(iotaf, 3)
                    hold(s["top_ok"], n3 + 1)
                    dve.max_index(TOPI[:, :], TOP[:, :], LG[:, :]).then_inc(s["topi_ok"], 1)
                    dve.wait_ge(s["topi_ok"], n3 + 1)
                    dve.tensor_copy(TOPF[:, :], TOPI[:, 0:1]).then_inc(s["topf_ok"], 1)
                    dve.wait_ge(s["topf_ok"], n3 + 1)
                    dve.tensor_scalar(OH[:, n3, :], IOTA8[:, :], TOPF[:, :], None, ALU.is_equal)\
                        .then_inc(s["oh_ok"], 1)

            def mult(t, hf):
                n = 2 * num(t) + hf
                dve.wait_ge(s["gelu_done"], n + 1)
                dve.wait_ge(s["h2_done"], n + 1)
                dve.tensor_tensor(HA[:, 4 * hf:4 * hf + 4, :].rearrange("p k t -> p (k t)"),
                                  PB[7][:, :], G[:, hf * 512:(hf + 1) * 512], ALU.mult)\
                    .then_inc(s["mult_done"], 1)

            def places():
                steps = [0]

                def link(ins):
                    steps[0] += 1
                    ins.then_inc(route, 1)
                    dve.wait_ge(route, steps[0])

                def row(v, n, parts=P):
                    return spread(v.rearrange("p (o e) -> p o e", o=1), 1, n)

                def col(v, n):
                    return spread(v.rearrange("p (e o) -> p e o", o=1), 2, n)

                def grid(v, a):
                    return v.rearrange("p (a b) -> p a b", a=a)

                link(dve.tensor_tensor(LESS[:, :, :], row(IOTA8[:, :], NE), col(IOTA8[:, :], NE), ALU.is_lt))
                dve.wait_ge(rank_ps, 2)
                link(dve.tensor_copy(NTE[:, :], PB[4][:, 0:NE]))
                link(dve.tensor_tensor(grid(CMP[:, :], NE), col(NTE[:, :], T), row(IOTAM[:, :], NE), ALU.is_gt))
                link(dve.tensor_reduce(NTE[:, :], grid(CMP[:, :], NE), AX.X, ALU.add))
                link(dve.tensor_tensor(LESS[:, :, :], LESS[:, :, :], row(NTE[:, :], NE), ALU.mult))
                link(dve.tensor_reduce(BASE[:, :], LESS[:, :, :], AX.X, ALU.add))
                link(dve.tensor_scalar(NTE[:, :], BASE[:, :], float(P), None, ALU.mult))
                link(dve.tensor_tensor(RANK[:, :, :], row(NTE[:, :], T), grid(PB[1][:, 0:T * NE], T), ALU.add))
                link(dve.tensor_tensor(RANK[:, :, :], RANK[:, :, :], OH[:, :, :], ALU.mult))
                link(dve.tensor_reduce(POSF[:, :], RANK[:, :, :], AX.X, ALU.add))
                dve.tensor_copy(POS[:, :], POSF[:, :]).then_inc(pos_ready, 1)
                b1 = BASE[0:1, :]
                link(dve.tensor_tensor(GE[:, :, :], row(b1, NT), col(IOTAT[:, :], NE), ALU.is_le))
                link(dve.tensor_reduce(EI[:, :], GE[:, :, :], AX.X, ALU.add))
                link(dve.tensor_scalar(EI[:, :], EI[:, :], -1.0, None, ALU.add))
                link(dve.tensor_tensor(GE[:, :, :], row(IOTA8[0:1, :], NT), col(EI[:, :], NE), ALU.is_le))
                for k, (lo, hi) in enumerate(((3, 6), (4, 7), (2, 5))):
                    link(dve.tensor_tensor(SUM2[:, k, :], GE[:, :, lo], GE[:, :, hi], ALU.add))
                    link(dve.tensor_scalar(TAB[:, 1 + k, :], SUM2[:, k, :], 16.0, 16.0, ALU.mult, ALU.add))
                link(dve.scalar_tensor_tensor(TAB[:, 0, :], SUM2[:, 0, :], -3.0, EI[:, :], ALU.mult, ALU.add))
                dve.tensor_scalar(BASEI[:, :], b1, 1.0, None, ALU.add).then_inc(tables, 1)

            dve.wait_ge(iotas, 3)
            dve.tensor_copy(IOTA8[:, :], IOTAI[:, 0:NE]).then_inc(iotaf, 1)
            dve.tensor_copy(IOTAM[:, :], IOTAI[:, NE:NE + T]).then_inc(iotaf, 1)
            dve.tensor_copy(IOTAT[:, :], IOTAI[0:1, NE + T:NE + T + NT]).then_inc(iotaf, 1)
            sweep_a(dve, step)

            def step_b(of):
                t1, t2 = of(1), of(2)
                if t2 is not None:
                    n = num(t2)
                    dve.wait_ge(e["hT_done"], 2 * n + 2)
                    dve.tensor_copy(HBT[:, 4:8, :].rearrange("p k t -> p (k t)"), PB[6][:, :])\
                        .then_inc(e["hT_d"], 1)
                if t1 is not None:
                    n = num(t1)
                    for hf in range(2):
                        dve.wait_ge(e["b_gelu"], 2 * n + hf + 1)
                        dve.wait_ge(e["b_h2"], 2 * n + hf + 1)
                        if not first(t1, 2):
                            dve.wait_ge(e["hT_done"], 2 * n - 2)
                        dve.tensor_tensor(HB[:, t1[1], hf * 512:(hf + 1) * 512], PB[3 + hf][:, :],
                                          G[:, hf * 512:(hf + 1) * 512], ALU.mult).then_inc(e["b_mult"], 1)

            sweep_b(dve, step_b, lambda: None)

            dve.wait_ge(c_in, 16 * 14)
            dve.tensor_tensor(BCD[:, :], BIAS[:, 2, :], BIAS[:, 3, :], ALU.add).then_inc(bcd_ready, 1)

            def norm_stats(t0, g):
                for q in range(TB):
                    dve.bn_stats(STC[:, q, :], X[:, t0 + q, :]).then_inc(c["c_stats"], 1)
                for q in range(TB):
                    hold(c["c_stats"], TB * g + q + 1)
                    dve.bn_aggr(MVC[:, q, :], STC[:, q, :]).then_inc(c["c_agg"], 1)
                for q in range(TB):
                    dve.wait_ge(c["c_agg"], TB * g + q + 1)
                    dve.tensor_scalar(VE[:, q:q + 1], MVC[:, q, 1:2], EPS, None, ALU.add).then_inc(c["c_eps"], 1)

            def norm_rows(t0, g):
                dve.wait_ge(c["c_rstd"], g + 1)
                if not (isinstance(g, int) and g == 0):
                    dve.wait_ge(c["c_xT"], TB * g)
                for q in range(TB):
                    dve.tensor_scalar(XNC[:, q, :], X[:, t0 + q, :], MVC[:, q, 0:1], RS[:, q:q + 1],
                                      ALU.subtract, ALU.mult).then_inc(c["c_xn"], 1)

            def finish(b, q):
                m = TB * b - TB + q
                dve.wait_ge(ring_full[q % 2], ring_before(b, 14 + q) + 1)
                if isinstance(m, int) or q:
                    dve.wait_ge(c["fin_ready"], m)
                dve.tensor_tensor(TY, PB[6 + q % 2][:, 0:D], BCD[:, :], ALU.add).then_inc(ring_free[q % 2], 1)
                dve.wait_ge(ring_free[q % 2], ring_before(b, 14 + q) + 1)
                dve.scalar_tensor_tensor(X[:, m, :], TY, TG[:, 3:4], X[:, m, :], ALU.mult, ALU.add)\
                    .then_inc(c["fin_ready"], 1)

            def next_rows(b):
                dve.wait_ge(gathered, 16 * TB * b + 16 * TB)
                for q in range(TB):
                    dve.scalar_tensor_tensor(X[:, TB * b + q, :], YG[:, q, :], TG[:, 2:3], X[:, TB * b + q, :],
                                             ALU.mult, ALU.add).then_inc(x2_added, 1)
                hold(x2_added, TB * b + TB)
                norm_stats(TB * b, norm_c(b))

            def step_cd(b, has_c, has_d, has_next):
                if has_d:
                    hold(c["x3_ready"], TB * b)
                    norm_stats(TB * b - TB, norm_d(b))
                    norm_rows(TB * b - TB, norm_d(b))
                    if not has_c:
                        for q in range(TB):
                            finish(b, q)
                        return

                def add_out(q):
                    m = TB * b + q
                    dve.wait_ge(c["out_done"], m + 1)
                    dve.tensor_tensor(TO, PB[4][:, 0:D], BIAS[:, 1, :], ALU.add).then_inc(c["tmp_o"], 1)
                    dve.wait_ge(c["tmp_o"], m + 1)
                    dve.scalar_tensor_tensor(X[:, m, :], TO, TG[:, 1:2], X[:, m, :], ALU.mult, ALU.add)\
                        .then_inc(c["x3_ready"], 1)

                def largest(q):
                    m = TB * b + q
                    dve.wait_ge(c["sc_done"], m + 1)
                    dve.tensor_reduce(NM[:, :], PB[1][:, :], AX.X, ALU.max, negate=True).then_inc(c["nmax"], 1)
                    dve.wait_ge(c["nmax"], m + 1)
                    if not (isinstance(m, int) and m < 2):
                        dve.wait_ge(c["p_done"], m - 1)
                    dve.tensor_scalar(NMS[:, q % 2:q % 2 + 1], NM[:, :], float(D) ** -0.5, None, ALU.mult)\
                        .then_inc(c["nmax_s"], 1)

                largest(0)
                for q in range(TB):
                    m = TB * b + q
                    dve.wait_ge(c["p_done"], m + 1)
                    dve.reciprocal(RC[:, :], SU[:, q % 2:q % 2 + 1]).then_inc(c["rinv"], 1)
                    if q + 1 < TB:
                        largest(q + 1)
                    dve.wait_ge(c["av_done"], m + 1)
                    dve.wait_ge(c["rinv"], m + 1)
                    if not (isinstance(m, int) and m == 0):
                        dve.wait_ge(c["cT_done"], m)
                    dve.scalar_tensor_tensor(CC, PB[3][:, 0:D], RC[:, :], BIAS[:, 0, :], ALU.mult, ALU.add)\
                        .then_inc(c["c_ready"], 1)
                    if has_next and q == 0:
                        next_rows(b + 1)
                    if has_next and q == 1:
                        norm_rows(TB * b + TB, norm_c(b + 1))
                    if has_d and q >= 2:
                        finish(b, 2 * q - 4)
                        finish(b, 2 * q - 3)
                    add_out(q)

            dve.wait_ge(bcd_ready, 1)
            next_rows(0)
            norm_rows(0, 0)
            sweep_cd(dve, step_cd)


def kernel(x, ctx_1024, g_xattn, g_ffn, L0_xattn_Wq, L0_xattn_Wk, L0_xattn_Wv, L0_xattn_Wo,
           L0_ffn_w1s, L0_ffn_w2s, L0_ffn_w3s, L0_ffn_W1, L0_ffn_W2, L0_ffn_W3, L0_ffn_Wg,
           L1_xattn_Wk, L1_xattn_Wv, L1_xattn_bv, L1_xattn_Wq, L1_xattn_bq, L1_xattn_Wo, L1_xattn_bo,
           L1_ffn_W_exp, L1_ffn_b_exp, L1_ffn_up_weights, L1_ffn_up_bias, L1_ffn_down_weights,
           L1_ffn_W_con, L1_ffn_b_con, L1_ffn_down_bias):
    import concourse.bacc as bacc
    from concourse.bass_utils import run_bass_kernel_spmd

    def by_dim(w):
        return np.asarray(w).reshape(NH, DK, D).transpose(2, 1, 0).reshape(D, D)

    def chunks(w):
        w = np.asarray(w)
        return w.reshape(w.shape[0] // P, P, w.shape[1]).transpose(1, 0, 2).reshape(P, -1)

    experts = [[chunks(w[n]) for w in (L0_ffn_W1, L0_ffn_W2, L0_ffn_W3)] for n in range(NE)]
    experts.append([chunks(w) for w in (L0_ffn_w1s, L0_ffn_w2s, L0_ffn_w3s)])
    arrays = {
        "x": np.asarray(x).reshape(B * L, D),
        "ctxT": np.asarray(ctx_1024).reshape(B * L, D).T,
        "gates": np.concatenate([np.asarray(g_xattn), np.asarray(g_ffn)]),
        "wq0": by_dim(L0_xattn_Wq),
        "wkv0": np.concatenate([by_dim(L0_xattn_Wk), np.asarray(L0_xattn_Wv).T], axis=1),
        "wo0": np.asarray(L0_xattn_Wo).T.reshape(NH, DK, D).transpose(1, 0, 2).reshape(D, D),
        "wg": np.asarray(L0_ffn_Wg),
        "wexp": np.stack([np.concatenate(w, axis=1) for w in experts]),
        "wk1": np.asarray(L1_xattn_Wk).T, "wv1": np.asarray(L1_xattn_Wv).T,
        "wq1": np.asarray(L1_xattn_Wq).T, "wo1": np.asarray(L1_xattn_Wo).T,
        "bv1": np.asarray(L1_xattn_bv), "bq1": np.asarray(L1_xattn_bq), "bo1": np.asarray(L1_xattn_bo),
        "weT": np.asarray(L1_ffn_W_exp).T, "be": np.asarray(L1_ffn_b_exp),
        "upw": np.asarray(L1_ffn_up_weights).reshape(LOW + HIGH, F // 2, 4),
        "upb": np.asarray(L1_ffn_up_bias),
        "dnw": np.asarray(L1_ffn_down_weights).reshape(LOW + HIGH, F // 2, 4),
        "wc": np.asarray(L1_ffn_W_con), "bc": np.asarray(L1_ffn_b_con), "db": np.asarray(L1_ffn_down_bias),
    }
    arrays = {k: np.ascontiguousarray(v) for k, v in arrays.items()}
    nc = bacc.Bacc("TRN2", target_bir_lowering=False, num_devices=1)
    args = [nc.dram_tensor(k, v.shape, mybir.dt.from_np(v.dtype), kind="ExternalInput").ap()
            for k, v in arrays.items()]
    out = nc.dram_tensor("out", (B * L, D), F32, kind="ExternalOutput").ap()
    build(nc, *args, out)
    r = run_bass_kernel_spmd(nc, [arrays], core_ids=[0])
    return r.results[0]["out"].reshape(B, L, D)
```

```python
from contextlib import ExitStack

import numpy as np

import concourse.bass as bass
from concourse import mybir

F32 = mybir.dt.float32
F32R = mybir.dt.float32r
I32 = mybir.dt.int32
U32 = mybir.dt.uint32
ALU = mybir.AluOpType
ACT = mybir.ActivationFunctionType
AX = mybir.AxisListType

P = 128
B, L, D = 4, 512, 256
T = B * L // P
TB = L // P
KD = D // P
NH = 16
DK = D // NH
F = 1024
KF = F // P
NE = 8
NT = T + NE - 1
SLOTS = 3
WS = 3 * KD * F
LOW, HIGH = 7, 3
EPS = 1e-5


def spread(v, axis, n):
    shape = list(v.shape)
    shape[axis] = n
    return v.broadcast_to(shape)


def build(nc, x, ctxT, gates, wq0, wkv0, wo0, wg, wexp, wk1, wv1, wq1, wo1, bv1, bq1, bo1,
          weT, be, upw, upb, dnw, wc, bc, db, out):
    with ExitStack() as ctx:
        start, twins = {}, {}

        def sb(name, shape, dt=F32):
            start[name] = (nc.sbuf_base + 31) // 32 * 32
            return ctx.enter_context(nc.sbuf_tensor(name, shape, dt))

        def f32r(v):
            t = v.tensor
            if t.name not in twins:
                twins[t.name] = nc.alloc_sbuf_tensor_at(t.name + "_r", list(t.shape), F32R, offset=start[t.name])
            return bass.AP(tensor=twins[t.name], offset=v.offset, ap=[list(a) for a in v.ap])

        def rounded(v):
            return f32r(v).bitcast(F32)

        def sem(name):
            return ctx.enter_context(nc.semaphore(name))

        xs = nc.dram_tensor("sorted_rows", (NT * P, D), F32).ap()
        ys = nc.dram_tensor("expert_rows", (NT * P, D), F32).ap()

        X = sb("X", [P, T, D])
        XN2 = sb("XN2", [P, T, D])
        SLOT = sb("SLOT", [P, SLOTS, WS])
        WQ0 = sb("WQ0", [P, KD, D])
        WKV0 = sb("WKV0", [P, KD, 2 * D])
        WO0 = sb("WO0", [P, KD, D])
        WG = sb("WG", [P, KD, NE])
        WK1 = sb("WK1", [P, KD, D])
        WV1 = sb("WV1", [P, KD, D])
        WQ1 = sb("WQ1", [P, KD, D])
        WO1 = sb("WO1", [P, KD, D])
        BIAS = sb("BIAS", [P, 4, D])
        BQ = sb("BQ", [P, KD])
        IDENT = sb("IDENT", [P, P])
        ABOVE = sb("ABOVE", [P, P])
        ONES = sb("ONES", [P, P])
        MHALF = sb("MHALF", [P, 1])
        GATE = sb("GATE", [P, 4])
        TG = sb("TG", [P, 4])
        IOTA8 = sb("IOTA8", [P, NE])
        IOTAM = sb("IOTAM", [P, T])
        IOTAT = sb("IOTAT", [1, NT])
        IOTAI = sb("IOTAI", [P, NE + T + NT], I32)
        PRODQ = sb("PRODQ", [P, DK * DK * NH])
        PRODV = sb("PRODV", [P, DK * DK * NH])
        SHARED = sb("SHARED", [P, 2 * F])
        CTX = SHARED[:, 0:2 * KD * P].rearrange("p (r k t) -> p r k t", r=2, k=KD)
        PR = SHARED[:, 2 * KD * P:2 * KD * P + 2 * D].rearrange("p (r d) -> p r d", r=2)
        KV = SHARED[:, 2 * KD * P + 2 * D:2 * F].rearrange("p (r d) -> p r d", r=2)
        XN = sb("XN", [P, D])
        XH = sb("XH", [P, D])
        XT = sb("XT", [P, KD, P])
        SC = sb("SC", [P, D])
        AO = sb("AO", [P, D])
        AT = sb("AT", [P, KD, P])
        X2T = sb("X2T", [P, KD, P])
        ST = sb("ST", [P, 2, 6])
        MV = sb("MV", [P, 2, 4])
        SM = sb("SM", [P, 2, DK])
        RI = sb("RI", [P, DK])
        LG = sb("LG", [P, NE])
        TOP = sb("TOP", [P, NE])
        TOPI = sb("TOPI", [P, NE], U32)
        TOPF = sb("TOPF", [P, 1])
        G = sb("G", [P, F])
        HA = sb("HA", [P, KF, P])
        OH = sb("OH", [P, T, NE])
        RANK = sb("RANK", [P, T, NE])
        LESS = sb("LESS", [P, NE, NE])
        CMP = sb("CMP", [P, NE * T])
        NTE = sb("NTE", [P, NE])
        BASE = sb("BASE", [P, NE])
        POSF = sb("POSF", [P, T])
        POS = sb("POS", [P, T], U32)
        EI = sb("EI", [1, NT])
        GE = sb("GE", [1, NT, NE])
        SUM2 = sb("SUM2", [1, SLOTS, NT])
        TAB = sb("TAB", [1, 1 + SLOTS, NT], I32)
        BASEI = sb("BASEI", [1, NE], I32)

        flatA = PRODQ[:, :]
        flatV = PRODV[:, :]
        XS = sb("XS", [P, 2, D])
        XST = sb("XST", [P, 2, KD, P])
        HB = SHARED[:, :].rearrange("p (r f) -> p r f", r=2)
        HBT = HA
        YS = sb("YS", [P, D])
        COEF = flatA.rearrange("p (r k c) -> p r k c", r=2, c=4)
        WEFF = flatA[:, 0:KD * F].rearrange("p (k f) -> p k f", k=KD)
        MDN = flatA[:, KD * F:2 * KD * F].rearrange("p (c d) -> p c d", c=KF)
        Z = flatV[:, 0:KF * D].rearrange("p (c d) -> p c d", c=KF)
        EB = flatV[:, KF * D:KF * D + 2 * F].rearrange("p (r f) -> p r f", r=2)
        W1P = D + 1
        x2 = XN2[:, :, :].rearrange("p t d -> p (t d)")
        RT = x2[:, 0:KF * W1P].rearrange("p (c d) -> p c d", c=KF)
        EC = x2[:, KF * W1P:KF * W1P + F]
        TMPZ = x2[:, 0:4 * D].rearrange("p (a d) -> p a d", a=4)
        WET = sb("WET", [P, KF, W1P])
        CTXB = WET[:, :, :].rearrange("p c d -> p (c d)")[:, 0:KD * L].rearrange("p (k t) -> p k t", k=KD)
        HIC = sb("HIC", [P, 2, HIGH, 4, 4])
        UPB = sb("UPB", [P, KF])
        TMPH = sb("TMPH", [P, 4, W1P])
        TMP = TMPH[:, :, :].rearrange("p a b -> p (a b)")
        BH = sb("BH", [P, KF])
        sf = SLOT[:, :, :].rearrange("p s w -> p (s w)")
        at = [0]

        def part(n):
            at[0] += n
            return sf[:, at[0] - n:at[0]]

        XN3T = part(KD * L).rearrange("p (k t) -> p k t", k=KD)
        XN4T = part(KD * L).rearrange("p (k t) -> p k t", k=KD)
        QT = part(KD * L).rearrange("p (k t) -> p k t", k=KD)
        K1T = part(KD * L).rearrange("p (k t) -> p k t", k=KD)
        V1 = part(TB * D).rearrange("p (t d) -> p t d", t=TB)
        PS = part(2 * L).rearrange("p (r t) -> p r t", r=2)
        PT = part(L).rearrange("p (k t) -> p k t", k=TB)
        XNC = part(TB * D).rearrange("p (r d) -> p r d", r=TB)
        CC = part(D)
        CT = part(D).rearrange("p (k t) -> p k t", k=KD)
        H4 = part(KF * L).rearrange("p (c t) -> p c t", c=KF)
        TO = part(D)
        TY = part(D)
        YG = part(TB * D).rearrange("p (t d) -> p t d", t=TB)
        XN3TL, XN4TL, QTL, K1TL = [part(KD * L).rearrange("p (k t) -> p k t", k=KD) for _ in range(4)]
        PTL = part(L).rearrange("p (k t) -> p k t", k=TB)
        assert at[0] <= SLOTS * WS
        V1L = SHARED[:, 0:TB * D].rearrange("p (t d) -> p t d", t=TB)
        CTL = SHARED[:, TB * D:TB * D + D].rearrange("p (k t) -> p k t", k=KD)
        CTXL = WKV0[:, :, :].rearrange("p a b -> p (a b)").rearrange("p (k t) -> p k t", k=KD)
        WK1L = [WQ0[:, k, :] for k in range(KD)]
        WV1L = [WO0[:, k, :] for k in range(KD)]
        WQ1L = [XN[:, :], XH[:, :]]
        WO1L = [SC[:, :], AO[:, :]]
        WEFFL = [G[:, :], HA[:, :, :].rearrange("p k t -> p (k t)")]
        MDNL = x2[:, 0:KF * D].rearrange("p (c d) -> p c d", c=KF)
        HF = [v.rearrange("p r d -> p (r d)") for v in (XS[:, :, :], XST[:, :, :, :].rearrange("p r k t -> p r (k t)"))]
        H4L = flatV.rearrange("p (c t) -> p c t", c=KF)
        NM = sb("NM", [P, 1])
        NMS = sb("NMS", [P, 2])
        SU = sb("SU", [P, 2])
        RC = sb("RC", [P, 1])
        STC = sb("STC", [P, TB, 6])
        MVC = sb("MVC", [P, TB, 2])
        VE = sb("VE", [P, TB])
        RS = sb("RS", [P, TB])
        BCD = sb("BCD", [P, D])

        PB = [ctx.enter_context(nc.psum_tensor(f"bank{i}", [P, 512], F32)) for i in range(8)]

        w_in = sem("w_in")
        wg_in = sem("wg_in")
        c_in = sem("c_in")
        tile_in = [sem("tile_in0"), sem("tile_in1")]
        slot_in = [sem(f"slot_in{i}") for i in range(SLOTS)]
        consts = sem("consts")
        iotas = sem("iotas")
        iotaf = sem("iotaf")
        zero_ms = sem("zero_ms")
        zeroed = sem("zeroed")
        tanh_s = sem("tanh_s")

        names = """qk_prod scores rowmax shifted exp_done sums a_ready av_read ln1_stats ln1_agg ln1_eps
        ln1_rstd xn_ready ln2_stats ln2_agg ln2_eps ln2_rstd xn2_ready x1_ready xT_done xT_sb q_done
        kv_done kv_sb x2T_done x2T_sb aT_done aT_sb o_done gate_done lg_sb top_ok topi_ok topf_ok
        oh_ok xn2_kept h1_done h2_done gelu_done mult_done y_done y_added av_prod av_half recip""".split()
        s = {n: sem(n) for n in names}
        route = sem("route")
        held = sem("held")
        rank_ps = sem("rank_ps")
        tables = sem("tables")
        pos_ready = sem("pos_ready")
        scattered = sem("scattered")
        slot_uses = sem("slot_uses")

        bnames = """sT_done sT_sb b_h1 b_h2 b_gelu b_mult hT_done hT_a hT_d by_sb""".split()
        e = {n: sem(n) for n in bnames}
        xs_in = [sem("xs_in0"), sem("xs_in1")]
        ys_out = sem("ys_out")
        pool = sem("pool")
        coef_in = [sem("coef_in0"), sem("coef_in1")]
        e_up = sem("e_up")
        rt_ps = sem("rt_ps")
        rt_sb = sem("rt_sb")
        rt_high = sem("rt_high")
        z_first = sem("z_first")
        z_high = sem("z_high")
        wm_ps = sem("wm_ps")
        wm_high = sem("wm_high")
        wm_sb = sem("wm_sb")
        low_parts = sem("low_parts")
        ctx_split = sem("ctx_split")
        h4_high = sem("h4_high")
        h4_split = sem("h4_split")
        gathered = sem("gathered")
        x2_added = sem("x2_added")
        ctx_in = sem("ctx_in")

        cnames = """c_stats c_agg c_eps c_rstd c_xn c_xT c_xT_hi c_xT_sb v_done v_high v_sb sc_done nmax nmax_s p_done pT_done pT_hi pT_sb
        av_done rinv c_ready cT_done cT_hi cT_sb out_done tmp_o x3_ready fin_ready""".split()
        c = {n: sem(n) for n in cnames}
        ring_full = [sem("ring_full0"), sem("ring_full1")]
        ring_high = [sem("ring_high0"), sem("ring_high1")]
        ring_free = [sem("ring_free0"), sem("ring_free1")]
        stored = sem("stored")
        bcd_ready = sem("bcd_ready")

        block = ctx.enter_context(nc.Block())

        LAG = 4
        PAUSE = 7

        def lag(j, par, n):
            m = par - n
            return j + m // 2, m % 2

        def sweep(eng, step, count, lags, start, ahead=0, pause=None, at_pause=None):
            def tiles(j, par, t):
                def of(n):
                    if t is not None and not 0 <= t - n < count:
                        return None
                    return lag(j, par, n)
                return of
            for t in range(2 * start):
                step(tiles(t // 2, t % 2, t))
            end = (count - ahead) // 2
            for lo, hi in ((start, end),) if pause is None else ((start, pause), (pause, end)):
                with eng.Fori(lo, hi) as j:
                    step(tiles(j, 0, None))
                    step(tiles(j, 1, None))
                if hi == pause:
                    at_pause()
            for t in range(2 * end, count + lags):
                step(tiles(t // 2, t % 2, t))

        def sweep_a(eng, step):
            sweep(eng, step, T, LAG, LAG // 2 + 1)

        def sweep_b(eng, step, at_pause=None):
            sweep(eng, step, NT, 2, 2, 2, PAUSE if at_pause else None, at_pause)

        def num(jp):
            return 2 * jp[0] + jp[1]

        def first(jp, n):
            return isinstance(jp[0], int) and num(jp) < n

        def ring_before(b, n):
            if isinstance(b, int) and b == 0:
                return n // 2
            return 8 * b - 6 + (n - 4 if isinstance(b, int) and b == B else n) // 2

        def norm_c(b):
            return 0 if isinstance(b, int) and b == 0 else 2 * b - 1

        def norm_d(b):
            return 2 * b - 1 if isinstance(b, int) and b == B else 2 * b

        def pair(v, r):
            return v[:, :, 2 * r * P:(2 * r + 2) * P].rearrange("p k (q t) -> p k q t", q=2)

        def flipped_bank(r):
            return PB[5 * r][:, :].rearrange("p (q k t) -> p k q t", q=2, k=KD)

        def high_pair(n, bit, q):
            c0 = ((q >> bit) << (bit + 1)) | (q & ((1 << bit) - 1))
            cf = [HIC[:, n, bit, q, i:i + 1] for i in range(4)]
            if n:
                cf[1], cf[2] = cf[2], cf[1]
            return c0, c0 | (1 << bit), cf

        FOLD = [PB[n] for n in (6, 7, 1, 2)]

        def sweep_cd(eng, step):
            step(0, True, False, True)
            with eng.Fori(1, B - 1) as b:
                step(b, True, True, True)
            step(B - 1, True, True, False)
            step(B, False, True, False)

        @block.sync
        def _(sp):
            def load_tile(j, par):
                t = 2 * j + par
                if not (isinstance(j, int) and j == 0):
                    sp.wait_ge(tile_in[par], 32 * j)
                    sp.wait_ge(s["kv_done"], t - 1)
                sp.dma_start(X[:, t, :], x[bass.ds(t * P, P), :]).then_inc(tile_in[par], 16)
                sp.dma_start(CTX[:, par, :, :],
                             ctxT[:, bass.ds(t * P, P)].rearrange("(k p) t -> p k t", p=P))\
                    .then_inc(tile_in[par], 16)

            load_tile(0, 0)
            for w, src in ((WQ0, wq0), (WKV0, wkv0)):
                sp.dma_start(w[:, :, :], src.rearrange("(k p) n -> p k n", p=P)).then_inc(w_in, 16)
            load_tile(0, 1)
            for w, src in ((WO0, wo0), (WG, wg)):
                sp.dma_start(w[:, :, :], src.rearrange("(k p) n -> p k n", p=P)).then_inc(wg_in, 16)
            sp.dma_start(GATE[:, :], gates.partition_broadcast(P)).then_inc(wg_in, 16)
            sp.dma_start(SLOT[:, 2, :], wexp[NE]).then_inc(slot_in[2], 16)
            with sp.Fori(1, T // 2) as j:
                load_tile(j, 0)
                load_tile(j, 1)
            for w, src in ((WK1, wk1), (WV1, wv1), (WQ1, wq1), (WO1, wo1)):
                sp.dma_start(w[:, :, :], src.rearrange("(k p) n -> p k n", p=P)).then_inc(c_in, 16)
            for n, src in enumerate((bv1, bo1, bc, db)):
                sp.dma_start(BIAS[:, n, :], src.partition_broadcast(P)).then_inc(c_in, 16)
            with nc.allow_non_contiguous_dma("biases and coefficients by partition"):
                sp.dma_start(BQ[:, :], bq1.rearrange("(k p) -> p k", p=P)).then_inc(c_in, 16)
                sp.dma_start(UPB[:, :], upb.rearrange("(k p) -> p k", p=P)).then_inc(c_in, 16)
                for n, src in enumerate((upw, dnw)):
                    sp.dma_start(HIC[:, n, :, :, :], src[LOW:LOW + HIGH].rearrange(
                        "s (q p) c -> p s q c", p=P)).then_inc(c_in, 16)
                sp.dma_start(WET[:, :, 0:D], weT.rearrange("(c p) d -> p c d", p=P)).then_inc(c_in, 16)
                sp.dma_start(WET[:, :, D:W1P], be.rearrange("(c p o) -> p c o", p=P, o=1))\
                    .then_inc(c_in, 16)
            sp.dma_start(SLOT[:, 0, :], wexp[0]).then_inc(slot_in[0], 16)
            sp.dma_start(SLOT[:, 1, :], wexp[1]).then_inc(slot_in[1], 16)
            sp.wait_ge(s["y_done"], T)
            sp.wait_ge(scattered, 16 * T)
            for r in range(2):
                sp.wait_ge(xs_in[r], 32)
            sp.dma_start(SLOT[:, 2, :], wexp[2]).then_inc(slot_in[2], 16)
            sp.wait_ge(tables, 1)
            for n in range(SLOTS, NE):
                base = sp.value_load(BASEI[0:1, n - 2:n - 1], min_val=1, max_val=NT + 1)
                sp.wait_ge(slot_uses, base)
                sp.dma_start(SLOT[:, n % SLOTS, :], wexp[n]).then_inc(slot_in[n % SLOTS], 16)
            sp.wait_ge(rt_ps, KF)

            def load_ctx(b):
                sp.dma_start(CTXB, ctxT[:, bass.ds(b * L, L)].rearrange("(k p) t -> p k t", p=P))\
                    .then_inc(ctx_in, 16)

            load_ctx(0)

            def outputs(b):
                for q in range(TB):
                    tile = b * TB + q
                    sp.wait_ge(c["fin_ready"], tile + 1)
                    sp.dma_start(out[bass.ds(tile * P, P), :], X[:, tile, :]).then_inc(stored, 16)

            def context_used(b):
                sp.wait_ge(c["v_sb"], 2 * b + 2)

            context_used(0)
            load_ctx(1)
            with sp.Fori(1, B - 1) as b:
                context_used(b)
                load_ctx(b + 1)
                outputs(b - 1)
            outputs(B - 2)
            outputs(B - 1)
            sp.wait_ge(stored, 16 * T)

        @block.gpsimd
        def _(gp):
            gp.memset(IDENT[:, :], 0.0).then_inc(consts, 1)
            gp.memset(ABOVE[:, :], 0.0).then_inc(consts, 1)
            gp.memset(ONES[:, :], 1.0).then_inc(consts, 1)
            gp.memset(MHALF[:, :], -0.5).then_inc(consts, 1)
            gp.wait_ge(consts, 4)
            gp.affine_select(out=IDENT[:, :], in_=IDENT[:, :], compare_op=ALU.not_equal, fill=1.0,
                             base=0, pattern=[[-1, P]], channel_multiplier=1).then_inc(consts, 1)
            gp.affine_select(out=ABOVE[:, :], in_=ABOVE[:, :], compare_op=ALU.is_ge, fill=1.0,
                             base=0, pattern=[[-1, P]], channel_multiplier=1).then_inc(consts, 1)
            gp.iota(IOTAI[:, 0:NE], pattern=[[1, NE]], base=0, channel_multiplier=0).then_inc(iotas, 1)
            gp.iota(IOTAI[:, NE:NE + T], pattern=[[P, T]], base=0, channel_multiplier=0).then_inc(iotas, 1)
            gp.iota(IOTAI[:, NE + T:], pattern=[[1, NT]], base=0, channel_multiplier=0).then_inc(iotas, 1)
            gp.memset(PRODV[:, :], 0.0).then_inc(zero_ms, 1)
            gp.wait_ge(zero_ms, 1)
            for r0 in range(0, NT, T):
                n = min(T, NT - r0)
                gp.dma_start(xs[r0 * P:(r0 + n) * P, :].rearrange("(t p) d -> p t d", p=P),
                             PRODV[:, 0:n * D].rearrange("p (t d) -> p t d", t=n)).then_inc(zeroed, 16)

            def step(of):
                if (t3 := of(3)) is not None:
                    gp.wait_ge(s["ln2_eps"], num(t3) + 1)
                    gp.tensor_tensor(MV[:, 1, 3:4], MV[:, 1, 2:3], MHALF[:, :], ALU.pow)\
                        .then_inc(s["ln2_rstd"], 1)
                if (t0 := of(0)) is not None:
                    gp.wait_ge(s["ln1_eps"], num(t0) + 1)
                    gp.tensor_tensor(MV[:, 0, 3:4], MV[:, 0, 2:3], MHALF[:, :], ALU.pow)\
                        .then_inc(s["ln1_rstd"], 1)
                if (t1 := of(1)) is not None:
                    n, par = num(t1), t1[1]
                    gp.wait_ge(s["exp_done"], n + 1)
                    gp.wait_ge(s["kv_sb"], n + 1)
                    if first(t1, 1):
                        gp.wait_ge(zeroed, 32)
                    for hf in range(2):
                        if not first(t1, 1):
                            gp.wait_ge(s["av_read"], 2 * (n - 1) + hf + 1)
                        H2 = NH // 2
                        o = PRODV[:, :].rearrange("p (f i h j) -> p f i h j", f=2, i=DK, h=H2)[:, hf]
                        pr = spread(PR[:, par, :].rearrange("p (i o j) -> p i o j", i=DK, o=1), 2, H2)
                        v = KV[:, par, D + hf * H2 * DK:D + (hf + 1) * H2 * DK]
                        v = spread(v.rearrange("p (o h j) -> p o h j", o=1, j=DK), 1, DK)
                        gp.tensor_tensor(o, pr, v, ALU.mult).then_inc(s["av_prod"], 1)
                        gp.wait_ge(s["av_prod"], 2 * n + hf + 1)
                        gp.tensor_tensor(o[:, :, :, 0:DK // 2], o[:, :, :, 0:DK // 2], o[:, :, :, DK // 2:DK],
                                         ALU.add).then_inc(s["av_half"], 1)

            sweep_a(gp, step)

            stages = [(0, upw, k) for k in range(LOW)] + [(1, dnw, k) for k in reversed(range(LOW))]

            def load_coef(n):
                _, src, k = stages[n]
                gp.dma_start(COEF[:, n % 2, :, :].rearrange("p k c -> p (k c)"),
                             src[k].rearrange("k c -> (k c)").partition_broadcast(P))\
                    .then_inc(coef_in[n % 2], 16)

            gp.wait_ge(zeroed, 32)
            gp.wait_ge(s["a_ready"], T)
            load_coef(0)
            load_coef(1)
            gp.dma_start(Z, wc.rearrange("(c p) d -> p c d", p=P)).then_inc(zeroed, 16)

            gp.wait_ge(pos_ready, 1)
            gp.wait_ge(s["xn2_kept"], T)
            for t in range(T):
                gp.indirect_dma_start(out=xs, out_offset=bass.IndirectOffsetOnAxis(ap=POS[:, t:t + 1], axis=0),
                                      in_=XN2[:, t, :], in_offset=None).then_inc(scattered, 16)

            done = [0]

            def run(ins):
                done[0] += 1
                ins.then_inc(pool, 1)

            def settle():
                gp.wait_ge(pool, done[0])

            gp.wait_ge(scattered, 16 * T)
            bufs = [EB[:, 0, :], EB[:, 1, :], EC]

            def low(n, src, dst):
                down, _, k = stages[n]
                w = 2 ** k
                a, b = (src.rearrange("p (n two w) -> p n two w", two=2, w=w)[:, :, i, :] for i in (0, 1))
                oa, ob = (dst.rearrange("p (n two w) -> p n two w", two=2, w=w)[:, :, i, :] for i in (0, 1))
                cf = [COEF[:, n % 2, :, i].rearrange("p (n w) -> p n w", w=w) for i in range(4)]
                if down:
                    cf[1], cf[2] = cf[2], cf[1]
                t = [TMP[:, i * F // 2:(i + 1) * F // 2].rearrange("p (n w) -> p n w", w=w) for i in range(2)]
                gp.wait_ge(coef_in[n % 2], 16 * (n // 2 + 1))
                settle()
                run(gp.tensor_tensor(oa, a, cf[0], ALU.mult))
                run(gp.tensor_tensor(t[0], b, cf[1], ALU.mult))
                run(gp.tensor_tensor(ob, a, cf[2], ALU.mult))
                run(gp.tensor_tensor(t[1], b, cf[3], ALU.mult))
                settle()
                if n + 2 < len(stages):
                    load_coef(n + 2)
                run(gp.tensor_tensor(oa, oa, t[0], ALU.add))
                run(gp.tensor_tensor(ob, ob, t[1], ALU.add))

            def eye(dst):
                settle()
                run(gp.memset(dst, 0.0))
                settle()
                v = dst.rearrange("p (c m) -> p c m", c=KF)
                run(gp.affine_select(out=v, in_=v, compare_op=ALU.not_equal, fill=1.0, base=0,
                                     pattern=[[0, KF], [-1, P]], channel_multiplier=1))

            def high(n, m, width, stage):
                for q in range(4):
                    c0, c1, cf = high_pair(n, stage, q)
                    settle()
                    for i, (src, k) in enumerate(((c0, 0), (c1, 1), (c0, 2), (c1, 3))):
                        run(gp.tensor_scalar(TMPH[:, i, 0:width], m[:, src, :], cf[k], None, ALU.mult))
                    settle()
                    run(gp.tensor_tensor(m[:, c0, :], TMPH[:, 0, 0:width], TMPH[:, 1, 0:width], ALU.add))
                    run(gp.tensor_tensor(m[:, c1, :], TMPH[:, 2, 0:width], TMPH[:, 3, 0:width], ALU.add))

            eye(bufs[0])
            for n in range(LOW):
                low(n, bufs[n % 2], bufs[1 - n % 2])
            settle()
            gp.nop().then_inc(e_up, 1)
            eye(bufs[0])
            order = [0, 2]
            for n in range(LOW):
                low(LOW + n, bufs[order[n % 2]], bufs[order[1 - n % 2]])
            gp.wait_ge(c_in, 16 * 14)
            gp.wait_ge(z_first, 6 * 4)
            for st in reversed(range(HIGH - 1)):
                high(1, Z, D, st)
            settle()
            gp.nop().then_inc(z_high, 1)
            gp.wait_ge(rt_sb, KF)
            for st in range(HIGH):
                high(0, RT, W1P, st)
            settle()
            run(gp.tensor_tensor(BH[:, :], RT[:, :, D], UPB[:, :], ALU.add))
            settle()
            gp.nop().then_inc(rt_high, 1)

            def split(full, lo):
                settle()
                run(gp.tensor_copy(f32r(lo), full))
                settle()
                run(gp.tensor_tensor(f32r(lo), full, rounded(lo), ALU.subtract))
                settle()
                run(gp.tensor_tensor(f32r(full), full, rounded(lo), ALU.subtract))

            def flat(v):
                return v.rearrange("p k t -> p (k t)")

            def split_ctx(b):
                gp.wait_ge(ctx_in, 16 * b + 16)
                split(flat(CTXB), flat(CTXL))
                settle()
                gp.nop().then_inc(ctx_split, 1)

            gp.wait_ge(ys_out, 16 * NT)

            def gather(b):
                if b:
                    gp.wait_ge(x2_added, TB * b)
                for q in range(TB):
                    t = TB * b + q
                    gp.indirect_dma_start(out=YG[:, q, :], out_offset=None, in_=ys,
                                          in_offset=bass.IndirectOffsetOnAxis(ap=POS[:, t:t + 1], axis=0))\
                        .then_inc(gathered, 16)

            def roots(g):
                gp.wait_ge(c["c_eps"], TB * (g + 1))
                gp.tensor_tensor(RS[:, :], VE[:, :], spread(MHALF[:, :], 1, TB), ALU.pow)\
                    .then_inc(c["c_rstd"], 1)

            gather(0)
            roots(norm_c(0))
            gather(1)
            for b in range(B + 1):
                if b:
                    roots(norm_d(b))
                if b + 1 < B:
                    roots(norm_c(b + 1))
                if b + 1 < B:
                    split_ctx(b + 1)
                if b + 2 < B:
                    gather(b + 2)

        @block.tensor
        def _(pe):
            def product(dst, lhs, rhs, chunks, signal=None):
                for k in range(chunks):
                    last = pe.matmul(dst, lhs(k), rhs(k), start=(k == 0), stop=(k == chunks - 1))
                if signal is not None:
                    last.then_inc(signal, 1)

            def flip(bank, src, signal, n=KD):
                for k in range(n):
                    last = pe.transpose(bank[:, k * P:(k + 1) * P], src[:, k * P:(k + 1) * P], IDENT[:, :])
                last.then_inc(signal, 1)

            pe.nop().then_inc(slot_uses, 1)
            pe.wait_ge(consts, 6)
            W1 = SLOT[:, 2, 0:KD * F].rearrange("p (k f) -> p k f", k=KD)
            W2 = SLOT[:, 2, KD * F:2 * KD * F].rearrange("p (k f) -> p k f", k=KD)
            W3 = SLOT[:, 2, 2 * KD * F:WS].rearrange("p (c d) -> p c d", c=KF)

            def up_half(t3, hf):
                n = 2 * num(t3) + hf
                for bank, w, done, free in ((PB[6], W1, "h1_done", "gelu_done"),
                                            (PB[7], W2, "h2_done", "mult_done")):
                    if not (first(t3, 1) and hf == 0):
                        pe.wait_ge(s[free], n)
                    for q in range(4):
                        m = 4 * hf + q
                        product(bank[:, q * P:(q + 1) * P], lambda k: w[:, k, m * P:(m + 1) * P],
                                lambda k: X2T[:, k, :], KD, s[done] if q == 3 else None)

            def step(of):
                t0, t3, t4 = of(0), of(3), of(4)
                if t3 is not None:
                    n3 = num(t3)
                    pe.wait_ge(s["a_ready"], n3 + 1)
                    if first(t3, 1):
                        pe.wait_ge(wg_in, 48)
                        pe.wait_ge(slot_in[2], 16)
                    else:
                        pe.wait_ge(s["x2T_sb"], n3)
                    flip(PB[3], AO[:, :], s["aT_done"])
                    pe.wait_ge(s["aT_sb"], n3 + 1)
                    if not first(t3, 1):
                        pe.wait_ge(s["lg_sb"], n3)
                    product(PB[5][:, 0:D], lambda k: AT[:, k, :], lambda k: WO0[:, k, :], KD, s["o_done"])
                if t4 is not None:
                    up_half(t4, 1)
                if t0 is not None:
                    n = num(t0)
                    pe.wait_ge(tile_in[t0[1]], 32 * t0[0] + 32)
                    if first(t0, 1):
                        pe.wait_ge(w_in, 32)
                    else:
                        pe.wait_ge(s["kv_sb"], n)
                    product(PB[4][:, :], lambda k: CTX[:, t0[1], k, :], lambda k: WKV0[:, k, :], KD,
                            s["kv_done"])
                if t4 is not None:
                    n4 = num(t4)
                    pe.wait_ge(s["mult_done"], 2 * n4 + 2)
                    if not first(t4, 1):
                        pe.wait_ge(s["y_added"], n4)
                    product(PB[2][:, 0:D], lambda k: HA[:, k, :], lambda k: W3[:, k, :], KF, s["y_done"])
                if t3 is not None:
                    pe.wait_ge(s["xn2_ready"], n3 + 1)
                    flip(PB[3], XH[:, :], s["x2T_done"])
                if t0 is not None:
                    pe.wait_ge(s["xn_ready"], n + 1)
                    if not first(t0, 1):
                        pe.wait_ge(s["xT_sb"], n)
                    flip(PB[0], XN[:, :], s["xT_done"])
                if t3 is not None:
                    pe.wait_ge(s["x2T_sb"], n3 + 1)
                    product(PB[5][:, 0:NE], lambda k: X2T[:, k, :], lambda k: WG[:, k, :], KD,
                            s["gate_done"])
                if t0 is not None:
                    pe.wait_ge(s["xT_sb"], n + 1)
                    if not first(t0, 1):
                        pe.wait_ge(s["qk_prod"], n)
                    product(PB[1][:, 0:D], lambda k: XT[:, k, :], lambda k: WQ0[:, k, :], KD, s["q_done"])
                if t3 is not None:
                    up_half(t3, 0)
                    if isinstance(n3, int) and n3 == T - 1:
                        ranks()

            def ranks():
                pe.wait_ge(s["oh_ok"], T)
                pe.matmul(PB[1][:, 0:T * NE], ABOVE[:, :], OH[:, :, :].rearrange("p t e -> p (t e)"),
                          start=True, stop=False)
                for t in range(T - 1):
                    last = pe.matmul(PB[1][:, (t + 1) * NE:T * NE].rearrange("p (t e) -> p t e", e=NE), ONES[:, :],
                                     spread(OH[:, t:t + 1, :], 1, T - 1 - t), start=False, stop=(t == T - 2))
                last.then_inc(rank_ps, 1)
                pe.matmul(PB[4][:, 0:T * NE], ONES[:, :], OH[:, :, :].rearrange("p t e -> p (t e)"),
                          start=True, stop=True).then_inc(rank_ps, 1)

            sweep_a(pe, step)

            pe.wait_ge(tables, 1)
            pe.wait_ge(s["y_added"], T)

            def step_b(of):
                t0, t1, t2 = of(0), of(1), of(2)
                if t1 is not None:
                    n = num(t1)
                    slot, *counts = [pe.value_load(TAB[0:1, r, bass.ds(n, 1)], min_val=lo, max_val=hi)
                                     for r, (lo, hi) in enumerate([(0, SLOTS - 1)] + SLOTS * [(16, 64)])]
                if t2 is not None:
                    n2 = num(t2)
                    slot2 = pe.value_load(TAB[0:1, 0, bass.ds(n2, 1)], min_val=0, max_val=SLOTS - 1)
                    for r, free in enumerate(("hT_a", "hT_d")):
                        pe.wait_ge(e["b_mult"], 2 * n2 + 1 + r)
                        if not first(t2, 1):
                            pe.wait_ge(e[free], n2)
                        flip(PB[5 + r], HB[:, t2[1], r * 512:(r + 1) * 512], e["hT_done"], 4)
                if t0 is not None:
                    n = num(t0)
                    pe.wait_ge(xs_in[t0[1]], 16 * t0[0] + 16)
                    if not first(t0, 1):
                        pe.wait_ge(e["sT_sb"], n)
                    flip(PB[0], XS[:, t0[1], :], e["sT_done"])
                if t1 is not None:
                    n = num(t1)
                    for k in range(SLOTS):
                        pe.wait_ge(slot_in[k], counts[k])
                    pe.wait_ge(e["sT_sb"], n + 1)
                    for hf in range(2):
                        for bank, at, done, free in ((PB[1 + hf], 0, "b_h1", "b_gelu"),
                                                     (PB[3 + hf], KD * F, "b_h2", "b_mult")):
                            if not first(t1, 1):
                                pe.wait_ge(e[free], 2 * n + hf - 1)
                            product(bank[:, :], lambda k: XST[:, t1[1], k, :],
                                    lambda k: SLOT[:, bass.ds(slot, 1), at + k * F + hf * 512:
                                                   at + k * F + hf * 512 + 512].rearrange("p o f -> p (o f)"),
                                    KD, e[done])
                if t2 is not None:
                    pe.wait_ge(e["hT_a"], n2 + 1)
                    pe.wait_ge(e["hT_d"], n2 + 1)
                    if not first(t2, 1):
                        pe.wait_ge(e["by_sb"], n2)
                    product(PB[7][:, 0:D], lambda k: HBT[:, k, :],
                            lambda k: SLOT[:, bass.ds(slot2, 1), 2 * KD * F + k * D:
                                           2 * KD * F + (k + 1) * D].rearrange("p o f -> p (o f)"),
                            KF, slot_uses)

            def fold_up():
                pe.wait_ge(e_up, 1)
                pe.wait_ge(c_in, 16 * 14)
                pe.wait_ge(e["sT_sb"], 2 * PAUSE)
                pe.wait_ge(e["by_sb"], 2 * PAUSE - 2)
                for m in range(KF):
                    if m >= 2:
                        pe.wait_ge(rt_sb, m - 1)
                    product(PB[0 if m % 2 == 0 else 7][:, 0:W1P], lambda k: EB[:, 1, m * P:(m + 1) * P],
                            lambda k: WET[:, m, :], 1, rt_ps)
                pe.wait_ge(rt_sb, KF)

            sweep_b(pe, step_b, fold_up)

            def fill(b, n, make):
                before = ring_before(b, n)
                if not (isinstance(before, int) and before == 0):
                    pe.wait_ge(ring_free[n % 2], before)
                make(PB[6 + n % 2], ring_full[n % 2])

            def flips(g, r):
                for q in (2 * r, 2 * r + 1):
                    f = TB * g + q
                    pe.wait_ge(c["c_xn"], f + 1)
                    for k in range(KD):
                        last = pe.transpose(PB[5 * r][:, (KD * (q % 2) + k) * P:(KD * (q % 2) + k + 1) * P],
                                            XNC[:, q, k * P:(k + 1) * P], IDENT[:, :])
                    last.then_inc(c["c_xT"], 1)

            def flipped(g):
                pe.wait_ge(c["c_xT_sb"], 2 * g + 2)

            def parts(dst, lhs, rhs, chunks, signal=None):
                for k in range(chunks):
                    (lh, ll), (rh, rl) = lhs(k), rhs(k)
                    for n, (a, b) in enumerate(((lh, rh), (lh, rl), (ll, rh))):
                        last = pe.matmul(dst, f32r(a), f32r(b), start=(k == 0 and n == 0),
                                         stop=(k == chunks - 1 and n == 2))
                if signal is not None:
                    last.then_inc(signal, 1)

            def wide(w, wl, m, rhs, rl):
                at = slice(m * P, (m + 1) * P)
                return lambda bank, full: parts(bank[:, :], lambda k: (w[:, k, at], wl[k][:, at]),
                                                lambda k: (rhs[:, k, :], rl[:, k, :]), KD, full)

            def values(r):
                def make(bank, full):
                    for h in range(2):
                        q = 2 * r + h
                        at = slice(q * P, (q + 1) * P)
                        parts(bank[:, h * D:(h + 1) * D], lambda k: (CTXB[:, k, at], CTXL[:, k, at]),
                              lambda k: (WV1[:, k, :], WV1L[k]), KD, full if h else None)
                return make

            def down(q):
                at = slice(q * P, (q + 1) * P)
                return lambda bank, full: parts(bank[:, 0:D], lambda k: (H4[:, k, at], H4L[:, k, at]),
                                                lambda k: (MDN[:, k, :], MDNL[:, k, :]), KF, full)

            def piece(b, n):
                if n < 4:
                    for m in (2 * n, 2 * n + 1):
                        fill(b, 4 + m, wide(WEFF, WEFFL, m, XN4T, XN4TL))
                else:
                    if n == 4:
                        pe.wait_ge(h4_split, KF * b)
                    fill(b, 8 + n, down(n - 4))

            def keys(b):
                pe.wait_ge(ctx_split, b + 1)
                for m in range(KD):
                    fill(b, m, wide(WK1, WK1L, m, CTXB, CTXL))

            def values_of(b, r):
                values(r)(PB[2 + r], c["v_done"])

            def step_cd(b, has_c, has_d, has_next):
                if not has_c:
                    for r in range(2):
                        flips(norm_d(b), r)
                    flipped(norm_d(b))
                    for n in range(8):
                        piece(b, n)
                    return
                if has_d:
                    keys(b)
                    values_of(b, 0)
                flipped(norm_c(b))
                for m in range(KD):
                    fill(b, 2 + m, wide(WQ1, WQ1L, m, XN3T, XN3TL))
                if has_d:
                    values_of(b, 1)
                for n in (2, 3):
                    pe.wait_ge(ring_free[n % 2], ring_before(b, n) + 1)

                def out_product(q):
                    n = TB * b + q
                    pe.wait_ge(c["cT_sb"], n + 1)
                    if not (isinstance(n, int) and n == 0):
                        pe.wait_ge(c["x3_ready"], n)
                    parts(PB[4][:, 0:D], lambda k: (CT[:, k, :], CTL[:, k, :]),
                          lambda k: (WO1[:, k, :], WO1L[k]), KD, c["out_done"])

                def flip_c(q):
                    n = TB * b + q
                    pe.wait_ge(c["c_ready"], n + 1)
                    if not (isinstance(n, int) and n == 0):
                        pe.wait_ge(c["cT_sb"], n)
                    flip(PB[5], CC, c["cT_done"])

                def scores(q):
                    n = TB * b + q
                    if not (isinstance(n, int) and n == 0):
                        pe.wait_ge(c["p_done"], n)
                    at = slice(q * P, (q + 1) * P)
                    parts(PB[1][:, :], lambda k: (QT[:, k, at], QTL[:, k, at]),
                          lambda k: (K1T[:, k, :], K1TL[:, k, :]), KD, c["sc_done"])

                scores(0)
                if has_d:
                    for r in range(2):
                        flips(norm_d(b), r)
                pe.wait_ge(c["v_sb"], 2 * b + 2)
                for q in range(TB):
                    n = TB * b + q
                    pe.wait_ge(c["p_done"], n + 1)
                    if not (isinstance(n, int) and n == 0):
                        pe.wait_ge(c["pT_sb"], n)
                    flip(PB[2], PS[:, q % 2, :], c["pT_done"], TB)
                    if q + 1 < TB:
                        scores(q + 1)
                    if q:
                        out_product(q - 1)
                    if has_next and q == 3:
                        for r in range(2):
                            flips(norm_c(b + 1), r)
                    if has_d:
                        if q == 0:
                            flipped(norm_d(b))
                        if q < 2:
                            piece(b, 2 * q)
                    pe.wait_ge(c["pT_sb"], n + 1)
                    if not (isinstance(n, int) and n == 0):
                        pe.wait_ge(c["c_ready"], n)
                    parts(PB[3][:, 0:D], lambda k: (PT[:, k, :], PTL[:, k, :]),
                          lambda k: (V1[:, k, :], V1L[:, k, :]), TB, c["av_done"])
                    if has_d:
                        piece(b, 2 * q if q >= 2 else 2 * q + 1)
                    if has_next and q == 3:
                        flipped(norm_c(b + 1))
                    flip_c(q)
                    if has_d and q >= 2:
                        piece(b, 2 * q + 1)
                out_product(TB - 1)

            def fold_down():
                pe.wait_ge(rt_high, 1)
                pe.wait_ge(e["hT_d"], NT)
                pe.wait_ge(e["by_sb"], NT)
                for n in range(KF):
                    k, m0 = n // 4, 2 * (n % 4)
                    if n >= 4:
                        pe.wait_ge(wm_sb, n - 3)
                    for h in range(2):
                        last = pe.transpose(FOLD[n % 4][:, h * P:(h + 1) * P],
                                            RT[:, m0 + h, k * P:(k + 1) * P], IDENT[:, :])
                    last.then_inc(wm_ps, 1)
                for m in range(KF):
                    pe.wait_ge(wm_sb, KF + m - 3)
                    product(FOLD[m % 4][:, 0:D], lambda k: EC[:, m * P:(m + 1) * P],
                            lambda k: Z[:, m, :], 1, wm_ps)
                pe.wait_ge(wm_sb, 2 * KF)

            pe.wait_ge(c_in, 16 * 14)
            fold_down()
            pe.wait_ge(low_parts, 3 * 4 * KD)
            keys(0)
            for r in range(2):
                values_of(0, r)
            for r in range(2):
                flips(0, r)
            sweep_cd(pe, step_cd)

        @block.scalar
        def _(act):
            act.wait_ge(wg_in, 48)
            act.activation(TG[:, :], GATE[:, :], ACT.Tanh).then_inc(tanh_s, 1)

            def step(of):
                t0, t1, t3, t4 = of(0), of(1), of(3), of(4)

                def gelu(hf):
                    n = 2 * num(t4) + hf
                    act.wait_ge(s["h1_done"], n + 1)
                    if not first(t4, 1):
                        act.wait_ge(s["mult_done"], n - 1)
                    act.activation(G[:, hf * 512:(hf + 1) * 512], PB[6][:, :], ACT.Gelu)\
                        .then_inc(s["gelu_done"], 1)

                if t4 is not None:
                    gelu(0)
                if t3 is not None:
                    act.wait_ge(s["aT_done"], num(t3) + 1)
                    act.activation(AT[:, :, :].rearrange("p k t -> p (k t)"), PB[3][:, 0:D], ACT.Copy)\
                        .then_inc(s["aT_sb"], 1)
                if t4 is not None:
                    gelu(1)
                if t0 is not None:
                    n = num(t0)
                    act.wait_ge(s["kv_done"], n + 1)
                    if not first(t0, 2):
                        act.wait_ge(s["qk_prod"], n - 1)
                        act.wait_ge(s["av_prod"], 2 * n - 2)
                    act.activation(KV[:, t0[1], :], PB[4][:, :], ACT.Copy).then_inc(s["kv_sb"], 1)
                if t1 is not None:
                    n1 = num(t1)
                    act.wait_ge(s["shifted"], n1 + 1)
                    if not first(t1, 2):
                        act.wait_ge(s["av_prod"], 2 * n1 - 2)
                        act.wait_ge(s["sums"], n1 - 1)
                    act.activation(PR[:, t1[1], :], SC[:, :], ACT.Exp, scale=float(DK) ** -0.5)\
                        .then_inc(s["exp_done"], 1)
                if t3 is not None:
                    act.wait_ge(s["x2T_done"], num(t3) + 1)
                    act.activation(X2T[:, :, :].rearrange("p k t -> p (k t)"), PB[3][:, 0:D], ACT.Copy)\
                        .then_inc(s["x2T_sb"], 1)
                if t0 is not None:
                    act.wait_ge(s["xT_done"], num(t0) + 1)
                    act.activation(XT[:, :, :].rearrange("p k t -> p (k t)"), PB[0][:, 0:D], ACT.Copy)\
                        .then_inc(s["xT_sb"], 1)
                if t3 is not None:
                    act.activation(XN2[:, num(t3), :], XH[:, :], ACT.Copy).then_inc(s["xn2_kept"], 1)

            sweep_a(act, step)

            def load_rows(jp):
                act.dma_start(XS[:, jp[1], :], xs[bass.ds(num(jp) * P, P), :]).then_inc(xs_in[jp[1]], 16)

            act.wait_ge(scattered, 16 * T)
            load_rows((0, 0))
            load_rows((0, 1))

            def step_b(of):
                t0, t1, t2 = of(0), of(1), of(2)
                if t2 is not None:
                    n2 = num(t2)
                    act.wait_ge(e["hT_done"], 2 * n2 + 1)
                    act.activation(HBT[:, 0:4, :].rearrange("p k t -> p (k t)"), PB[5][:, :], ACT.Copy)\
                        .then_inc(e["hT_a"], 1)
                if t0 is not None:
                    n = num(t0)
                    act.wait_ge(e["sT_done"], n + 1)
                    act.activation(XST[:, t0[1], :, :].rearrange("p k t -> p (k t)"), PB[0][:, 0:D], ACT.Copy)\
                        .then_inc(e["sT_sb"], 1)
                    if not isinstance(n, int) or n + 2 < NT:
                        load_rows((t0[0] + 1, t0[1]))
                if t1 is not None:
                    n = num(t1)
                    for hf in range(2):
                        act.wait_ge(e["b_h1"], 2 * n + hf + 1)
                        if not first(t1, 1):
                            act.wait_ge(e["b_mult"], 2 * n + hf - 1)
                        act.activation(G[:, hf * 512:(hf + 1) * 512], PB[1 + hf][:, :], ACT.Gelu)\
                            .then_inc(e["b_gelu"], 1)
                if t2 is not None:
                    act.wait_ge(slot_uses, n2 + 2)
                    if not first(t2, 1):
                        act.wait_ge(ys_out, 16 * n2)
                    act.activation(YS[:, :], PB[7][:, 0:D], ACT.Copy).then_inc(e["by_sb"], 1)
                    act.wait_ge(e["by_sb"], n2 + 1)
                    act.dma_start(ys[bass.ds(n2 * P, P), :], YS[:, :]).then_inc(ys_out, 16)

            def fold_up():
                act.wait_ge(scattered, 16 * T)
                for m in range(KF):
                    act.wait_ge(rt_ps, m + 1)
                    act.activation(RT[:, m, :], PB[0 if m % 2 == 0 else 7][:, 0:W1P], ACT.Copy)\
                        .then_inc(rt_sb, 1)

            sweep_b(act, step_b, fold_up)

            def take(b, n, out, func, **extra):
                act.wait_ge(ring_full[n % 2], ring_before(b, n) + 1)
                act.activation(f32r(out) if n < 4 else out, PB[6 + n % 2][:, :], func, **extra)\
                    .then_inc((ring_high if n < 4 else ring_free)[n % 2], 1)

            def copies(g, r, dst):
                act.wait_ge(c["c_xT"], TB * g + 2 * r + 2)
                act.activation(f32r(pair(dst, r)), flipped_bank(r), ACT.Copy).then_inc(c["c_xT_hi"], 1)

            def piece(b, n):
                if n < 4:
                    if n:
                        act.wait_ge(h4_split, KF * b - KF + 2 * n)
                    for m in (2 * n, 2 * n + 1):
                        take(b, 4 + m, HF[m % 2], ACT.Gelu, bias=BH[:, m:m + 1])
                    for m in (2 * n, 2 * n + 1):
                        act.wait_ge(ring_free[m % 2], ring_before(b, 4 + m) + 1)
                        act.activation(f32r(H4[:, m, :]), HF[m % 2], ACT.Copy).then_inc(h4_high, 1)

            def keys(b):
                for m in range(KD):
                    take(b, m, K1T[:, m, :], ACT.Copy)

            def values_of(b, r):
                act.wait_ge(c["v_done"], 2 * b + r + 1)
                act.activation(f32r(V1[:, 2 * r:2 * r + 2, :].rearrange("p t d -> p (t d)")), PB[2 + r][:, :],
                               ACT.Copy).then_inc(c["v_high"], 1)

            def step_cd(b, has_c, has_d, has_next):
                if not has_c:
                    for r in range(2):
                        copies(norm_d(b), r, XN4T)
                    for n in range(4):
                        piece(b, n)
                    return
                if has_d:
                    keys(b)
                    values_of(b, 0)
                for m in range(KD):
                    take(b, 2 + m, QT[:, m, :], ACT.Identity, bias=BQ[:, m:m + 1])
                if has_d:
                    values_of(b, 1)

                def weights(q):
                    n = TB * b + q
                    act.wait_ge(c["nmax_s"], n + 1)
                    if not (isinstance(n, int) and n < 2):
                        act.wait_ge(c["pT_done"], n - 1)
                        act.wait_ge(c["rinv"], n - 1)
                    act.activation(PS[:, q % 2, :], PB[1][:, :], ACT.Exp, bias=NMS[:, q % 2:q % 2 + 1],
                                   scale=float(D) ** -0.5, accum_out=SU[:, q % 2:q % 2 + 1])\
                        .then_inc(c["p_done"], 1)

                weights(0)
                if has_d:
                    for r in range(2):
                        copies(norm_d(b), r, XN4T)
                for q in range(TB):
                    n = TB * b + q
                    act.wait_ge(c["pT_done"], n + 1)
                    if not (isinstance(n, int) and n == 0):
                        act.wait_ge(c["av_done"], n)
                    act.activation(f32r(PT.rearrange("p k t -> p (k t)")), PB[2][:, :], ACT.Copy)\
                        .then_inc(c["pT_hi"], 1)
                    if q + 1 < TB:
                        weights(q + 1)
                    if has_next and q == 3:
                        for r in range(2):
                            copies(norm_c(b + 1), r, XN3T)
                    if has_d:
                        piece(b, 2 * q)
                        piece(b, 2 * q + 1)
                    copy_c(n)

            def copy_c(n):
                act.wait_ge(c["cT_done"], n + 1)
                if not (isinstance(n, int) and n == 0):
                    act.wait_ge(c["out_done"], n)
                act.activation(f32r(CT.rearrange("p k t -> p (k t)")), PB[5][:, 0:D], ACT.Copy)\
                    .then_inc(c["cT_hi"], 1)

            for n in range(KF):
                k, m0 = n // 4, 2 * (n % 4)
                act.wait_ge(wm_ps, n + 1)
                act.activation(f32r(WEFF[:, k, m0 * P:(m0 + 2) * P]), FOLD[n % 4][:, 0:2 * P], ACT.Copy)\
                    .then_inc(wm_high, 1)
            for m in range(KF):
                act.wait_ge(wm_ps, KF + m + 1)
                act.activation(f32r(MDN[:, m, :]), FOLD[m % 4][:, 0:D], ACT.Copy).then_inc(wm_high, 1)
            keys(0)
            for r in range(2):
                values_of(0, r)
            for r in range(2):
                copies(0, r, XN3T)
            sweep_cd(act, step_cd)

        @block.vector
        def _(dve):
            def hold(signal, value):
                dve.wait_ge(signal, value)
                if not isinstance(value, int):
                    dve.sem_inc(held, 1)

            def step(of):
                t0, t1, t2, t3, t4 = of(0), of(1), of(2), of(3), of(4)
                if t1 is not None:
                    n, par = num(t1), t1[1]
                    dve.wait_ge(s["q_done"], n + 1)
                    dve.wait_ge(s["kv_sb"], n + 1)
                    prod = PRODQ[:, :].rearrange("p (i j h) -> p i j h", i=DK, j=DK)
                    dve.tensor_tensor(
                        prod,
                        spread(PB[1][:, 0:D].rearrange("p (i o h) -> p i o h", i=DK, o=1), 2, DK),
                        spread(KV[:, par, 0:D].rearrange("p (o j h) -> p o j h", o=1, j=DK), 1, DK),
                        ALU.mult).then_inc(s["qk_prod"], 1)
                if t4 is not None:
                    if isinstance(t4[0], int) and num(t4) == T - 1:
                        places()
                    mult(t4, 0)
                if t1 is not None:
                    dve.wait_ge(s["qk_prod"], n + 1)
                    if not first(t1, 1):
                        dve.wait_ge(s["exp_done"], n)
                    dve.tensor_reduce(SC[:, :].rearrange("p (i j) -> p i j", i=DK), prod, AX.X, ALU.add)\
                        .then_inc(s["scores"], 1)
                if t4 is not None:
                    mult(t4, 1)
                if t3 is not None:
                    n3 = num(t3)
                    dve.wait_ge(s["o_done"], n3 + 1)
                    if first(t3, 1):
                        dve.wait_ge(tanh_s, 1)
                    dve.scalar_tensor_tensor(X[:, n3, :], PB[5][:, 0:D], TG[:, 0:1], X[:, n3, :],
                                             ALU.mult, ALU.add).then_inc(s["x1_ready"], 1)
                if t0 is not None:
                    n0 = num(t0)
                    hold(tile_in[t0[1]], 32 * t0[0] + 32)
                    dve.bn_stats(ST[:, 0, :], X[:, n0, :]).then_inc(s["ln1_stats"], 1)
                if t3 is not None:
                    hold(s["x1_ready"], n3 + 1)
                    dve.bn_stats(ST[:, 1, :], X[:, n3, :]).then_inc(s["ln2_stats"], 1)
                if t1 is not None:
                    dve.wait_ge(s["scores"], n + 1)
                    dve.tensor_reduce(SM[:, 0, :], SC[:, :].rearrange("p (i j) -> p i j", i=DK), AX.X, ALU.max)\
                        .then_inc(s["rowmax"], 1)
                for tt, r, nm in ((t0, 0, "ln1"), (t3, 1, "ln2")):
                    if tt is not None:
                        hold(s[nm + "_stats"], num(tt) + 1)
                        dve.bn_aggr(MV[:, r, 0:2], ST[:, r, :]).then_inc(s[nm + "_agg"], 1)
                if t1 is not None:
                    dve.wait_ge(s["rowmax"], n + 1)
                    dve.tensor_tensor(SC[:, :].rearrange("p (i j) -> p i j", i=DK),
                                      SC[:, :].rearrange("p (i j) -> p i j", i=DK),
                                      spread(SM[:, 0, :].rearrange("p (i o) -> p i o", o=1), 2, DK),
                                      ALU.subtract).then_inc(s["shifted"], 1)
                for tt, r, nm in ((t3, 1, "ln2"), (t0, 0, "ln1")):
                    if tt is not None:
                        dve.wait_ge(s[nm + "_agg"], num(tt) + 1)
                        dve.tensor_scalar(MV[:, r, 2:3], MV[:, r, 1:2], EPS, None, ALU.add)\
                            .then_inc(s[nm + "_eps"], 1)
                if t2 is not None:
                    n2 = num(t2)
                    dve.wait_ge(s["exp_done"], n2 + 1)
                    dve.tensor_reduce(SM[:, 1, :], PR[:, t2[1], :].rearrange("p (i j) -> p i j", i=DK),
                                      AX.X, ALU.add).then_inc(s["sums"], 1)
                if t3 is not None:
                    dve.wait_ge(s["ln2_rstd"], n3 + 1)
                    if not first(t3, 1):
                        dve.wait_ge(s["x2T_done"], n3)
                        dve.wait_ge(s["xn2_kept"], n3)
                    dve.tensor_scalar(XH[:, :], X[:, n3, :], MV[:, 1, 0:1], MV[:, 1, 3:4],
                                      ALU.subtract, ALU.mult).then_inc(s["xn2_ready"], 1)
                if t0 is not None:
                    dve.wait_ge(s["ln1_rstd"], n0 + 1)
                    if not first(t0, 1):
                        dve.wait_ge(s["xT_done"], n0)
                    dve.tensor_scalar(XN[:, :], X[:, n0, :], MV[:, 0, 0:1], MV[:, 0, 3:4],
                                      ALU.subtract, ALU.mult).then_inc(s["xn_ready"], 1)
                if t2 is not None:
                    dve.wait_ge(s["sums"], n2 + 1)
                    dve.reciprocal(RI[:, :], SM[:, 1, :]).then_inc(s["recip"], 1)
                    if not first(t2, 1):
                        dve.wait_ge(s["aT_done"], n2)
                    aov = AO[:, :].rearrange("p (i h) -> p i h", i=DK)
                    for hf in range(2):
                        H2 = NH // 2
                        dve.wait_ge(s["av_half"], 2 * n2 + hf + 1)
                        dve.tensor_reduce(
                            aov[:, :, hf * H2:(hf + 1) * H2],
                            PRODV[:, :].rearrange("p (f i h j) -> p f i h j", f=2, i=DK, h=H2)
                            [:, hf, :, :, 0:DK // 2], AX.X, ALU.add).then_inc(s["av_read"], 1)
                if t3 is not None:
                    dve.wait_ge(s["gate_done"], n3 + 1)
                    dve.tensor_copy(LG[:, :], PB[5][:, 0:NE]).then_inc(s["lg_sb"], 1)
                if t2 is not None:
                    dve.wait_ge(s["av_read"], 2 * n2 + 2)
                    dve.wait_ge(s["recip"], n2 + 1)
                    dve.tensor_tensor(aov, aov, spread(RI[:, :].rearrange("p (i o) -> p i o", o=1), 2, NH),
                                      ALU.mult).then_inc(s["a_ready"], 1)
                if t3 is not None:
                    hold(s["lg_sb"], n3 + 1)
                    dve.max(TOP[:, :], LG[:, :]).then_inc(s["top_ok"], 1)
                if t4 is not None:
                    n4 = num(t4)
                    dve.wait_ge(s["y_done"], n4 + 1)
                    dve.scalar_tensor_tensor(X[:, n4, :], PB[2][:, 0:D], TG[:, 2:3], X[:, n4, :],
                                             ALU.mult, ALU.add).then_inc(s["y_added"], 1)
                if t3 is not None:
                    if first(t3, 1):
                        dve.wait_ge(iotaf, 3)
                    hold(s["top_ok"], n3 + 1)
                    dve.max_index(TOPI[:, :], TOP[:, :], LG[:, :]).then_inc(s["topi_ok"], 1)
                    dve.wait_ge(s["topi_ok"], n3 + 1)
                    dve.tensor_copy(TOPF[:, :], TOPI[:, 0:1]).then_inc(s["topf_ok"], 1)
                    dve.wait_ge(s["topf_ok"], n3 + 1)
                    dve.tensor_scalar(OH[:, n3, :], IOTA8[:, :], TOPF[:, :], None, ALU.is_equal)\
                        .then_inc(s["oh_ok"], 1)

            def mult(t, hf):
                n = 2 * num(t) + hf
                dve.wait_ge(s["gelu_done"], n + 1)
                dve.wait_ge(s["h2_done"], n + 1)
                dve.tensor_tensor(HA[:, 4 * hf:4 * hf + 4, :].rearrange("p k t -> p (k t)"),
                                  PB[7][:, :], G[:, hf * 512:(hf + 1) * 512], ALU.mult)\
                    .then_inc(s["mult_done"], 1)

            def places():
                steps = [0]

                def link(ins):
                    steps[0] += 1
                    ins.then_inc(route, 1)
                    dve.wait_ge(route, steps[0])

                def row(v, n, parts=P):
                    return spread(v.rearrange("p (o e) -> p o e", o=1), 1, n)

                def col(v, n):
                    return spread(v.rearrange("p (e o) -> p e o", o=1), 2, n)

                def grid(v, a):
                    return v.rearrange("p (a b) -> p a b", a=a)

                link(dve.tensor_tensor(LESS[:, :, :], row(IOTA8[:, :], NE), col(IOTA8[:, :], NE), ALU.is_lt))
                dve.wait_ge(rank_ps, 2)
                link(dve.tensor_reduce(NTE[:, :], PB[4][:, 0:T * NE].rearrange("p (t e) -> p e t", e=NE),
                                       AX.X, ALU.add))
                link(dve.tensor_tensor(grid(CMP[:, :], NE), col(NTE[:, :], T), row(IOTAM[:, :], NE), ALU.is_gt))
                link(dve.tensor_reduce(NTE[:, :], grid(CMP[:, :], NE), AX.X, ALU.add))
                link(dve.tensor_tensor(LESS[:, :, :], LESS[:, :, :], row(NTE[:, :], NE), ALU.mult))
                link(dve.tensor_reduce(BASE[:, :], LESS[:, :, :], AX.X, ALU.add))
                link(dve.tensor_scalar(NTE[:, :], BASE[:, :], float(P), None, ALU.mult))
                link(dve.tensor_tensor(RANK[:, :, :], row(NTE[:, :], T), grid(PB[1][:, 0:T * NE], T), ALU.add))
                link(dve.tensor_tensor(RANK[:, :, :], RANK[:, :, :], OH[:, :, :], ALU.mult))
                link(dve.tensor_reduce(POSF[:, :], RANK[:, :, :], AX.X, ALU.add))
                dve.tensor_copy(POS[:, :], POSF[:, :]).then_inc(pos_ready, 1)
                b1 = BASE[0:1, :]
                link(dve.tensor_tensor(GE[:, :, :], row(b1, NT), col(IOTAT[:, :], NE), ALU.is_le))
                link(dve.tensor_reduce(EI[:, :], GE[:, :, :], AX.X, ALU.add))
                link(dve.tensor_scalar(EI[:, :], EI[:, :], -1.0, None, ALU.add))
                link(dve.tensor_tensor(GE[:, :, :], row(IOTA8[0:1, :], NT), col(EI[:, :], NE), ALU.is_le))
                for k, (lo, hi) in enumerate(((3, 6), (4, 7), (2, 5))):
                    link(dve.tensor_tensor(SUM2[:, k, :], GE[:, :, lo], GE[:, :, hi], ALU.add))
                    link(dve.tensor_scalar(TAB[:, 1 + k, :], SUM2[:, k, :], 16.0, 16.0, ALU.mult, ALU.add))
                link(dve.scalar_tensor_tensor(TAB[:, 0, :], SUM2[:, 0, :], -3.0, EI[:, :], ALU.mult, ALU.add))
                dve.tensor_scalar(BASEI[:, :], b1, 1.0, None, ALU.add).then_inc(tables, 1)

            dve.wait_ge(iotas, 3)
            dve.tensor_copy(IOTA8[:, :], IOTAI[:, 0:NE]).then_inc(iotaf, 1)
            dve.tensor_copy(IOTAM[:, :], IOTAI[:, NE:NE + T]).then_inc(iotaf, 1)
            dve.tensor_copy(IOTAT[:, :], IOTAI[0:1, NE + T:NE + T + NT]).then_inc(iotaf, 1)
            sweep_a(dve, step)

            def step_b(of):
                t1, t2 = of(1), of(2)
                if t2 is not None:
                    n = num(t2)
                    dve.wait_ge(e["hT_done"], 2 * n + 2)
                    dve.tensor_copy(HBT[:, 4:8, :].rearrange("p k t -> p (k t)"), PB[6][:, :])\
                        .then_inc(e["hT_d"], 1)
                if t1 is not None:
                    n = num(t1)
                    for hf in range(2):
                        dve.wait_ge(e["b_gelu"], 2 * n + hf + 1)
                        dve.wait_ge(e["b_h2"], 2 * n + hf + 1)
                        if not first(t1, 2):
                            dve.wait_ge(e["hT_done"], 2 * n - 2)
                        dve.tensor_tensor(HB[:, t1[1], hf * 512:(hf + 1) * 512], PB[3 + hf][:, :],
                                          G[:, hf * 512:(hf + 1) * 512], ALU.mult).then_inc(e["b_mult"], 1)
                t0 = of(0)
                if t0 is not None and first(t0, 4):
                    if num(t0) == 0:
                        dve.wait_ge(c_in, 16 * 14)
                        dve.wait_ge(zeroed, 48)
                        dve.wait_ge(scattered, 16 * T)
                    first_stage(num(t0))

            def split(n, full, lo):
                dve.tensor_copy(f32r(lo), full).then_inc(low_parts, 1)
                dve.wait_ge(low_parts, 3 * n + 1)
                dve.tensor_tensor(f32r(lo), full, rounded(lo), ALU.subtract).then_inc(low_parts, 1)
                dve.wait_ge(low_parts, 3 * n + 2)
                return dve.tensor_tensor(f32r(full), full, rounded(lo), ALU.subtract)

            def split_weights():
                dve.wait_ge(c_in, 16 * 14)
                for i, (w, los) in enumerate(((WK1, WK1L), (WV1, WV1L), (WQ1, WQ1L), (WO1, WO1L))):
                    for k in range(KD):
                        split(KD * i + k, w[:, k, :], los[k]).then_inc(low_parts, 1)

            def first_stage(q):
                c0, c1, cf = high_pair(1, HIGH - 1, q)
                for i, (src, k) in enumerate(((c0, 0), (c1, 1), (c0, 2), (c1, 3))):
                    dve.tensor_scalar(TMPZ[:, i, :], Z[:, src, :], cf[k], None, ALU.mult).then_inc(z_first, 1)
                dve.wait_ge(z_first, 6 * q + 4)
                dve.tensor_tensor(Z[:, c0, :], TMPZ[:, 0, :], TMPZ[:, 1, :], ALU.add).then_inc(z_first, 1)
                dve.tensor_tensor(Z[:, c1, :], TMPZ[:, 2, :], TMPZ[:, 3, :], ALU.add).then_inc(z_first, 1)
                dve.wait_ge(z_first, 6 * q + 6)

            sweep_b(dve, step_b, split_weights)
            dve.wait_ge(ctx_in, 16)
            split(4 * KD, CTXB.rearrange("p k t -> p (k t)"), CTXL.rearrange("p k t -> p (k t)"))\
                .then_inc(ctx_split, 1)

            dve.wait_ge(c_in, 16 * 14)
            dve.tensor_tensor(BCD[:, :], BIAS[:, 2, :], BIAS[:, 3, :], ALU.add).then_inc(bcd_ready, 1)

            def lower(lo, value, high, done):
                dve.tensor_tensor(f32r(lo), value, rounded(high), ALU.subtract).then_inc(done, 1)

            for n in range(KF):
                k, m0 = n // 4, 2 * (n % 4)
                dve.wait_ge(wm_high, n + 1)
                lower(WEFFL[k][:, m0 * P:(m0 + 2) * P], FOLD[n % 4][:, 0:2 * P],
                      WEFF[:, k, m0 * P:(m0 + 2) * P], wm_sb)
            for m in range(KF):
                dve.wait_ge(wm_high, KF + m + 1)
                lower(MDNL[:, m, :], FOLD[m % 4][:, 0:D], MDN[:, m, :], wm_sb)

            def lower_ring(b, n, lo, high):
                dve.wait_ge(ring_high[n % 2], 2 * b + n // 2 + 1)
                lower(lo, PB[6 + n % 2][:, :], high, ring_free[n % 2])

            def lower_keys(b):
                for m in range(KD):
                    lower_ring(b, m, K1TL[:, m, :], K1T[:, m, :])

            def lower_values(b, r):
                at = slice(2 * r, 2 * r + 2)
                dve.wait_ge(c["v_high"], 2 * b + r + 1)
                lower(V1L[:, at, :].rearrange("p t d -> p (t d)"), PB[2 + r][:, :],
                      V1[:, at, :].rearrange("p t d -> p (t d)"), c["v_sb"])

            def lower_queries(b):
                for m in range(KD):
                    dve.wait_ge(ring_high[m % 2], 2 * b + 2)
                    dve.scalar_tensor_tensor(f32r(QTL[:, m, :]), PB[6 + m % 2][:, :], BQ[:, m:m + 1],
                                             rounded(QT[:, m, :]), ALU.add, ALU.subtract).then_inc(ring_free[m % 2], 1)

            def lower_rows(g, dst, lo):
                for r in range(2):
                    dve.wait_ge(c["c_xT_hi"], 2 * g + r + 1)
                    lower(pair(lo, r), flipped_bank(r), pair(dst, r), c["c_xT_sb"])

            def lower_hidden(b, n):
                if n < 4:
                    for m in (2 * n, 2 * n + 1):
                        dve.wait_ge(h4_high, KF * b - KF + m + 1)
                        lower(H4L[:, m, :], HF[m % 2], H4[:, m, :], h4_split)

            def norm_stats(t0, g):
                for q in range(TB):
                    dve.bn_stats(STC[:, q, :], X[:, t0 + q, :]).then_inc(c["c_stats"], 1)
                for q in range(TB):
                    hold(c["c_stats"], TB * g + q + 1)
                    dve.bn_aggr(MVC[:, q, :], STC[:, q, :]).then_inc(c["c_agg"], 1)
                for q in range(TB):
                    dve.wait_ge(c["c_agg"], TB * g + q + 1)
                    dve.tensor_scalar(VE[:, q:q + 1], MVC[:, q, 1:2], EPS, None, ALU.add).then_inc(c["c_eps"], 1)

            def norm_rows(t0, g):
                dve.wait_ge(c["c_rstd"], g + 1)
                if not (isinstance(g, int) and g == 0):
                    dve.wait_ge(c["c_xT"], TB * g)
                for q in range(TB):
                    dve.tensor_scalar(XNC[:, q, :], X[:, t0 + q, :], MVC[:, q, 0:1], RS[:, q:q + 1],
                                      ALU.subtract, ALU.mult).then_inc(c["c_xn"], 1)

            def finish(b, q):
                m = TB * b - TB + q
                dve.wait_ge(ring_full[q % 2], ring_before(b, 12 + q) + 1)
                if isinstance(m, int) or q:
                    dve.wait_ge(c["fin_ready"], m)
                dve.tensor_tensor(TY, PB[6 + q % 2][:, 0:D], BCD[:, :], ALU.add).then_inc(ring_free[q % 2], 1)
                dve.wait_ge(ring_free[q % 2], ring_before(b, 12 + q) + 1)
                dve.scalar_tensor_tensor(X[:, m, :], TY, TG[:, 3:4], X[:, m, :], ALU.mult, ALU.add)\
                    .then_inc(c["fin_ready"], 1)

            def next_rows(b):
                dve.wait_ge(gathered, 16 * TB * b + 16 * TB)
                for q in range(TB):
                    dve.scalar_tensor_tensor(X[:, TB * b + q, :], YG[:, q, :], TG[:, 2:3], X[:, TB * b + q, :],
                                             ALU.mult, ALU.add).then_inc(x2_added, 1)

            def next_stats(b):
                hold(x2_added, TB * b + TB)
                norm_stats(TB * b, norm_c(b))

            def step_cd(b, has_c, has_d, has_next):
                if has_c and has_d:
                    lower_keys(b)
                if has_d:
                    hold(c["x3_ready"], TB * b)
                    norm_stats(TB * b - TB, norm_d(b))
                if has_c and has_d:
                    lower_values(b, 0)
                if has_c:
                    lower_queries(b)
                if has_d:
                    norm_rows(TB * b - TB, norm_d(b))
                if not has_c:
                    lower_rows(norm_d(b), XN4T, XN4TL)
                if not has_c:
                    for n in range(4):
                        lower_hidden(b, n)
                    for q in range(TB):
                        finish(b, q)
                    return

                def add_out(q):
                    m = TB * b + q
                    dve.wait_ge(c["out_done"], m + 1)
                    dve.tensor_tensor(TO, PB[4][:, 0:D], BIAS[:, 1, :], ALU.add).then_inc(c["tmp_o"], 1)
                    dve.wait_ge(c["tmp_o"], m + 1)
                    dve.scalar_tensor_tensor(X[:, m, :], TO, TG[:, 1:2], X[:, m, :], ALU.mult, ALU.add)\
                        .then_inc(c["x3_ready"], 1)

                def largest(q):
                    m = TB * b + q
                    dve.wait_ge(c["sc_done"], m + 1)
                    dve.tensor_reduce(NM[:, :], PB[1][:, :], AX.X, ALU.max, negate=True).then_inc(c["nmax"], 1)
                    dve.wait_ge(c["nmax"], m + 1)
                    if not (isinstance(m, int) and m < 2):
                        dve.wait_ge(c["p_done"], m - 1)
                    dve.tensor_scalar(NMS[:, q % 2:q % 2 + 1], NM[:, :], float(D) ** -0.5, None, ALU.mult)\
                        .then_inc(c["nmax_s"], 1)

                largest(0)
                if has_d:
                    lower_values(b, 1)
                    lower_rows(norm_d(b), XN4T, XN4TL)
                for q in range(TB):
                    m = TB * b + q
                    dve.wait_ge(c["p_done"], m + 1)
                    dve.reciprocal(RC[:, :], SU[:, q % 2:q % 2 + 1]).then_inc(c["rinv"], 1)
                    dve.wait_ge(c["pT_hi"], m + 1)
                    lower(PTL.rearrange("p k t -> p (k t)"), PB[2][:, :], PT.rearrange("p k t -> p (k t)"), c["pT_sb"])
                    if q + 1 < TB:
                        largest(q + 1)
                    if q:
                        add_out(q - 1)
                    if has_next and q == 3:
                        lower_rows(norm_c(b + 1), XN3T, XN3TL)
                    if has_d:
                        lower_hidden(b, 2 * q)
                    dve.wait_ge(c["av_done"], m + 1)
                    dve.wait_ge(c["rinv"], m + 1)
                    if not (isinstance(m, int) and m == 0):
                        dve.wait_ge(c["cT_done"], m)
                    dve.scalar_tensor_tensor(CC, PB[3][:, 0:D], RC[:, :], BIAS[:, 0, :], ALU.mult, ALU.add)\
                        .then_inc(c["c_ready"], 1)
                    if has_next and q == 0:
                        next_rows(b + 1)
                    if has_next and q == 1:
                        next_stats(b + 1)
                    if has_next and q == 2:
                        norm_rows(TB * b + TB, norm_c(b + 1))
                    if has_d and q >= 2:
                        finish(b, 2 * q - 4)
                    if has_d:
                        lower_hidden(b, 2 * q + 1)
                    dve.wait_ge(c["cT_hi"], m + 1)
                    lower(CTL.rearrange("p k t -> p (k t)"), PB[5][:, 0:D], CT.rearrange("p k t -> p (k t)"), c["cT_sb"])
                    if has_d and q >= 2:
                        finish(b, 2 * q - 3)
                add_out(TB - 1)

            dve.wait_ge(bcd_ready, 1)
            next_rows(0)
            next_stats(0)
            lower_keys(0)
            norm_rows(0, 0)
            for r in range(2):
                lower_values(0, r)
            lower_rows(0, XN3T, XN3TL)
            sweep_cd(dve, step_cd)


def kernel(x, ctx_1024, g_xattn, g_ffn, L0_xattn_Wq, L0_xattn_Wk, L0_xattn_Wv, L0_xattn_Wo,
           L0_ffn_w1s, L0_ffn_w2s, L0_ffn_w3s, L0_ffn_W1, L0_ffn_W2, L0_ffn_W3, L0_ffn_Wg,
           L1_xattn_Wk, L1_xattn_Wv, L1_xattn_bv, L1_xattn_Wq, L1_xattn_bq, L1_xattn_Wo, L1_xattn_bo,
           L1_ffn_W_exp, L1_ffn_b_exp, L1_ffn_up_weights, L1_ffn_up_bias, L1_ffn_down_weights,
           L1_ffn_W_con, L1_ffn_b_con, L1_ffn_down_bias):
    import concourse.bacc as bacc
    from concourse.bass_utils import run_bass_kernel_spmd

    def by_dim(w):
        return np.asarray(w).reshape(NH, DK, D).transpose(2, 1, 0).reshape(D, D)

    def chunks(w):
        w = np.asarray(w)
        return w.reshape(w.shape[0] // P, P, w.shape[1]).transpose(1, 0, 2).reshape(P, -1)

    experts = [[chunks(w[n]) for w in (L0_ffn_W1, L0_ffn_W2, L0_ffn_W3)] for n in range(NE)]
    experts.append([chunks(w) for w in (L0_ffn_w1s, L0_ffn_w2s, L0_ffn_w3s)])
    arrays = {
        "x": np.asarray(x).reshape(B * L, D),
        "ctxT": np.asarray(ctx_1024).reshape(B * L, D).T,
        "gates": np.concatenate([np.asarray(g_xattn), np.asarray(g_ffn)]),
        "wq0": by_dim(L0_xattn_Wq),
        "wkv0": np.concatenate([by_dim(L0_xattn_Wk), np.asarray(L0_xattn_Wv).T], axis=1),
        "wo0": np.asarray(L0_xattn_Wo).T.reshape(NH, DK, D).transpose(1, 0, 2).reshape(D, D),
        "wg": np.asarray(L0_ffn_Wg),
        "wexp": np.stack([np.concatenate(w, axis=1) for w in experts]),
        "wk1": np.asarray(L1_xattn_Wk).T, "wv1": np.asarray(L1_xattn_Wv).T,
        "wq1": np.asarray(L1_xattn_Wq).T, "wo1": np.asarray(L1_xattn_Wo).T,
        "bv1": np.asarray(L1_xattn_bv), "bq1": np.asarray(L1_xattn_bq), "bo1": np.asarray(L1_xattn_bo),
        "weT": np.asarray(L1_ffn_W_exp).T, "be": np.asarray(L1_ffn_b_exp),
        "upw": np.asarray(L1_ffn_up_weights).reshape(LOW + HIGH, F // 2, 4),
        "upb": np.asarray(L1_ffn_up_bias),
        "dnw": np.asarray(L1_ffn_down_weights).reshape(LOW + HIGH, F // 2, 4),
        "wc": np.asarray(L1_ffn_W_con), "bc": np.asarray(L1_ffn_b_con), "db": np.asarray(L1_ffn_down_bias),
    }
    arrays = {k: np.ascontiguousarray(v) for k, v in arrays.items()}
    nc = bacc.Bacc("TRN2", target_bir_lowering=False, num_devices=1)
    args = [nc.dram_tensor(k, v.shape, mybir.dt.from_np(v.dtype), kind="ExternalInput").ap()
            for k, v in arrays.items()]
    out = nc.dram_tensor("out", (B * L, D), F32, kind="ExternalOutput").ap()
    build(nc, *args, out)
    r = run_bass_kernel_spmd(nc, [arrays], core_ids=[0])
    return r.results[0]["out"].reshape(B, L, D)
```
